# Optimizing a Trainium2 kernel written in Bass

```python
import numpy as np
import jax
import jax.numpy as jnp

def _softmax(x, axis=-1):
    return jax.nn.softmax(x, axis=axis)

def _gelu(x):
    return jax.nn.gelu(x, approximate=True)

def _silu(x):
    return jax.nn.silu(x)

def _sigmoid(x):
    return jax.nn.sigmoid(x)

def _layernorm(x, axis=-1, eps=1e-05):
    m = jnp.mean(x, axis=axis, keepdims=True)
    v = jnp.var(x, axis=axis, keepdims=True)
    return (x - m) / jnp.sqrt(v + eps)

def _scatter_add(tgt, idx, src, axis=0):
    return tgt.at[idx].add(src)

def _segment_sum(src, seg, n):
    return jax.ops.segment_sum(src, seg, n)
kernel_name = 'mk_hybrid_d1_jaxref_r8_e53c9d'

def setup_inputs(seed: int=0):
    np.random.seed(seed)
    _w = jnp.asarray

    def _L0_attn_a_setup():
        import jax, jax.numpy as jnp
        import numpy as np
        EPS = 1e-12
        key = jax.random.key(seed)
        k1, k2 = jax.random.split(key)
        b, n, d = (4, 512, 128)
        x = jax.random.normal(k1, (b, n, d), dtype=jnp.float32)
        W_qkva = jax.random.normal(k2, (3 * d, d), dtype=jnp.float32) * 0.02
        gamma = jnp.ones((d,), dtype=jnp.float32)
        return {'x': x, 'W_qkva': W_qkva, 'gamma': gamma}
    _L0_attn_a_in = _L0_attn_a_setup()

    def _L0_attn_b_setup():
        import jax, jax.numpy as jnp
        import numpy as np
        B, S, D, H = (4, 512, 128, 16)
        HD = D // H
        EPS = 1e-06

        def _feature_map(t):
            return jax.nn.elu(t) + 1.0
        key = jax.random.key(seed)
        ks = jax.random.split(key, 5)
        scale = 0.02
        return {'x': jax.random.normal(ks[0], (B, S, D), dtype=jnp.float32), 'wq': jax.random.normal(ks[1], (D, D), dtype=jnp.float32) * scale, 'wk': jax.random.normal(ks[2], (D, D), dtype=jnp.float32) * scale, 'wv': jax.random.normal(ks[3], (D, D), dtype=jnp.float32) * scale, 'wo': jax.random.normal(ks[4], (D, D), dtype=jnp.float32) * scale}
    _L0_attn_b_in = _L0_attn_b_setup()

    def _L0_ffn_setup():
        import jax, jax.numpy as jnp
        import numpy as np
        D_MODEL, HIDDEN, N_EXPERTS, TOP_K = (128, 256, 8, 2)
        RMS_EPS = 1e-06
        key = jax.random.key(seed)
        ks = jax.random.split(key, 6)
        B, S = (4, 256)
        return {'x': jax.random.normal(ks[0], (B, S, D_MODEL), jnp.float32), 'norm_weight': jnp.ones((D_MODEL,), jnp.float32), 'gate_w': jax.random.normal(ks[1], (N_EXPERTS, D_MODEL), jnp.float32) * 0.02, 'w1': jax.random.normal(ks[2], (N_EXPERTS, HIDDEN, D_MODEL), jnp.float32) * 0.02, 'b1': jnp.zeros((N_EXPERTS, HIDDEN), jnp.float32), 'w2': jax.random.normal(ks[3], (N_EXPERTS, D_MODEL, HIDDEN), jnp.float32) * 0.02, 'b2': jnp.zeros((N_EXPERTS, D_MODEL), jnp.float32)}
    _L0_ffn_in = _L0_ffn_setup()
    _d = {'L0_attn_a_x': _L0_attn_a_in['x'], 'L0_attn_a_W_qkva': _L0_attn_a_in['W_qkva'], 'L0_attn_a_gamma': _L0_attn_a_in['gamma'], 'L0_attn_b_wq': _L0_attn_b_in['wq'], 'L0_attn_b_wk': _L0_attn_b_in['wk'], 'L0_attn_b_wv': _L0_attn_b_in['wv'], 'L0_attn_b_wo': _L0_attn_b_in['wo'], 'L0_ffn_norm_weight': _L0_ffn_in['norm_weight'], 'L0_ffn_gate_w': _L0_ffn_in['gate_w'], 'L0_ffn_w1': _L0_ffn_in['w1'], 'L0_ffn_b1': _L0_ffn_in['b1'], 'L0_ffn_w2': _L0_ffn_in['w2'], 'L0_ffn_b2': _L0_ffn_in['b2']}
    _x0 = _d['L0_attn_a_x']
    _d['L0_attn_a_x'] = jax.random.normal(jax.random.fold_in(jax.random.key(seed), 1), (32, 256, 128), dtype=_x0.dtype)
    del _x0
    return _d

def reference(L0_attn_a_x, L0_attn_a_W_qkva, L0_attn_a_gamma, L0_attn_b_wq, L0_attn_b_wk, L0_attn_b_wv, L0_attn_b_wo, L0_ffn_norm_weight, L0_ffn_gate_w, L0_ffn_w1, L0_ffn_b1, L0_ffn_w2, L0_ffn_b2):

    def _L0_attn_a_ref(x, W_qkva, gamma):
        import jax, jax.numpy as jnp
        import numpy as np
        EPS = 1e-12
        d = gamma.shape[0]
        scale = d ** 0.5
        norm = jnp.maximum(jnp.linalg.norm(x, axis=-1, keepdims=True), EPS)
        xn = x / norm * scale * gamma
        h = jnp.einsum('bnd,ed->bne', xn, W_qkva)
        q, kv, a = jnp.split(h, 3, axis=-1)
        a = jax.nn.sigmoid(a)

        def binop(e_i, e_j):
            a_i, kv_i = e_i
            a_j, kv_j = e_j
            return (a_j * a_i, a_j * kv_i + kv_j)
        _, y = jax.lax.associative_scan(binop, (a, kv), axis=1)
        return q * y

    def _L0_attn_b_ref(x, wq, wk, wv, wo):
        import jax, jax.numpy as jnp
        import numpy as np
        B, S, D, H = (4, 512, 128, 16)
        HD = D // H
        EPS = 1e-06

        def _feature_map(t):
            return jax.nn.elu(t) + 1.0
        b, s, d = x.shape
        q = _feature_map((x @ wq).reshape(b, s, H, HD))
        k = _feature_map((x @ wk).reshape(b, s, H, HD))
        v = (x @ wv).reshape(b, s, H, HD)
        qs = jnp.moveaxis(q, 1, 0)
        ks = jnp.moveaxis(k, 1, 0)
        vs = jnp.moveaxis(v, 1, 0)

        def step(carry, qkv):
            S_kv, z = carry
            qt, kt, vt = qkv
            S_kv = S_kv + jnp.einsum('bhd,bhe->bhde', kt, vt)
            z = z + kt
            num = jnp.einsum('bhd,bhde->bhe', qt, S_kv)
            den = jnp.einsum('bhd,bhd->bh', qt, z)[..., None] + EPS
            return ((S_kv, z), num / den)
        init = (jnp.zeros((b, H, HD, HD), x.dtype), jnp.zeros((b, H, HD), x.dtype))
        _, outs = jax.lax.scan(step, init, (qs, ks, vs))
        out = jnp.moveaxis(outs, 0, 1).reshape(b, s, d) @ wo
        return out

    def _L0_ffn_ref(x, norm_weight, gate_w, w1, b1, w2, b2):
        import jax, jax.numpy as jnp
        import numpy as np
        D_MODEL, HIDDEN, N_EXPERTS, TOP_K = (128, 256, 8, 2)
        RMS_EPS = 1e-06
        B, S, D = x.shape
        E = gate_w.shape[0]
        t = x * jax.lax.rsqrt(jnp.mean(x * x, axis=-1, keepdims=True) + RMS_EPS) * norm_weight
        tokens = t.reshape(-1, D)
        T = tokens.shape[0]
        gate_logits = tokens @ gate_w.T
        gate_scores, expert_idx = jax.lax.top_k(gate_logits, TOP_K)
        routing_weights = jax.nn.softmax(gate_scores, axis=-1)
        combine = jnp.zeros((T, E), tokens.dtype).at[jnp.arange(T)[:, None], expert_idx].add(routing_weights)

        def body(acc, params):
            W1, B1, W2, B2, c = params
            h = jax.nn.gelu(tokens @ W1.T + B1, approximate=False)
            o = h @ W2.T + B2
            return (acc + c[:, None] * o, None)
        out, _ = jax.lax.scan(body, jnp.zeros_like(tokens), (w1, b1, w2, b2, combine.T))
        return x + out.reshape(B, S, D)
    x = L0_attn_a_x
    x = x + _L0_attn_a_ref(_layernorm(x, axis=-1), L0_attn_a_W_qkva, L0_attn_a_gamma)
    x = x + _L0_ffn_ref(_layernorm(x, axis=-1), L0_ffn_norm_weight, L0_ffn_gate_w, L0_ffn_w1, L0_ffn_b1, L0_ffn_w2, L0_ffn_b2)
    x = x + _L0_attn_b_ref(_layernorm(x, axis=-1), L0_attn_b_wq, L0_attn_b_wk, L0_attn_b_wv, L0_attn_b_wo)
    x = x + _L0_ffn_ref(_layernorm(x, axis=-1), L0_ffn_norm_weight, L0_ffn_gate_w, L0_ffn_w1, L0_ffn_b1, L0_ffn_w2, L0_ffn_b2)
    return x

_drawn_inputs = setup_inputs


def setup_inputs(seed=0):
    import zlib

    import numpy as np

    out = dict(_drawn_inputs(seed))
    spreads = {'L0_attn_a_gamma': (1.0, 0.6),
     'L0_ffn_norm_weight': (1.0, 0.584),
     'L0_ffn_b1': (0.0, 0.765),
     'L0_ffn_b2': (0.0, 0.1)}
    factors = {'L0_attn_b_wq': 8.0, 'L0_attn_b_wk': 8.0, 'L0_attn_b_wv': 8.0, 'L0_attn_b_wo': 8.0}
    for name, (base, spread) in spreads.items():
        noise = np.random.default_rng([zlib.crc32(name.encode()), seed]).standard_normal(out[name].shape)
        drawn = base * np.exp(spread * noise) if base else spread * noise
        out[name] = jnp.asarray(drawn.astype(out[name].dtype))
    for name, factor in factors.items():
        out[name] = (out[name] * factor).astype(out[name].dtype)
    return out
```

```python
from contextlib import ExitStack

import concourse.bass as bass
from concourse import mybir

F32 = mybir.dt.float32
BF16 = mybir.dt.bfloat16
I32 = mybir.dt.int32
U32 = mybir.dt.uint32
ALU = mybir.AluOpType
ACT = mybir.ActivationFunctionType
X = mybir.AxisListType.X
P = 128

HEADS, HD = 16, 8
LN_EPS = 1e-5
A_EPS = 1e-12
RMS_EPS = 1e-6
B_EPS = 1e-6
HALVES = 2
QUAD = 4
SLOTS = 256
BIG = 3.0e38


def run_steps(eng, steps, unroll, body):
    for m in range(unroll):
        body(m, m)
    with eng.Fori(1, steps // unroll - 1) as n:
        for j in range(unroll):
            body(n * unroll + j, j)
    for m in range(steps - unroll, steps):
        body(m, m % unroll)


def is_at(step, n):
    return isinstance(step, int) and step == n


def wait(eng, sem, value):
    if not isinstance(value, int) or value > 0:
        eng.wait_ge(sem, value)


def build_hybrid(nc, x_in, w_qkva, gamma, b_wq, b_wk, b_wv, b_wo, norm_w, gate_w, w1, b1, w2, b2, x_out, stages=4):
    B, S, D = x_in.shape
    E, HID, _ = w1.shape
    HC = HID // P
    TILES = B * S // P
    HT = TILES // HALVES
    A_STEPS = HT // QUAD
    B_STEPS = HT * P // S
    G_STEPS = HT // QUAD
    E_UNROLL = 8
    AHEAD = 6
    E_STEPS = -(-((2 * HT * P + E * (SLOTS - 1)) // SLOTS) // E_UNROLL) * E_UNROLL
    ROWS = E_STEPS * SLOTS
    SUB = SLOTS // P
    W1C = HID + HC
    SCALE = float(D) ** 0.5
    assert D == P and S == 2 * P and HEADS * HD == D and SLOTS == 2 * P

    x_tiles = x_in.rearrange("b (t p) d -> p (b t) d", p=P)
    out_tiles = x_out.rearrange("b (t p) d -> p (b t) d", p=P)
    tok_rows = [nc.dram_tensor(f"tok_rows{h}", [ROWS, D], F32).ap() for h in range(HALVES)]
    exp_rows = [nc.dram_tensor(f"exp_rows{h}", [ROWS, D], F32).ap() for h in range(HALVES)]

    with ExitStack() as ctx:
        def sb(name, shape, dt=F32):
            return ctx.enter_context(nc.sbuf_tensor(name, shape, dt))

        def sem(name):
            return ctx.enter_context(nc.semaphore(name))

        ps = ctx.enter_context(nc.psum_tensor("ps", [P, 8, 512], F32))
        x = sb("x", [P, TILES, D])
        ident = sb("ident", [P, P])
        before = sb("before", [P, P], BF16)
        ones = sb("ones", [P, P], BF16)
        causal = sb("causal", [P, P])
        head_diag = sb("head_diag", [P, P])
        head_sum = sb("head_sum", [P, HEADS])
        head_pick = sb("head_pick", [P, 4])
        desc = sb("desc", [P, E])
        step_slot = sb("step_slot", [P, E_STEPS])
        not_first = sb("not_first", [P, E, HT])
        ones8 = sb("ones8", [P, E])
        one_row = sb("one_row", [P, S])
        wa = sb("wa", [P, 3, P])
        wb = sb("wb", [P, 4, P])
        gT = sb("gT", [P, E])
        w1T = sb("w1T", [P, E, W1C])
        w2T = sb("w2T", [P, E * HC, P])
        b2_all = sb("b2_all", [P, E, D])
        gam = sb("gam", [P, 1])
        nw = sb("nw", [P, 1])
        stats = sb("stats", [P, TILES, 6])
        mean = sb("mean", [P, TILES])
        var = sb("var", [P, TILES])
        rstd = sb("rstd", [P, TILES])
        res_scale = sb("res_scale", [P, TILES])
        res_bias = sb("res_bias", [P, TILES])
        sv = sb("sv", [P, 6, HT])
        xn = sb("xn", [P, 2, QUAD, D])
        xnT = sb("xnT", [P, 2, QUAD * P])
        gate = sb("gate", [P, 2, QUAD * P])
        yq = sb("yq", [P, 2, QUAD * P])
        t_rows = sb("t_rows", [P, HALVES, HT, D])
        got = sb("got", [P, 2, HT, D])
        logits = sb("logits", [P, HT, E])
        r_a = sb("r_a", [P, HT, E])
        r_b = sb("r_b", [P, HT, E])
        pick1 = sb("pick1", [P, HT, E])
        pick2 = sb("pick2", [P, HT, E])
        picked = sb("picked", [P, HT, E], BF16)
        tile_tot = sb("tile_tot", [P, E, HT])
        tile_inc = sb("tile_inc", [P, E, HT])
        m1 = sb("m1", [P, HT])
        m2 = sb("m2", [P, HT])
        mi = sb("mi", [P, HT])
        ex = sb("ex", [P, HT])
        prob = sb("prob", [P, 2, HALVES, HT])
        cnt_i = sb("cnt_i", [P, E], I32)
        cnt_f = sb("cnt_f", [P, E])
        ends = sb("ends", [P, E])
        base = sb("base", [P, E])
        slot = sb("slot", [P, 2, HALVES, HT], U32)
        step_cmp = sb("step_cmp", [P, E_STEPS, E])
        step_e = sb("step_e", [P, E_STEPS])
        step_exp = sb("step_exp", [P, HALVES, E_STEPS], I32)
        ts = sb("ts", [P, E_UNROLL, SUB, D])
        tT = sb("tT", [P, 2, SLOTS])
        w1s = sb("w1s", [P, 2, W1C])
        hT = sb("hT", [P, 2, HC, SLOTS])
        o_sb = sb("o_sb", [P, E_UNROLL, SUB, D])

        VW = HEADS // 4 * (P + HD)
        b_xn = sb("b_xn", [P, 2, 2, D])
        b_xnT = sb("b_xnT", [P, S])
        b_exp = sb("b_exp", [P, 2 * S])
        qk = sb("qk", [P, 2, 2, S])
        zc = sb("zc", [P, S])
        qz = sb("qz", [P, S])
        den = sb("den", [P, 2 * HEADS])
        rec = sb("rec", [P, 2 * HEADS])
        recx = sb("recx", [P, 2 * HEADS, HD])
        qx = sb("qx", [P, 2, 4, S])
        vx = sb("vx", [P, 2, 2, VW])
        k_tok = sb("k_tok", [P, P])
        state = gate
        oT = yq

        x_loaded = [sem(f"x_loaded{n}") for n in range(HALVES)]
        w_loaded = sem("w_loaded")
        consts = sem("consts")
        wT_psum = sem("wT_psum")
        wT_done = sem("wT_done")
        chain = sem("chain")
        pchain = sem("pchain")
        first_bn = sem("first_bn")
        ve_ready = sem("ve_ready")
        sqrt_ready = sem("sqrt_ready")
        a_xn, a_xnT_psum, a_xnT, a_mm, a_gate, a_scan, a_yq, a_back, a_added = (
            sem(f"a_{n}") for n in ("xn", "xnT_psum", "xnT", "mm", "gate", "scan", "yq", "back", "added"))
        g_t, g_tT_psum, g_tT, g_mm, g_logits, g_res = (
            sem(f"g_{n}") for n in ("t", "tT_psum", "tT", "mm", "logits", "res"))
        r_diff, r_exp, r_picked, r_rank, r_slots = (sem(f"r_{n}") for n in ("diff", "exp", "picked", "rank", "slots"))
        zeroed = [sem(f"zeroed{h}") for h in range(HALVES)]
        zero_tile = sem("zero_tile")
        scattered = [sem(f"scattered{h}") for h in range(HALVES)]
        gathered = [sem(f"gathered{h}") for h in range(HALVES)]
        e_loaded = [sem(f"e_loaded{k}") for k in range(E_UNROLL)]
        e_stored = [sem(f"e_stored{k}") for k in range(E_UNROLL)]
        e_tT_psum, e_tT, e_w1, e_h_psum, e_h, e_o_psum, e_o = (
            sem(f"e_{n}") for n in ("tT_psum", "tT", "w1", "h_psum", "h", "o_psum", "o"))
        (b_norm, b_xnT_psum, b_xnT_ok, b_qkv, b_expd, b_feat, b_qz, b_den, b_rec, b_recx, b_kt_psum, b_kt, b_st_psum,
         b_st, b_rT, b_q, b_qx, b_v, b_sc, b_masked, b_o_psum, b_o, b_y, b_added) = (sem(f"b_{n}") for n in (
             "norm", "xnT_psum", "xnT_ok", "qkv", "expd", "feat", "qz", "den", "rec", "recx", "kt_psum", "kt", "st_psum",
             "st", "rT", "q", "qx", "v", "sc", "masked", "o_psum", "o", "y", "added"))
        b_clip, b_keys, b_eps = (sem(f"b_{n}") for n in ("clip", "keys", "eps"))
        vx_zero = sem("vx_zero")
        combined = sem("combined")
        stored = sem("stored")

        def rounds(call, m, k):
            per = 16 // E_UNROLL
            return 16 * call * (E_STEPS // E_UNROLL) + (m - k) * per

        def plain_v(b, t):
            return vx[:, b, t, :].rearrange("p (k z) -> p k z", k=4)[:, :, 0:P].rearrange("p k (g c) -> p g k c", g=4)[
                :, :, :, 0:HD]

        def scores_of(h):
            return t_rows[:, h, :, :].rearrange("p (t g k) d -> p t g k d", t=2, g=4)

        def tile_of(buf, i):
            return buf[:, bass.ds(i, 1), :].rearrange("p a d -> p (a d)")

        block = ctx.enter_context(nc.Block())
        ALL_CONSTS = 12
        LOADS = 12

        @block.sync
        def _(sp):
            for h in range(HALVES):
                sp.dma_start(x[:, h * HT:(h + 1) * HT, :], x_tiles[:, h * HT:(h + 1) * HT, :]).then_inc(x_loaded[h], 16)
            sp.wait_ge(zero_tile, 1)
            zt = got[:, 0, 0:16, :].rearrange("p t d -> p (t d)")
            for h in range(HALVES):
                for c in range(ROWS // (16 * P)):
                    sp.dma_start(tok_rows[h][c * 16 * P:(c + 1) * 16 * P, :].rearrange("(p t) d -> p (t d)", t=16),
                                 zt).then_inc(zeroed[h], 16)

            def experts(call, h):
                sp.wait_ge(scattered[h], 16 * 2 * HT * (call // HALVES + 1))
                n0 = call * E_STEPS

                def load(m, k):
                    wait(sp, e_tT_psum, n0 + m - (E_UNROLL - 1))
                    sp.dma_start(ts[:, k, :, :], tok_rows[h][bass.ds(m * SLOTS, SLOTS), :].rearrange(
                        "(p s) d -> p s d", s=SUB)).then_inc(e_loaded[k], 16)

                def store(m, k):
                    sp.wait_ge(e_o, n0 + m + 1)
                    sp.dma_start(exp_rows[h][bass.ds(m * SLOTS, SLOTS), :].rearrange("(p s) d -> p s d", s=SUB),
                                 o_sb[:, k, :, :]).then_inc(e_stored[k], 16)

                def step(m, k):
                    if not isinstance(m, int) or m + AHEAD < E_STEPS:
                        load(m + AHEAD, (k + AHEAD) % E_UNROLL)
                    store(m, k)
                for m in range(AHEAD):
                    load(m, m)
                run_steps(sp, E_STEPS, E_UNROLL, step)

            if stages >= 2:
                for rnd in range(stages // 2):
                    for h in range(HALVES):
                        experts(rnd * HALVES + h, h)
            for h in range(HALVES):
                sp.wait_ge(combined, (stages // 2 - 1) * HALVES + h + 1)
                if stages == 3:
                    sp.wait_ge(b_added, 2 * B_STEPS)
                sp.dma_start(out_tiles[:, h * HT:(h + 1) * HT, :], x[:, h * HT:(h + 1) * HT, :]).then_inc(stored, 16)
            sp.wait_ge(stored, 16 * HALVES)

        @block.gpsimd
        def _(pool):
            links = [0]

            def link(ins):
                links[0] += 1
                ins.then_inc(pchain, 1)
                pool.wait_ge(pchain, links[0])

            nc.gpsimd.memset(got[:, 0, 0:16, :], 0.0).then_inc(zero_tile, 1)
            link(nc.gpsimd.memset(ident[:, :], 0.0))
            nc.gpsimd.affine_select(out=ident[:, :], in_=ident[:, :], compare_op=ALU.not_equal, fill=1.0, base=0,
                                    pattern=[[-1, P]], channel_multiplier=1).then_inc(consts, 1)
            nc.gpsimd.memset(ones[:, :], 1.0).then_inc(consts, 1)
            nc.gpsimd.memset(one_row[:, :], 1.0).then_inc(consts, 1)
            link(nc.gpsimd.memset(before[:, :], 1.0))
            nc.gpsimd.affine_select(out=before[:, :], in_=before[:, :], compare_op=ALU.is_gt, fill=0.0, base=0,
                                    pattern=[[1, P]], channel_multiplier=-1).then_inc(consts, 1)
            link(nc.gpsimd.memset(causal[:, :], 1.0))
            nc.gpsimd.affine_select(out=causal[:, :], in_=causal[:, :], compare_op=ALU.is_ge, fill=0.0, base=0,
                                    pattern=[[1, P]], channel_multiplier=-1).then_inc(consts, 1)
            link(nc.gpsimd.memset(head_diag[:, :], 1.0))
            hd3 = head_diag[:, :].rearrange("p (h e) -> p h e", e=HD)
            link(nc.gpsimd.affine_select(out=hd3, in_=hd3, compare_op=ALU.is_ge, fill=0.0, base=0,
                                         pattern=[[-HD, HEADS], [0, HD]], channel_multiplier=1))
            link(nc.gpsimd.affine_select(out=hd3, in_=hd3, compare_op=ALU.is_ge, fill=0.0, base=HD - 1,
                                         pattern=[[HD, HEADS], [0, HD]], channel_multiplier=-1))
            nc.gpsimd.tensor_copy(head_sum[:, :], hd3[:, :, 0]).then_inc(consts, 1)
            link(nc.gpsimd.memset(desc[:, :], 1.0))
            for e in range(E):
                last = nc.gpsimd.memset(desc[:, e:e + 1], float(E - e))
            last.then_inc(consts, 1)
            nc.gpsimd.iota(step_slot[:, :], pattern=[[SLOTS, E_STEPS]], base=0, channel_multiplier=0,
                           allow_small_or_imprecise_dtypes=True).then_inc(consts, 1)
            link(nc.gpsimd.memset(not_first[:, :, :], 1.0))
            nc.gpsimd.memset(not_first[:, :, 0:1], 0.0).then_inc(consts, 1)
            nc.gpsimd.memset(ones8[:, :], 1.0).then_inc(consts, 1)
            link(nc.gpsimd.memset(head_pick[:, :], 0.0))
            pool.wait_ge(consts, 10)
            hs4 = head_sum[:, :].rearrange("p (g k) -> p g k", k=4)
            link(nc.gpsimd.tensor_tensor(head_pick[:, :], hs4[:, 0, :], hs4[:, 1, :], ALU.add))
            link(nc.gpsimd.tensor_tensor(head_pick[:, :], head_pick[:, :], hs4[:, 2, :], ALU.add))
            nc.gpsimd.tensor_tensor(head_pick[:, :], head_pick[:, :], hs4[:, 3, :], ALU.add).then_inc(consts, 1)
            nc.gpsimd.memset(sv[:, 5, :], 1.0).then_inc(consts, 1)

            def scatter(call, h):
                pool.wait_ge(r_slots, call + 1)
                pool.wait_ge(zeroed[h], 16 * (ROWS // (16 * P)))
                for t in range(HT):
                    for k in range(2):
                        pool.indirect_dma_start(tok_rows[h], bass.IndirectOffsetOnAxis(ap=slot[:, k, h, t:t + 1], axis=0),
                                                t_rows[:, h, t, :], None).then_inc(scattered[h], 16)

            def gather(call, h):
                for k in range(E_UNROLL):
                    pool.wait_ge(e_stored[k], 16 * (E_STEPS // E_UNROLL) * (call + 1))
                wait(pool, combined, call)
                for t in range(HT):
                    for k in range(2):
                        pool.indirect_dma_start(got[:, k, t, :], None, exp_rows[h],
                                                bass.IndirectOffsetOnAxis(ap=slot[:, k, h, t:t + 1], axis=0)
                                                ).then_inc(gathered[h], 16)
            for rnd in range(stages // 2):
                for h in range(HALVES):
                    scatter(rnd * HALVES + h, h)
                for h in range(HALVES):
                    gather(rnd * HALVES + h, h)

        @block.tensor
        def _(pe):
            pe.wait_ge(consts, ALL_CONSTS)
            pe.wait_ge(w_loaded, 16 * LOADS)
            wrows = t_rows[:, 0, :, :]
            groups = [range(0, 4), range(4, 8), range(8, 12), range(12, 16), range(16, 20), range(20, 24), range(24, 28),
                      range(28, 32), range(32, 35)]
            big = t_rows[:, :, :, :].rearrange("p h t d -> p (h t) d")
            for n, group in enumerate(groups):
                for k, r in enumerate(group):
                    last = nc.tensor.transpose(ps[:, n % 8, k * P:(k + 1) * P], big[:, r, :], ident[:, :])
                if n == 7:
                    last.then_inc(wT_psum, 1)
                    pe.wait_ge(wT_done, 1)
            r = big[0:E, 35, :]
            nc.tensor.transpose(ps[:, 0, 3 * P:3 * P + E], big[0:E, 35, :], ident[0:E, 0:E])
            nc.tensor.transpose(ps[:, 0, 3 * P + E:3 * P + E + E * HC], big[0:E * HC, 36, :],
                                ident[0:E * HC, 0:E * HC]).then_inc(wT_psum, 1)

            def layer_a(h):
                n0 = h * A_STEPS

                def turn(i, b):
                    pe.wait_ge(a_xn, n0 + i + 1)
                    wait(pe, a_xnT, n0 + i)
                    for t in range(QUAD):
                        last = nc.tensor.transpose(ps[:, 0, t * P:(t + 1) * P], xn[:, b, t, :], ident[:, :])
                    last.then_inc(a_xnT_psum, 1)

                def project(i, b):
                    pe.wait_ge(a_xnT, n0 + i + 1)
                    wait(pe, a_yq, n0 + i - 1)
                    for bank, c in ((6, 2), (4, 1), (2, 0)):
                        nc.tensor.matmul(ps[:, bank + b, :], wa[:, c, :], xnT[:, b, :], start=True,
                                         stop=True).then_inc(a_mm, 1)

                def back(i, b):
                    pe.wait_ge(a_yq, n0 + i + 1)
                    wait(pe, a_added, n0 + i)
                    for t in range(QUAD):
                        last = nc.tensor.transpose(ps[:, 1, t * P:(t + 1) * P], yq[:, b, t * P:(t + 1) * P], ident[:, :])
                    last.then_inc(a_back, 1)

                def step(i, b):
                    if not isinstance(i, int) or i + 1 < A_STEPS:
                        turn(i + 1, 1 - b)
                    project(i, b)
                    if not is_at(i, 0):
                        back(i - 1, 1 - b)
                turn(0, 0)
                run_steps(pe, A_STEPS, 2, step)
                back(A_STEPS - 1, 1)

            def gates(call):
                n0 = call * G_STEPS

                def turn(i, b):
                    pe.wait_ge(g_t, n0 + i + 1)
                    wait(pe, g_tT, n0 + i - 1)
                    for t in range(QUAD):
                        last = nc.tensor.transpose(ps[:, b, t * P:(t + 1) * P], t_rows[:, call % HALVES, i * QUAD + t, :],
                                                   ident[:, :])
                    last.then_inc(g_tT_psum, 1)

                def logit(i, b):
                    pe.wait_ge(g_tT, n0 + i + 1)
                    wait(pe, g_logits, n0 + i - 1)
                    for t in range(QUAD):
                        last = nc.tensor.matmul(ps[:, 2 + b, t * E:(t + 1) * E], xnT[:, b, t * P:(t + 1) * P], gT[:, :],
                                                start=True, stop=True)
                    last.then_inc(g_mm, 1)
                turn(0, 0)
                for i in range(G_STEPS):
                    if i + 1 < G_STEPS:
                        turn(i + 1, (i + 1) % 2)
                    logit(i, i % 2)
                pe.wait_ge(r_picked, call + 1)
                cols = picked[:, :, :].rearrange("p t e -> p (t e)")
                nc.tensor.matmul(ps[:, 6, 0:HT * E], before[:, :], cols, start=True, stop=True)
                nc.tensor.matmul(ps[:, 7, 0:HT * E], ones[:, :], cols, start=True, stop=True).then_inc(r_rank, 1)

            def experts(call, h):
                n0 = call * E_STEPS

                def turn(m, k):
                    pe.wait_ge(e_loaded[k], rounds(call, m, k) + 16)
                    wait(pe, e_tT, n0 + m - 1)
                    for s in range(SUB):
                        last = nc.tensor.transpose(ps[:, k % 2, s * P:(s + 1) * P], ts[:, k, s, :], ident[:, :])
                    last.then_inc(e_tT_psum, 1)

                def up(m, b):
                    pe.wait_ge(e_tT, n0 + m + 1)
                    pe.wait_ge(e_w1, n0 + m + 1)
                    wait(pe, e_h, n0 + m - 1)
                    for c in range(HC):
                        last = nc.tensor.matmul(ps[:, 2 + b, c * SLOTS:(c + 1) * SLOTS], w1s[:, b, c * P:(c + 1) * P],
                                                tT[:, b, :], start=True, stop=True)
                    last.then_inc(e_h_psum, 1)

                def down(m, b):
                    pe.wait_ge(e_h, n0 + m + 1)
                    wait(pe, e_o, n0 + m - 1)
                    e = pe.value_load(step_exp[0:1, h, bass.ds(m, 1)], min_val=0, max_val=E - 1)
                    for s in range(SUB):
                        for c in range(HC):
                            last = nc.tensor.matmul(ps[:, 4 + b, s * P:(s + 1) * P], hT[:, b, c, s * P:(s + 1) * P],
                                                    tile_of(w2T, e * HC + c), start=(c == 0), stop=(c == HC - 1))
                    last.then_inc(e_o_psum, 1)

                def step(m, k):
                    if not isinstance(m, int) or m + 1 < E_STEPS:
                        turn(m + 1, (k + 1) % E_UNROLL)
                    up(m, k % 2)
                    if not is_at(m, 0):
                        down(m - 1, (k + 1) % 2)
                turn(0, 0)
                run_steps(pe, E_STEPS, E_UNROLL, step)
                down(E_STEPS - 1, 1)

            def layer_b(h):
                scores = scores_of(h)
                n0 = h * B_STEPS

                def turn(m, b):
                    pe.wait_ge(b_norm, n0 + m + 1)
                    wait(pe, b_q, n0 + m)
                    for t in range(2):
                        last = nc.tensor.transpose(ps[:, 0, t * P:(t + 1) * P], b_xn[:, b, t, :], ident[:, :])
                    last.then_inc(b_xnT_psum, 1)

                def project(m, b):
                    pe.wait_ge(b_xnT_ok, n0 + m + 1)
                    wait(pe, b_feat, n0 + m)
                    wait(pe, b_st, n0 + m)
                    for k in range(2):
                        nc.tensor.matmul(ps[:, 1, k * S:(k + 1) * S], wb[:, k, :], b_xnT[:, :], start=True, stop=True)
                    for t in range(2):
                        last = nc.tensor.matmul(ps[:, 2, t * P:(t + 1) * P], b_xnT[:, t * P:(t + 1) * P], wb[:, 2, :],
                                                start=True, stop=True)
                    last.then_inc(b_qkv, 1)

                def denominators(m, b):
                    pe.wait_ge(b_qz, n0 + m + 1)
                    pe.wait_ge(b_v, n0 + m + 1)
                    for t in range(2):
                        last = nc.tensor.matmul(ps[:, 2, S + t * HEADS:S + (t + 1) * HEADS], qz[:, t * P:(t + 1) * P],
                                                head_sum[:, :], start=True, stop=True)
                    last.then_inc(b_den, 1)
                    nc.tensor.transpose(ps[:, 0, S:S + P], qk[:, b, 1, 0:P], ident[:, :]).then_inc(b_kt_psum, 1)

                def states(m, b):
                    pe.wait_ge(b_kt, n0 + m + 1)
                    pe.wait_ge(b_rec, n0 + m + 1)
                    nc.tensor.matmul(ps[:, 2, S + 2 * HEADS:S + 2 * HEADS + P], k_tok[:, :], plain_v(b, 0), start=True,
                                     stop=True).then_inc(b_st_psum, 1)
                    pe.wait_ge(b_recx, n0 + m + 1)
                    for t in range(2):
                        last = nc.tensor.transpose(ps[:, 0, t * P:(t + 1) * P], recx[:, t * HEADS:(t + 1) * HEADS, :].rearrange(
                            "p h e -> p (h e)"), ident[:, :])
                    last.then_inc(b_rT, 1)

                def score(n, b, blk, g):
                    c = 8 * (n0 + n) + 4 * blk + g
                    wait(pe, b_masked, c - 3)
                    if g == 0 and blk == 0:
                        pe.wait_ge(b_qx, n0 + n + 1)
                    q = slice(32 * g, 32 * g + 32)
                    nc.tensor.matmul(ps[:, 3 + g, :], qk[q, b, 1, blk * P:(blk + 1) * P], qx[q, b, :, blk * P:(blk + 1) * P],
                                     start=True, stop=True, tile_position=(32 * g, 0)).then_inc(b_sc, 1)

                def weigh(n, b, blk):
                    pe.wait_ge(b_masked, 8 * (n0 + n) + 4 * blk + 4)
                    wait(pe, b_o, 2 * (n0 + n) + blk)
                    out = ps[:, 7, blk * P:(blk + 1) * P]
                    if blk == 0:
                        wait(pe, b_added, n0 + n)
                    else:
                        pe.wait_ge(b_st, n0 + n + 1)
                        nc.tensor.matmul(out, state[:, b, 0:P], qk[:, b, 0, P:S], start=True, stop=False,
                                         skip_group_check=True)
                    for k in range(4):
                        for g in range(4):
                            q = slice(32 * g, 32 * g + 32)
                            last = nc.tensor.matmul(out[q, :], vx[:, b, blk, k * P + g * 32:k * P + g * 32 + 32],
                                                    scores[:, blk, g, k, :], start=(k == 0 and blk == 0), stop=(k == 3),
                                                    tile_position=(0, 32 * g), skip_group_check=True)
                    last.then_inc(b_o_psum, 1)

                def back(n, b):
                    pe.wait_ge(b_o, 2 * (n0 + n) + 2)
                    for t in range(2):
                        last = nc.tensor.matmul(ps[:, 7, S + t * P:S + (t + 1) * P], oT[:, b, t * P:(t + 1) * P],
                                                wb[:, 3, :], start=True, stop=True)
                    last.then_inc(b_y, 1)

                def step(n, b):
                    more = not isinstance(n, int) or n + 1 < B_STEPS
                    score(n, b, 0, 0)
                    score(n, b, 0, 1)
                    if more:
                        turn(n + 1, 1 - b)
                    score(n, b, 0, 2)
                    score(n, b, 0, 3)
                    if more:
                        project(n + 1, 1 - b)
                    if not is_at(n, 0):
                        back(n - 1, 1 - b)
                    for g in range(4):
                        score(n, b, 1, g)
                    weigh(n, b, 0)
                    if more:
                        denominators(n + 1, 1 - b)
                        states(n + 1, 1 - b)
                    weigh(n, b, 1)
                turn(0, 0)
                project(0, 0)
                denominators(0, 0)
                states(0, 0)
                run_steps(pe, B_STEPS, 2, step)
                back(B_STEPS - 1, 1)

            for rnd in range(2):
                for h in range(HALVES):
                    if rnd == 0:
                        layer_a(h)
                    elif stages >= 3:
                        layer_b(h)
                    if rnd * 2 + 2 <= stages:
                        gates(rnd * HALVES + h)
                for h in range(HALVES):
                    if rnd * 2 + 2 <= stages:
                        experts(rnd * HALVES + h, h)

        @block.scalar
        def _(act):
            big = t_rows[:, :, :, :].rearrange("p h t d -> p (h t) d")
            act.dma_start(big[:, 32:35, :], w_qkva.rearrange("(c p) d -> p c d", p=P)).then_inc(w_loaded, 16)
            act.dma_start(big[:, 0:16, :], w1.rearrange("e (c p) d -> p (e c) d", p=P)).then_inc(w_loaded, 16)
            act.dma_start(big[:, 16:32, :].rearrange("p (e c) d -> p e (c d)", e=E),
                          w2.rearrange("e d h -> d e h")).then_inc(w_loaded, 16)
            act.dma_start(big[0:E, 35, :], gate_w).then_inc(w_loaded, 16)
            act.dma_start(big[0:E * HC, 36, :], b1.rearrange("e (c p) -> (e c) p", p=P)).then_inc(w_loaded, 16)
            act.dma_start(gam[:, :], gamma.rearrange("(p a) -> p a", a=1)).then_inc(w_loaded, 16)
            act.dma_start(nw[:, :], norm_w.rearrange("(p a) -> p a", a=1)).then_inc(w_loaded, 16)
            for k, w in enumerate((b_wq, b_wk, b_wv, b_wo)):
                act.dma_start(wb[:, k, :], w).then_inc(w_loaded, 16)
            act.dma_start(b2_all[:, :, :], b2.rearrange("(a e) d -> a e d", a=1).to_broadcast([P, E, D])).then_inc(w_loaded, 16)
            act.wait_ge(w_loaded, 16 * LOADS)
            act.wait_ge(wT_psum, 1)
            for n in range(4):
                for k in range(2):
                    nc.scalar.activation(w1T[:, 2 * n + k, 0:HID], ps[:, n, k * HID:(k + 1) * HID], ACT.Copy,
                                         scale=nw[:, 0:1])
            for n in range(4):
                last = nc.scalar.copy(w2T[:, 4 * n:4 * n + 4, :].rearrange("p a d -> p (a d)"), ps[:, 4 + n, :])
            last.then_inc(wT_done, 1)
            act.wait_ge(wT_psum, 2)
            nc.scalar.activation(wa[:, :, :].rearrange("p c e -> p (c e)"), ps[:, 0, 0:3 * P], ACT.Copy, scale=gam[:, 0:1])
            nc.scalar.activation(gT[:, :], ps[:, 0, 3 * P:3 * P + E], ACT.Copy, scale=nw[:, 0:1])
            nc.scalar.copy(w1T[:, :, HID:W1C], ps[:, 0, 3 * P + E:3 * P + E + E * HC].rearrange("p (e c) -> p e c", c=HC)
                           ).then_inc(wT_done, 1)
            sqrts = [0]

            def root(src, dst):
                sqrts[0] += 1
                act.wait_ge(ve_ready, sqrts[0])
                nc.scalar.activation(dst, src, ACT.Sqrt).then_inc(sqrt_ready, 1)

            def layer_a(h):
                n0 = h * A_STEPS

                def copy_xnT(i, b):
                    act.wait_ge(a_xnT_psum, n0 + i + 1)
                    wait(act, a_mm, 3 * (n0 + i - 1))
                    nc.scalar.copy(xnT[:, b, :], ps[:, 0, :]).then_inc(a_xnT, 1)

                def step(i, b):
                    if not isinstance(i, int) or i + 1 < A_STEPS:
                        copy_xnT(i + 1, 1 - b)
                    act.wait_ge(a_mm, (n0 + i) * 3 + 1)
                    wait(act, a_scan, n0 + i - 1)
                    nc.scalar.activation(gate[:, b, :], ps[:, 6 + b, :], ACT.Sigmoid).then_inc(a_gate, 1)
                if h and stages >= 2:
                    act.wait_ge(g_mm, h * G_STEPS)
                copy_xnT(0, 0)
                run_steps(act, A_STEPS, 2, step)

            def gates(call):
                n0 = call * G_STEPS
                if call < HALVES:
                    act.wait_ge(a_mm, 3 * A_STEPS * (call + 1))
                for i in range(G_STEPS + 1):
                    b = i % 2
                    if i < G_STEPS:
                        act.wait_ge(g_tT_psum, n0 + i + 1)
                        wait(act, g_mm, n0 + i - 1)
                        nc.scalar.copy(xnT[:, b, :], ps[:, b, :]).then_inc(g_tT, 1)
                    if i:
                        j = i - 1
                        act.wait_ge(g_mm, n0 + j + 1)
                        nc.scalar.copy(logits[:, j * QUAD:(j + 1) * QUAD, :].rearrange("p t e -> p (t e)"),
                                       ps[:, 2 + j % 2, 0:QUAD * E]).then_inc(g_logits, 1)
                        for t in range(call % HALVES * HT + j * QUAD, call % HALVES * HT + (j + 1) * QUAD):
                            last = nc.scalar.activation(x[:, t, :], x[:, t, :], ACT.Identity, bias=res_bias[:, t:t + 1],
                                                        scale=res_scale[:, t:t + 1])
                        last.then_inc(g_res, 1)
                act.wait_ge(r_diff, call + 1)
                nc.scalar.activation(ex[:, :], m2[:, :], ACT.Exp).then_inc(r_exp, 1)

            def experts(call, h):
                n0 = call * E_STEPS

                def feed(m, b):
                    act.wait_ge(e_tT_psum, n0 + m + 1)
                    wait(act, e_h_psum, n0 + m - 1)
                    nc.scalar.copy(tT[:, b, :], ps[:, b, 0:SLOTS]).then_inc(e_tT, 1)
                    e = act.value_load(step_exp[0:1, h, bass.ds(m, 1)], min_val=0, max_val=E - 1)
                    wait(act, e_h, n0 + m - 1)
                    nc.scalar.copy(w1s[:, b, :], tile_of(w1T, e)).then_inc(e_w1, 1)

                def step(m, k):
                    b = k % 2
                    if not isinstance(m, int) or m + 1 < E_STEPS:
                        feed(m + 1, 1 - b)
                    act.wait_ge(e_h_psum, n0 + m + 1)
                    wait(act, e_o_psum, n0 + m - 1)
                    for c in range(HC):
                        last = nc.scalar.activation(hT[:, b, c, :], ps[:, 2 + b, c * SLOTS:(c + 1) * SLOTS], ACT.Gelu,
                                                    bias=w1s[:, b, HID + c:HID + c + 1])
                    last.then_inc(e_h, 1)
                feed(0, 0)
                run_steps(act, E_STEPS, E_UNROLL, step)

            def layer_b(h):
                scores = scores_of(h)
                n0 = h * B_STEPS

                def front(m, b):
                    act.wait_ge(b_xnT_psum, n0 + m + 1)
                    wait(act, b_qkv, n0 + m)
                    nc.scalar.copy(b_xnT[:, :], ps[:, 0, 0:S]).then_inc(b_xnT_ok, 1)
                    act.wait_ge(b_qkv, n0 + m + 1)
                    wait(act, b_feat, n0 + m)
                    nc.scalar.activation(b_exp[:, :], ps[:, 1, :], ACT.Exp).then_inc(b_expd, 1)
                    wait(act, b_o_psum, 2 * (n0 + m) - 2)
                    for t in range(2):
                        last = nc.scalar.copy(plain_v(b, t), ps[:, 2, t * P:(t + 1) * P].rearrange(
                            "p (g k e) -> p g k e", g=4, k=4))
                    last.then_inc(b_v, 1)

                def middle(m, b):
                    act.wait_ge(b_kt_psum, n0 + m + 1)
                    wait(act, b_st_psum, n0 + m)
                    nc.scalar.copy(k_tok[:, :], ps[:, 0, S:S + P]).then_inc(b_kt, 1)
                    act.wait_ge(b_rec, n0 + m + 1)
                    wait(act, b_rT, n0 + m)
                    nc.scalar.copy(recx[:, :, :], rec[:, :].rearrange("p (h a) -> p h a", a=1).to_broadcast(
                        [P, 2 * HEADS, HD])).then_inc(b_recx, 1)

                def split(m, b):
                    act.wait_ge(b_q, n0 + m + 1)
                    wait(act, b_sc, 8 * (n0 + m - 1))
                    for k in range(4):
                        last = nc.scalar.activation(qx[:, b, k, :], qk[:, b, 0, :], ACT.Copy, scale=head_pick[:, k:k + 1])
                    last.then_inc(b_qx, 1)

                def out(n, b, blk):
                    act.wait_ge(b_o_psum, 2 * (n0 + n) + blk + 1)
                    wait(act, b_y, n0 + n - 1)
                    nc.scalar.copy(oT[:, b, blk * P:(blk + 1) * P], ps[:, 7, blk * P:(blk + 1) * P]).then_inc(b_o, 1)

                def step(n, b):
                    more = not isinstance(n, int) or n + 1 < B_STEPS
                    if more:
                        front(n + 1, 1 - b)
                    out(n, b, 0)
                    if more:
                        middle(n + 1, 1 - b)
                        split(n + 1, 1 - b)
                    out(n, b, 1)
                if h == 0:
                    act.wait_ge(vx_zero, 1)
                front(0, 0)
                middle(0, 0)
                split(0, 0)
                run_steps(act, B_STEPS, 2, step)

            for rnd in range(2):
                for h in range(HALVES):
                    if rnd == 0:
                        root(sv[:, 0, :], sv[:, 1, :])
                        root(sv[:, 0, :], sv[:, 3, :])
                        layer_a(h)
                    elif stages >= 3:
                        root(sv[:, 0, :], sv[:, 1, :])
                        layer_b(h)
                    if rnd * 2 + 2 <= stages:
                        root(sv[:, 0, :], sv[:, 1, :])
                        root(sv[:, 0, :], sv[:, 3, :])
                        gates(rnd * HALVES + h)
                for h in range(HALVES):
                    if rnd * 2 + 2 <= stages:
                        act.wait_ge(r_slots, rnd * HALVES + h + 1)
                        experts(rnd * HALVES + h, h)

        @block.vector
        def _(dve):
            links = [0]

            def link(ins):
                links[0] += 1
                ins.then_inc(chain, 1)
                dve.wait_ge(chain, links[0])

            sqrts = [0]

            def inv_root(dst, scratch, n):
                v, r = sv[:, 0, :], sv[:, n, :]
                sqrts[0] += 1
                dve.wait_ge(sqrt_ready, sqrts[0])
                link(nc.vector.reciprocal(r, r))
                link(nc.vector.tensor_tensor(sv[:, 4, :], r, r, ALU.mult))
                link(nc.vector.tensor_tensor(sv[:, 4, :], sv[:, 4, :], v, ALU.mult))
                link(nc.vector.tensor_scalar(sv[:, 4, :], sv[:, 4, :], -0.5, 1.5, ALU.mult, ALU.add))
                link(nc.vector.tensor_tensor(dst, r, sv[:, 4, :], ALU.mult))

            def moments(h):
                sl = slice(h * HT, (h + 1) * HT)
                me, qe, mo, qo = (stats[:, sl, k] for k in (1, 2, 4, 5))
                link(nc.vector.tensor_tensor(sv[:, 0, :], me, mo, ALU.subtract))
                link(nc.vector.tensor_tensor(sv[:, 0, :], sv[:, 0, :], sv[:, 0, :], ALU.mult))
                link(nc.vector.tensor_scalar(sv[:, 0, :], sv[:, 0, :], 0.25, None, ALU.mult))
                link(nc.vector.tensor_tensor(sv[:, 1, :], qe, qo, ALU.add))
                link(nc.vector.scalar_tensor_tensor(out=var[:, sl], in0=sv[:, 1, :], scalar=1.0 / D, in1=sv[:, 0, :],
                                                    op0=ALU.mult, op1=ALU.add))
                link(nc.vector.tensor_tensor(sv[:, 1, :], me, mo, ALU.add))
                link(nc.vector.tensor_scalar(mean[:, sl], sv[:, 1, :], 0.5, None, ALU.mult))
                nc.vector.tensor_scalar(sv[:, 0, :], var[:, sl], LN_EPS, None, ALU.add).then_inc(ve_ready, 1)
                inv_root(rstd[:, sl], sv, 1)

            def scale_a(h):
                sl = slice(h * HT, (h + 1) * HT)
                link(nc.vector.tensor_tensor(sv[:, 0, :], rstd[:, sl], rstd[:, sl], ALU.mult))
                link(nc.vector.tensor_tensor(sv[:, 0, :], sv[:, 0, :], var[:, sl], ALU.mult))
                link(nc.vector.tensor_scalar(sv[:, 0, :], sv[:, 0, :], float(D), A_EPS * A_EPS, ALU.mult, ALU.max))
                nc.vector.tensor_copy(sv[:, 2, :], sv[:, 0, :]).then_inc(ve_ready, 1)
                inv_root(sv[:, 2, :], sv, 3)
                link(nc.vector.tensor_scalar(sv[:, 2, :], sv[:, 2, :], SCALE, None, ALU.mult))
                link(nc.vector.tensor_tensor(rstd[:, sl], rstd[:, sl], sv[:, 2, :], ALU.mult))

            def scale_f(h):
                sl = slice(h * HT, (h + 1) * HT)
                nc.vector.tensor_scalar(res_scale[:, sl], rstd[:, sl], 1.0, None, ALU.add)
                nc.vector.scalar_tensor_tensor(out=res_bias[:, sl], in0=mean[:, sl], scalar=-1.0, in1=rstd[:, sl],
                                               op0=ALU.mult, op1=ALU.mult)
                link(nc.vector.tensor_tensor(sv[:, 0, :], rstd[:, sl], rstd[:, sl], ALU.mult))
                link(nc.vector.tensor_tensor(sv[:, 0, :], sv[:, 0, :], var[:, sl], ALU.mult))
                link(nc.vector.tensor_scalar(sv[:, 0, :], sv[:, 0, :], RMS_EPS, None, ALU.add))
                nc.vector.tensor_copy(sv[:, 2, :], sv[:, 0, :]).then_inc(ve_ready, 1)
                inv_root(sv[:, 2, :], sv, 3)
                link(nc.vector.tensor_tensor(rstd[:, sl], rstd[:, sl], sv[:, 2, :], ALU.mult))

            def normalise(dst, t):
                return nc.vector.tensor_scalar(dst, tile_of(x, t), mean[:, bass.ds(t, 1)], rstd[:, bass.ds(t, 1)],
                                               ALU.subtract, ALU.mult)

            def tile_stats(t):
                return nc.vector.bn_stats(tile_of(stats, t), tile_of(x, t))

            def layer_a(h):
                n0 = h * A_STEPS
                t0 = h * HT

                def norm(i, b):
                    wait(dve, a_xnT_psum, n0 + i - 1)
                    for t in range(QUAD):
                        last = normalise(xn[:, b, t, :], t0 + i * QUAD + t)
                    last.then_inc(a_xn, 1)

                def scan(i, b):
                    dve.wait_ge(a_gate, n0 + i + 1)
                    dve.wait_ge(a_mm, (n0 + i) * 3 + 3)
                    wait(dve, a_back, n0 + i - 1)
                    for k in range(QUAD * P // S):
                        last = nc.vector.tensor_tensor_scan(yq[:, b, k * S:(k + 1) * S], gate[:, b, k * S:(k + 1) * S],
                                                            ps[:, 4 + b, k * S:(k + 1) * S], 0.0, ALU.mult, ALU.add)
                    last.then_inc(a_scan, 1)
                    dve.wait_ge(a_scan, n0 + i + 1)
                    nc.vector.tensor_tensor(yq[:, b, :], yq[:, b, :], ps[:, 2 + b, :], ALU.mult).then_inc(a_yq, 1)

                def add(i):
                    dve.wait_ge(a_back, n0 + i + 1)
                    xs = x[:, bass.ds(t0 + i * QUAD, QUAD), :]
                    nc.vector.tensor_tensor(xs, xs, ps[:, 1, :].rearrange("p (t d) -> p t d", d=D), ALU.add
                                            ).then_inc(a_added, 1)
                    dve.wait_ge(a_added, n0 + i + 1)
                    for t in range(QUAD):
                        tile_stats(t0 + i * QUAD + t)

                def step(i, b):
                    if not isinstance(i, int) or i + 2 < A_STEPS:
                        norm(i + 2, b)
                    scan(i, b)
                    if not is_at(i, 0):
                        add(i - 1)
                norm(0, 0)
                norm(1, 1)
                run_steps(dve, A_STEPS, 2, step)
                add(A_STEPS - 1)
                link(nc.vector.tensor_copy(sv[:, 4, 0:1], sv[:, 5, 0:1]))

            def gates(call, h):
                n0 = call * G_STEPS
                if call == 0:
                    dve.wait_ge(wT_psum, 2)
                wait(dve, scattered[h], 16 * 2 * HT * (call // HALVES))
                with dve.Fori(0, G_STEPS) as i:
                    for t in range(QUAD):
                        last = normalise(tile_of(t_rows[:, h, :, :], i * QUAD + t), h * HT + i * QUAD + t)
                    last.then_inc(g_t, 1)
                route(call, h)

            def route(call, h):
                V = nc.vector
                tiles = [P, HT, E]

                def per_tile(v):
                    return v.rearrange("p (t a) -> p t a", a=1).to_broadcast(tiles)
                descb = desc[:, :].rearrange("p (a e) -> p a e", a=1).to_broadcast(tiles)
                dve.wait_ge(g_logits, (call + 1) * G_STEPS)
                if call == 0:
                    dve.wait_ge(consts, ALL_CONSTS)
                wait(dve, r_rank, call)
                for src, m, pick in ((logits, m1, pick1), (r_b, m2, pick2)):
                    if m is m2:
                        link(V.scalar_tensor_tensor(out=r_b[:, :, :], in0=pick1[:, :, :], scalar=-BIG,
                                                    in1=logits[:, :, :], op0=ALU.mult, op1=ALU.add))
                    link(V.tensor_reduce(m[:, :], src[:, :, :], X, ALU.max))
                    link(V.tensor_tensor(r_a[:, :, :], src[:, :, :], per_tile(m[:, :]), ALU.is_equal))
                    link(V.tensor_tensor(r_a[:, :, :], r_a[:, :, :], descb, ALU.mult))
                    link(V.tensor_reduce(mi[:, :], r_a[:, :, :], X, ALU.max))
                    link(V.tensor_tensor(pick[:, :, :], per_tile(mi[:, :]), descb, ALU.is_equal))
                V.tensor_tensor(picked[:, :, :], pick1[:, :, :], pick2[:, :, :], ALU.add).then_inc(r_picked, 1)
                wait(dve, combined, call - 1)
                V.tensor_tensor(m2[:, :], m2[:, :], m1[:, :], ALU.subtract).then_inc(r_diff, 1)
                dve.wait_ge(r_exp, call + 1)
                link(V.tensor_scalar(m1[:, :], ex[:, :], 1.0, None, ALU.add))
                link(V.reciprocal(prob[:, 0, h, :], m1[:, :]))
                link(V.tensor_tensor(prob[:, 1, h, :], prob[:, 0, h, :], ex[:, :], ALU.mult))
                dve.wait_ge(r_rank, call + 1)
                te = "p (t e) -> p t e"
                link(V.tensor_copy(tile_tot[:, :, :], ps[:, 7, 0:HT * E].rearrange("p (t e) -> p e t", e=E)))
                flat = "p e t -> p (e t)"
                link(V.tensor_tensor_scan(tile_inc[:, :, :].rearrange(flat), not_first[:, :, :].rearrange(flat),
                                          tile_tot[:, :, :].rearrange(flat), 0.0, ALU.mult, ALU.add))
                link(V.tensor_scalar(cnt_i[:, :], tile_inc[:, :, HT - 1], float(SLOTS - 1), None, ALU.add))
                link(V.tensor_scalar(cnt_i[:, :], cnt_i[:, :], -SLOTS, None, ALU.bitwise_and))
                link(V.tensor_copy(cnt_f[:, :], cnt_i[:, :]))
                link(V.tensor_tensor_scan(ends[:, :], ones8[:, :], cnt_f[:, :], 0.0, ALU.mult, ALU.add))
                link(V.tensor_tensor(base[:, :], ends[:, :], cnt_f[:, :], ALU.subtract))
                link(V.tensor_tensor(tile_inc[:, :, :], tile_inc[:, :, :], tile_tot[:, :, :], ALU.subtract))
                link(V.tensor_tensor(tile_inc[:, :, :], tile_inc[:, :, :],
                                     base[:, :].rearrange("p (e a) -> p e a", a=1).to_broadcast([P, E, HT]), ALU.add))
                link(V.tensor_tensor(r_a[:, :, :], ps[:, 6, 0:HT * E].rearrange(te, e=E),
                                     tile_inc[:, :, :].rearrange("p e t -> p t e"), ALU.add))
                for k, pick in enumerate((pick1, pick2)):
                    link(V.tensor_tensor(r_b[:, :, :], r_a[:, :, :], pick[:, :, :], ALU.mult))
                    link(V.tensor_reduce(mi[:, :], r_b[:, :, :], X, ALU.add))
                    link(V.tensor_copy(slot[:, k, h, :], mi[:, :]))
                link(V.tensor_tensor(step_cmp[:, :, :],
                                     step_slot[:, :].rearrange("p (m a) -> p m a", a=1).to_broadcast([P, E_STEPS, E]),
                                     ends[:, :].rearrange("p (a e) -> p a e", a=1).to_broadcast([P, E_STEPS, E]),
                                     ALU.is_ge))
                link(V.tensor_reduce(step_e[:, :], step_cmp[:, :, :], X, ALU.add))
                V.tensor_scalar(step_exp[:, h, :], step_e[:, :], float(E - 1), None, ALU.min).then_inc(r_slots, 1)

            def experts(call, h):
                n0 = call * E_STEPS

                def step(m, k):
                    dve.wait_ge(e_o_psum, n0 + m + 1)
                    wait(dve, e_stored[k], rounds(call, m, k))
                    e = dve.value_load(step_exp[0:1, h, bass.ds(m, 1)], min_val=0, max_val=E - 1)
                    nc.vector.tensor_tensor(o_sb[:, k, :, :], ps[:, 4 + k % 2, 0:SLOTS].rearrange("p (s d) -> p s d", d=D),
                                            b2_all[:, bass.ds(e, 1), :].to_broadcast([P, SUB, D]), ALU.add
                                            ).then_inc(e_o, 1)
                run_steps(dve, E_STEPS, E_UNROLL, step)

            def combine(call, h):
                dve.wait_ge(gathered[h], 16 * 2 * HT * (call // HALVES + 1))
                dve.wait_ge(g_res, (call + 1) * G_STEPS)
                for k in range(2):
                    with dve.Fori(0, HT // 4) as i:
                        for j in range(4):
                            t = i * 4 + j
                            xt = tile_of(x, h * HT + t)
                            last = nc.vector.scalar_tensor_tensor(out=xt, in0=tile_of(got[:, k, :, :], t),
                                                                  scalar=prob[:, k, h, bass.ds(t, 1)], in1=xt,
                                                                  op0=ALU.mult, op1=ALU.add)
                    link(nc.vector.tensor_copy(sv[:, 4, 0:1], sv[:, 5, 0:1]))
                with dve.Fori(0, HT // 4) as i:
                    for j in range(4):
                        tile_stats(h * HT + i * 4 + j)
                nc.vector.tensor_copy(sv[:, 4, 0:1], sv[:, 5, 0:1]).then_inc(combined, 1)
                dve.wait_ge(combined, call + 1)

            def layer_b(h):
                scores = scores_of(h)
                n0 = h * B_STEPS
                t0 = h * HT

                def norm(m, b):
                    wait(dve, b_xnT_psum, n0 + m - 1)
                    for t in range(2):
                        last = normalise(b_xn[:, b, t, :], t0 + 2 * m + t)
                    last.then_inc(b_norm, 1)

                def features(m, b):
                    dve.wait_ge(b_expd, n0 + m + 1)
                    wait(dve, b_o_psum, 2 * (n0 + m) - 2)
                    nc.vector.tensor_scalar(b_exp[:, :], b_exp[:, :], 1.0, None, ALU.min).then_inc(b_clip, 1)
                    dve.wait_ge(b_clip, n0 + m + 1)
                    nc.vector.scalar_tensor_tensor(out=qk[:, b, :, :].rearrange("p a s -> p (a s)"), in0=ps[:, 1, :],
                                                   scalar=0.0, in1=b_exp[:, :], op0=ALU.max, op1=ALU.add
                                                   ).then_inc(b_feat, 1)
                    dve.wait_ge(b_feat, n0 + m + 1)
                    wait(dve, b_den, n0 + m)
                    nc.vector.tensor_tensor_scan(zc[:, :], one_row[:, :], qk[:, b, 1, :], 0.0, ALU.mult, ALU.add
                                                 ).then_inc(b_keys, 1)
                    dve.wait_ge(b_keys, n0 + m + 1)
                    nc.vector.tensor_tensor(qz[:, :], zc[:, :], qk[:, b, 0, :], ALU.mult).then_inc(b_qz, 1)

                def mask(n, b, blk, g):
                    dve.wait_ge(b_sc, 8 * (n0 + n) + 4 * blk + g + 1)
                    wait(dve, b_o_psum, 2 * (n0 + n) + blk - 1)
                    nc.vector.tensor_tensor(scores[:, blk, g, :, :], ps[:, 3 + g, :].rearrange("p (k i) -> p k i", k=4),
                                            causal[:, :].rearrange("p (a i) -> p a i", a=1).to_broadcast([P, 4, P]),
                                            ALU.mult).then_inc(b_masked, 1)

                def middle(m, b):
                    dve.wait_ge(b_den, n0 + m + 1)
                    wait(dve, b_recx, n0 + m)
                    nc.vector.tensor_scalar(den[:, :], ps[:, 2, S:S + 2 * HEADS], B_EPS, None, ALU.add).then_inc(b_eps, 1)
                    dve.wait_ge(b_eps, n0 + m + 1)
                    nc.vector.reciprocal(rec[:, :], den[:, :]).then_inc(b_rec, 1)
                    dve.wait_ge(b_st_psum, n0 + m + 1)
                    wait(dve, b_o_psum, 2 * (n0 + m) - 2)
                    nc.vector.tensor_tensor(state[:, b, 0:P], ps[:, 2, S + 2 * HEADS:S + 2 * HEADS + P], head_diag[:, :],
                                            ALU.mult).then_inc(b_st, 1)
                    dve.wait_ge(b_rT, n0 + m + 1)
                    nc.vector.tensor_tensor(qk[:, b, 0, :], qk[:, b, 0, :], ps[:, 0, 0:S], ALU.mult).then_inc(b_q, 1)

                def add(n):
                    dve.wait_ge(b_y, n0 + n + 1)
                    xs = x[:, bass.ds(t0 + n * 2, 2), :]
                    nc.vector.tensor_tensor(xs, xs, ps[:, 7, S:2 * S].rearrange("p (t d) -> p t d", d=D), ALU.add
                                            ).then_inc(b_added, 1)
                    dve.wait_ge(b_added, n0 + n + 1)
                    for t in range(2):
                        tile_stats(t0 + n * 2 + t)

                def step(n, b):
                    more = not isinstance(n, int) or n + 1 < B_STEPS
                    mask(n, b, 0, 0)
                    mask(n, b, 0, 1)
                    if not isinstance(n, int) or n + 2 < B_STEPS:
                        norm(n + 2, b)
                    mask(n, b, 0, 2)
                    mask(n, b, 0, 3)
                    if more:
                        features(n + 1, 1 - b)
                    if not is_at(n, 0):
                        add(n - 1)
                    for g in range(4):
                        mask(n, b, 1, g)
                    if more:
                        middle(n + 1, 1 - b)
                norm(0, 0)
                norm(1, 1)
                features(0, 0)
                middle(0, 0)
                run_steps(dve, B_STEPS, 2, step)
                add(B_STEPS - 1)
                link(nc.vector.tensor_copy(sv[:, 4, 0:1], sv[:, 5, 0:1]))

            dve.wait_ge(consts, ALL_CONSTS)
            nc.vector.memset(vx[:, :, :, :], 0.0).then_inc(vx_zero, 1)
            for h in range(HALVES):
                dve.wait_ge(x_loaded[h], 16)
                with dve.Fori(0, HT // 4) as i:
                    for j in range(4):
                        tile_stats(h * HT + i * 4 + j)
                link(nc.vector.tensor_copy(sv[:, 4, 0:1], sv[:, 5, 0:1]))
            for rnd in range(2):
                for h in range(HALVES):
                    if rnd == 0:
                        moments(h)
                        scale_a(h)
                        layer_a(h)
                    elif stages >= 3:
                        combine(h, h)
                        moments(h)
                        layer_b(h)
                    if rnd * 2 + 2 <= stages:
                        moments(h)
                        scale_f(h)
                        gates(rnd * HALVES + h, h)
                for h in range(HALVES):
                    if rnd * 2 + 2 <= stages:
                        experts(rnd * HALVES + h, h)
                if rnd * 2 + 2 <= stages < rnd * 2 + 3:
                    for h in range(HALVES):
                        combine(rnd * HALVES + h, h)
            if stages == 1:
                link(nc.vector.tensor_copy(sv[:, 4, 0:1], sv[:, 5, 0:1]))
                nc.vector.tensor_copy(sv[:, 4, 0:1], sv[:, 5, 0:1]).then_inc(combined, 1)
                dve.wait_ge(combined, call + 1)


_INS = ['L0_attn_a_x', 'L0_attn_a_W_qkva', 'L0_attn_a_gamma', 'L0_attn_b_wq', 'L0_attn_b_wk', 'L0_attn_b_wv',
        'L0_attn_b_wo', 'L0_ffn_norm_weight', 'L0_ffn_gate_w', 'L0_ffn_w1', 'L0_ffn_b1', 'L0_ffn_w2', 'L0_ffn_b2']
STAGES = 4


def kernel(**inputs):
    import numpy as _np
    import concourse.bacc as _bacc
    from concourse import mybir as _mybir
    from concourse.bass_utils import run_bass_kernel_spmd as _run

    nc = _bacc.Bacc("TRN2", target_bir_lowering=False, num_devices=1)
    arrays, args = {}, []
    for name in _INS:
        a = _np.ascontiguousarray(inputs[name])
        arrays[f"in_{name}"] = a
        args.append(nc.dram_tensor(f"in_{name}", a.shape, _mybir.dt.from_np(a.dtype), kind="ExternalInput").ap())
    out = nc.dram_tensor("out_x", inputs['L0_attn_a_x'].shape, _mybir.dt.float32, kind="ExternalOutput").ap()
    build_hybrid(nc, *args, out, stages=STAGES)
    r = _run(nc, [arrays], core_ids=[0])
    return r.results[0]["out_x"]
```

```python
from contextlib import ExitStack

import concourse.bass as bass
from concourse import mybir

F32 = mybir.dt.float32
BF16 = mybir.dt.bfloat16
I32 = mybir.dt.int32
U32 = mybir.dt.uint32
ALU = mybir.AluOpType
ACT = mybir.ActivationFunctionType
X = mybir.AxisListType.X
P = 128

HEADS, HD = 16, 8
LN_EPS = 1e-5
A_EPS = 1e-12
RMS_EPS = 1e-6
B_EPS = 1e-6
PARTS = 2
HALVES = 2
QUAD = 4
SLOTS = 256
BIG = 3.0e38


def straight(lo, hi, unroll, body):
    for m in range(lo, hi):
        body(m, m % unroll)


def looped(eng, lo, hi, unroll, body):
    with eng.Fori(lo // unroll, hi // unroll) as n:
        for j in range(unroll):
            body(n * unroll + j, j)


def run_steps(eng, steps, unroll, body):
    straight(0, unroll, unroll, body)
    looped(eng, unroll, steps - unroll, unroll, body)
    straight(steps - unroll, steps, unroll, body)


def is_at(step, n):
    return isinstance(step, int) and step == n


def wait(eng, sem, value):
    if not isinstance(value, int) or value > 0:
        eng.wait_ge(sem, value)


def build_hybrid(nc, x_in, w_qkva, gamma, b_wq, b_wk, b_wv, b_wo, norm_w, gate_w, w1, b1, w2, b2, x_out, stages=4):
    B, S, D = x_in.shape
    E, HID, _ = w1.shape
    HC = HID // P
    TILES = B * S // P
    HT = TILES // HALVES
    PT = HT // PARTS
    CHUNKS = HT // QUAD
    PART_CHUNKS = PT // QUAD
    A_STEPS = HT // QUAD
    B_STEPS = HT * P // S
    G_STEPS = HT // QUAD
    E_UNROLL = 8
    AHEAD = 6
    E_STEPS = -(-((2 * HT * P + E * (SLOTS - 1)) // SLOTS) // E_UNROLL) * E_UNROLL
    ROWS = E_STEPS * SLOTS
    SUB = SLOTS // P
    W1C = HID + HC
    SCALE = float(D) ** 0.5
    assert D == P and S == 2 * P and HEADS * HD == D and SLOTS == 2 * P

    x_tiles = x_in.rearrange("b (t p) d -> p (b t) d", p=P)
    out_tiles = x_out.rearrange("b (t p) d -> p (b t) d", p=P)
    tok_rows = [nc.dram_tensor(f"tok_rows{h}", [ROWS, D], F32).ap() for h in range(HALVES)]
    exp_rows = [nc.dram_tensor(f"exp_rows{h}", [ROWS, D], F32).ap() for h in range(HALVES)]

    with ExitStack() as ctx:
        def sb(name, shape, dt=F32):
            return ctx.enter_context(nc.sbuf_tensor(name, shape, dt))

        def sem(name):
            return ctx.enter_context(nc.semaphore(name))

        ps = ctx.enter_context(nc.psum_tensor("ps", [P, 8, 512], F32))
        x = sb("x", [P, TILES, D])
        ident = sb("ident", [P, P])
        before = sb("before", [P, P], BF16)
        ones = sb("ones", [P, P], BF16)
        causal = sb("causal", [P, P])
        head_diag = sb("head_diag", [P, P])
        head_sum = sb("head_sum", [P, HEADS])
        head_pick = sb("head_pick", [P, 4])
        desc = sb("desc", [P, E])
        step_slot = sb("step_slot", [P, E_STEPS])
        not_first = sb("not_first", [P, E, HT])
        ones8 = sb("ones8", [P, E])
        one_row = sb("one_row", [P, S])
        wa = sb("wa", [P, 3, P])
        wb = sb("wb", [P, 4, P])
        gT = sb("gT", [P, E])
        w1T = sb("w1T", [P, E, W1C])
        w2T = sb("w2T", [P, E * HC, P])
        b2_all = sb("b2_all", [P, E, D])
        gam = sb("gam", [P, 1])
        nw = sb("nw", [P, 1])
        stats = sb("stats", [P, TILES, 6])
        mean = sb("mean", [P, TILES])
        var = sb("var", [P, TILES])
        n_scale = sb("n_scale", [P, TILES])
        n_bias = sb("n_bias", [P, TILES])
        res_scale = sb("res_scale", [P, TILES])
        res_bias = sb("res_bias", [P, TILES])
        sv = sb("sv", [P, 6, 2 * HT])
        xn = sb("xn", [P, 2, QUAD, D])
        xnT = sb("xnT", [P, 2, QUAD * P])
        gate = sb("gate", [P, 2, QUAD * P])
        yq = sb("yq", [P, 2, QUAD * P])
        t_rows = sb("t_rows", [P, HALVES, HT, D])
        got = sb("got", [P, 2, HT, D])
        logits = sb("logits", [P, HT, E])
        r_a = sb("r_a", [P, HT, E])
        r_b = sb("r_b", [P, HT, E])
        pick1 = sb("pick1", [P, HT, E])
        pick2 = sb("pick2", [P, HT, E])
        picked = sb("picked", [P, HT, E], BF16)
        tile_tot = sb("tile_tot", [P, E, HT])
        tile_inc = sb("tile_inc", [P, E, HT])
        m1 = sb("m1", [P, HT])
        m2 = sb("m2", [P, HT])
        mi = sb("mi", [P, HT])
        ex = sb("ex", [P, HT])
        prob = sb("prob", [P, 2, HALVES, HT])
        cnt_i = sb("cnt_i", [P, E], I32)
        cnt_f = sb("cnt_f", [P, E])
        ends = sb("ends", [P, E])
        base = sb("base", [P, E])
        slot = sb("slot", [P, 2, HALVES, HT], U32)
        step_cmp = sb("step_cmp", [P, E_STEPS, E])
        step_e = sb("step_e", [P, E_STEPS])
        step_exp = sb("step_exp", [P, HALVES, E_STEPS], I32)
        ts = sb("ts", [P, E_UNROLL, SUB, D])
        tT = sb("tT", [P, 2, SLOTS])
        w1s = sb("w1s", [P, 2, W1C])
        hT = sb("hT", [P, 2, HC, SLOTS])
        o_sb = sb("o_sb", [P, E_UNROLL, SUB, D])

        VW = HEADS // 4 * (P + HD)
        b_xn = xn
        b_xnT = sb("b_xnT", [P, S])
        b_exp = sb("b_exp", [P, 2 * S])
        qk = sb("qk", [P, 2, 2, S])
        zc = sb("zc", [P, S])
        qz = sb("qz", [P, S])
        den = sb("den", [P, 2 * HEADS])
        rec = sb("rec", [P, 2 * HEADS])
        recx = sb("recx", [P, 2 * HEADS, HD])
        qx = sb("qx", [P, 2, 4, S])
        group_mask = sb("group_mask", [P, 4])
        vx = sb("vx", [P, 2, 2, VW])
        k_tok = sb("k_tok", [P, P])
        kx = ts[:, :, :, :].rearrange("p (b g) s d -> p b g (s d)", b=2)
        state = gate
        oT = yq
        recT = yq[:, :, S:2 * S]

        x_loaded = [sem(f"x_loaded{n}") for n in range(HALVES)]
        scaled_a, scaled_f, scaled_b = (sem(f"scaled_{n}") for n in "afb")
        w_loaded = sem("w_loaded")
        consts = sem("consts")
        wT_psum = sem("wT_psum")
        wT_done = sem("wT_done")
        chain = sem("chain")
        pchain = sem("pchain")
        first_bn = sem("first_bn")
        a_xn, a_xnT_psum, a_xnT, a_mm, a_gate, a_scan, a_yq, a_back, a_added = (
            sem(f"a_{n}") for n in ("xn", "xnT_psum", "xnT", "mm", "gate", "scan", "yq", "back", "added"))
        g_t, g_tT_psum, g_tT, g_mm, g_logits, g_res = (
            sem(f"g_{n}") for n in ("t", "tT_psum", "tT", "mm", "logits", "res"))
        r_diff, r_exp, r_picked, r_rank, r_read, r_slots = (
            sem(f"r_{n}") for n in ("diff", "exp", "picked", "rank", "read", "slots"))
        zeroed = [sem(f"zeroed{h}") for h in range(HALVES)]
        zero_tile = sem("zero_tile")
        scattered = [sem(f"scattered{h}") for h in range(HALVES)]
        gathered = [[sem(f"gathered{h}_{q}") for q in range(PARTS)] for h in range(HALVES)]
        e_loaded = [sem(f"e_loaded{k}") for k in range(E_UNROLL)]
        e_stored = [sem(f"e_stored{k}") for k in range(E_UNROLL)]
        e_tT_psum, e_tT, e_w1, e_h_psum, e_h, e_o_psum, e_o = (
            sem(f"e_{n}") for n in ("tT_psum", "tT", "w1", "h_psum", "h", "o_psum", "o"))
        (b_norm, b_xnT_psum, b_xnT_ok, b_qkv, b_expd, b_feat, b_qz, b_den, b_rec, b_recx, b_kt_psum, b_kt, b_st_psum,
         b_st, b_rT, b_recT, b_qx, b_v, b_sc, b_masked, b_o_psum, b_o, b_y, b_added) = (sem(f"b_{n}") for n in (
             "norm", "xnT_psum", "xnT_ok", "qkv", "expd", "feat", "qz", "den", "rec", "recx", "kt_psum", "kt", "st_psum",
             "st", "rT", "recT", "qx", "v", "sc", "masked", "o_psum", "o", "y", "added"))
        b_clip, b_keys, b_eps, b_kx = (sem(f"b_{n}") for n in ("clip", "keys", "eps", "kx"))
        vx_zero = sem("vx_zero")
        first_added = sem("first_added")
        combined = sem("combined")
        stored = sem("stored")

        def rounds(call, m, k):
            per = 16 // E_UNROLL
            return 16 * call * (E_STEPS // E_UNROLL) + (m - k) * per

        def plain_v(b, t):
            return vx[:, b, t, :].rearrange("p (k z) -> p k z", k=4)[:, :, 0:P].rearrange("p k (g c) -> p g k c", g=4)[
                :, :, :, 0:HD]

        def scores_of(h):
            return t_rows[:, h, :, :].rearrange("p (t g k) d -> p t g k d", t=2, g=4)

        def tile_of(buf, i):
            return buf[:, bass.ds(i, 1), :].rearrange("p a d -> p (a d)")

        block = ctx.enter_context(nc.Block())
        ALL_CONSTS = 13
        LOADS = 12

        @block.sync
        def _(sp):
            for h in range(HALVES):
                sp.dma_start(x[:, h * HT:(h + 1) * HT, :], x_tiles[:, h * HT:(h + 1) * HT, :]).then_inc(x_loaded[h], 16)
                if h == 0:
                    sp.wait_ge(x_loaded[0], 16)
                    sp.wait_ge(w_loaded, 16 * LOADS)
            sp.wait_ge(x_loaded[1], 16)
            sp.wait_ge(zero_tile, 1)
            zt = got[:, 0, 0:16, :].rearrange("p t d -> p (t d)")
            for h in range(HALVES):
                for c in range(ROWS // (16 * P)):
                    sp.dma_start(tok_rows[h][c * 16 * P:(c + 1) * 16 * P, :].rearrange("(p t) d -> p (t d)", t=16),
                                 zt).then_inc(zeroed[h], 16)

            def experts(call, h):
                sp.wait_ge(scattered[h], 16 * 2 * HT * (call // HALVES + 1))
                if call == HALVES:
                    sp.wait_ge(b_sc, 8 * HALVES * B_STEPS)
                n0 = call * E_STEPS

                def load(m, k):
                    wait(sp, e_tT_psum, n0 + m - (E_UNROLL - 1))
                    sp.dma_start(ts[:, k, :, :], tok_rows[h][bass.ds(m * SLOTS, SLOTS), :].rearrange(
                        "(p s) d -> p s d", s=SUB)).then_inc(e_loaded[k], 16)

                def store(m, k):
                    sp.wait_ge(e_o, n0 + m + 1)
                    sp.dma_start(exp_rows[h][bass.ds(m * SLOTS, SLOTS), :].rearrange("(p s) d -> p s d", s=SUB),
                                 o_sb[:, k, :, :]).then_inc(e_stored[k], 16)

                def step(m, k):
                    if not isinstance(m, int) or m + AHEAD < E_STEPS:
                        load(m + AHEAD, (k + AHEAD) % E_UNROLL)
                    store(m, k)
                for m in range(AHEAD):
                    load(m, m)
                run_steps(sp, E_STEPS, E_UNROLL, step)

            if stages >= 2:
                for rnd in range(stages // 2):
                    for h in range(HALVES):
                        experts(rnd * HALVES + h, h)
            for h in range(HALVES):
                for q in range(PARTS):
                    sp.wait_ge(combined, (HALVES + h) * CHUNKS + (q + 1) * PART_CHUNKS)
                    tiles = slice(h * HT + q * PT, h * HT + (q + 1) * PT)
                    sp.dma_start(out_tiles[:, tiles, :], x[:, tiles, :]).then_inc(stored, 16)
            sp.wait_ge(stored, 16 * HALVES * PARTS)

        @block.gpsimd
        def _(pool):
            links = [0]

            def link(ins):
                links[0] += 1
                ins.then_inc(pchain, 1)
                pool.wait_ge(pchain, links[0])

            nc.gpsimd.memset(got[:, 0, 0:16, :], 0.0).then_inc(zero_tile, 1)
            link(nc.gpsimd.memset(ident[:, :], 0.0))
            nc.gpsimd.affine_select(out=ident[:, :], in_=ident[:, :], compare_op=ALU.not_equal, fill=1.0, base=0,
                                    pattern=[[-1, P]], channel_multiplier=1).then_inc(consts, 1)
            nc.gpsimd.memset(ones[:, :], 1.0).then_inc(consts, 1)
            nc.gpsimd.memset(one_row[:, :], 1.0).then_inc(consts, 1)
            link(nc.gpsimd.memset(before[:, :], 1.0))
            nc.gpsimd.affine_select(out=before[:, :], in_=before[:, :], compare_op=ALU.is_gt, fill=0.0, base=0,
                                    pattern=[[1, P]], channel_multiplier=-1).then_inc(consts, 1)
            link(nc.gpsimd.memset(causal[:, :], 1.0))
            nc.gpsimd.affine_select(out=causal[:, :], in_=causal[:, :], compare_op=ALU.is_ge, fill=0.0, base=0,
                                    pattern=[[1, P]], channel_multiplier=-1).then_inc(consts, 1)
            link(nc.gpsimd.memset(head_diag[:, :], 1.0))
            hd3 = head_diag[:, :].rearrange("p (h e) -> p h e", e=HD)
            link(nc.gpsimd.affine_select(out=hd3, in_=hd3, compare_op=ALU.is_ge, fill=0.0, base=0,
                                         pattern=[[-HD, HEADS], [0, HD]], channel_multiplier=1))
            link(nc.gpsimd.affine_select(out=hd3, in_=hd3, compare_op=ALU.is_ge, fill=0.0, base=HD - 1,
                                         pattern=[[HD, HEADS], [0, HD]], channel_multiplier=-1))
            nc.gpsimd.tensor_copy(head_sum[:, :], hd3[:, :, 0]).then_inc(consts, 1)
            link(nc.gpsimd.memset(desc[:, :], 1.0))
            for e in range(E):
                last = nc.gpsimd.memset(desc[:, e:e + 1], float(E - e))
            last.then_inc(consts, 1)
            nc.gpsimd.iota(step_slot[:, :], pattern=[[SLOTS, E_STEPS]], base=0, channel_multiplier=0,
                           allow_small_or_imprecise_dtypes=True).then_inc(consts, 1)
            link(nc.gpsimd.memset(not_first[:, :, :], 1.0))
            nc.gpsimd.memset(not_first[:, :, 0:1], 0.0).then_inc(consts, 1)
            nc.gpsimd.memset(ones8[:, :], 1.0).then_inc(consts, 1)
            link(nc.gpsimd.memset(head_pick[:, :], 0.0))
            pool.wait_ge(consts, 10)
            hs4 = head_sum[:, :].rearrange("p (g k) -> p g k", k=4)
            link(nc.gpsimd.tensor_tensor(head_pick[:, :], hs4[:, 0, :], hs4[:, 1, :], ALU.add))
            link(nc.gpsimd.tensor_tensor(head_pick[:, :], head_pick[:, :], hs4[:, 2, :], ALU.add))
            nc.gpsimd.tensor_tensor(head_pick[:, :], head_pick[:, :], hs4[:, 3, :], ALU.add).then_inc(consts, 1)
            link(nc.gpsimd.memset(group_mask[:, :], 1.0))
            link(nc.gpsimd.affine_select(out=group_mask[:, :], in_=group_mask[:, :], compare_op=ALU.is_ge, fill=0.0, base=0,
                                         pattern=[[-4 * HD, 4]], channel_multiplier=1))
            nc.gpsimd.affine_select(out=group_mask[:, :], in_=group_mask[:, :], compare_op=ALU.is_ge, fill=0.0,
                                    base=4 * HD - 1, pattern=[[4 * HD, 4]], channel_multiplier=-1).then_inc(consts, 1)
            nc.gpsimd.memset(sv[:, 5, :], 1.0).then_inc(consts, 1)

            def scatter(call, h):
                pool.wait_ge(r_slots, call + 1)
                pool.wait_ge(zeroed[h], 16 * (ROWS // (16 * P)))
                for t in range(HT):
                    for k in range(2):
                        pool.indirect_dma_start(tok_rows[h], bass.IndirectOffsetOnAxis(ap=slot[:, k, h, t:t + 1], axis=0),
                                                t_rows[:, h, t, :], None).then_inc(scattered[h], 16)

            def gather(call, h):
                for k in range(E_UNROLL):
                    pool.wait_ge(e_stored[k], 16 * (E_STEPS // E_UNROLL) * (call + 1))
                for q in range(PARTS):
                    wait(pool, combined, (call - 1) * CHUNKS + (q + 1) * PART_CHUNKS)
                    for t in range(q * PT, (q + 1) * PT):
                        for k in range(2):
                            pool.indirect_dma_start(got[:, k, t, :], None, exp_rows[h],
                                                    bass.IndirectOffsetOnAxis(ap=slot[:, k, h, t:t + 1], axis=0)
                                                    ).then_inc(gathered[h][q], 16)
            for rnd in range(stages // 2):
                for h in range(HALVES):
                    scatter(rnd * HALVES + h, h)
                for h in range(HALVES):
                    gather(rnd * HALVES + h, h)

        @block.tensor
        def _(pe):
            pe.wait_ge(consts, ALL_CONSTS)
            pe.wait_ge(w_loaded, 16 * LOADS)
            wrows = t_rows[:, 0, :, :]
            groups = [range(0, 4), range(4, 8), range(8, 12), range(12, 16), range(16, 20), range(20, 24), range(24, 28),
                      range(28, 32), range(32, 35)]
            big = t_rows[:, :, :, :].rearrange("p h t d -> p (h t) d")
            for n, group in enumerate(groups):
                for k, r in enumerate(group):
                    last = nc.tensor.transpose(ps[:, n % 8, k * P:(k + 1) * P], big[:, r, :], ident[:, :])
                if n == 7:
                    last.then_inc(wT_psum, 1)
                    pe.wait_ge(wT_done, 1)
            r = big[0:E, 35, :]
            nc.tensor.transpose(ps[:, 0, 3 * P:3 * P + E], big[0:E, 35, :], ident[0:E, 0:E])
            nc.tensor.transpose(ps[:, 0, 3 * P + E:3 * P + E + E * HC], big[0:E * HC, 36, :],
                                ident[0:E * HC, 0:E * HC]).then_inc(wT_psum, 1)

            def layer_a(h):
                n0 = h * A_STEPS

                def turn(i, b):
                    pe.wait_ge(a_xn, n0 + i + 1)
                    wait(pe, a_xnT, n0 + i)
                    for t in range(QUAD):
                        last = nc.tensor.transpose(ps[:, 0, t * P:(t + 1) * P], xn[:, b, t, :], ident[:, :])
                    last.then_inc(a_xnT_psum, 1)

                def project(i, b):
                    pe.wait_ge(a_xnT, n0 + i + 1)
                    wait(pe, a_yq, n0 + i - 1)
                    for bank, c in ((6, 2), (4, 1), (2, 0)):
                        nc.tensor.matmul(ps[:, bank + b, :], wa[:, c, :], xnT[:, b, :], start=True,
                                         stop=True).then_inc(a_mm, 1)

                def back(i, b):
                    pe.wait_ge(a_yq, n0 + i + 1)
                    wait(pe, a_added, n0 + i)
                    for t in range(QUAD):
                        last = nc.tensor.transpose(ps[:, 1, t * P:(t + 1) * P], yq[:, b, t * P:(t + 1) * P], ident[:, :])
                    last.then_inc(a_back, 1)

                def step(i, b):
                    if not isinstance(i, int) or i + 1 < A_STEPS:
                        turn(i + 1, 1 - b)
                    project(i, b)
                    if not is_at(i, 0):
                        back(i - 1, 1 - b)
                turn(0, 0)
                run_steps(pe, A_STEPS, 2, step)
                back(A_STEPS - 1, 1)

            def gates(call):
                n0 = call * G_STEPS

                def turn(i, b):
                    pe.wait_ge(g_t, n0 + i + 1)
                    wait(pe, g_tT, n0 + i - 1)
                    for t in range(QUAD):
                        last = nc.tensor.transpose(ps[:, b, t * P:(t + 1) * P], t_rows[:, call % HALVES, i * QUAD + t, :],
                                                   ident[:, :])
                    last.then_inc(g_tT_psum, 1)

                def logit(i, b):
                    pe.wait_ge(g_tT, n0 + i + 1)
                    wait(pe, g_logits, n0 + i - 1)
                    for t in range(QUAD):
                        last = nc.tensor.matmul(ps[:, 2 + b, t * E:(t + 1) * E], xnT[:, b, t * P:(t + 1) * P], gT[:, :],
                                                start=True, stop=True)
                    last.then_inc(g_mm, 1)
                turn(0, 0)
                for i in range(G_STEPS):
                    if i + 1 < G_STEPS:
                        turn(i + 1, (i + 1) % 2)
                    logit(i, i % 2)
                pe.wait_ge(r_picked, call + 1)
                cols = picked[:, :, :].rearrange("p t e -> p (t e)")
                nc.tensor.matmul(ps[:, 6, 0:HT * E], before[:, :], cols, start=True, stop=True)
                nc.tensor.matmul(ps[:, 7, 0:HT * E], ones[:, :], cols, start=True, stop=True).then_inc(r_rank, 1)
                pe.wait_ge(r_read, call + 1)

            def experts(call, h):
                n0 = call * E_STEPS

                def turn(m, k):
                    pe.wait_ge(e_loaded[k], rounds(call, m, k) + 16)
                    wait(pe, e_tT, n0 + m - 1)
                    for s in range(SUB):
                        last = nc.tensor.transpose(ps[:, k % 2, s * P:(s + 1) * P], ts[:, k, s, :], ident[:, :])
                    last.then_inc(e_tT_psum, 1)

                def up(m, b):
                    pe.wait_ge(e_tT, n0 + m + 1)
                    pe.wait_ge(e_w1, n0 + m + 1)
                    wait(pe, e_h, n0 + m - 1)
                    for c in range(HC):
                        last = nc.tensor.matmul(ps[:, 2 + b, c * SLOTS:(c + 1) * SLOTS], w1s[:, b, c * P:(c + 1) * P],
                                                tT[:, b, :], start=True, stop=True)
                    last.then_inc(e_h_psum, 1)

                def down(m, b):
                    pe.wait_ge(e_h, n0 + m + 1)
                    wait(pe, e_o, n0 + m - 1)
                    e = pe.value_load(step_exp[0:1, h, bass.ds(m, 1)], min_val=0, max_val=E - 1)
                    for s in range(SUB):
                        for c in range(HC):
                            last = nc.tensor.matmul(ps[:, 4 + b, s * P:(s + 1) * P], hT[:, b, c, s * P:(s + 1) * P],
                                                    tile_of(w2T, e * HC + c), start=(c == 0), stop=(c == HC - 1))
                    last.then_inc(e_o_psum, 1)

                def step(m, k):
                    if not isinstance(m, int) or m + 1 < E_STEPS:
                        turn(m + 1, (k + 1) % E_UNROLL)
                    up(m, k % 2)
                    if not is_at(m, 0):
                        down(m - 1, (k + 1) % 2)
                turn(0, 0)
                run_steps(pe, E_STEPS, E_UNROLL, step)
                down(E_STEPS - 1, 1)

            def layer_b(h):
                scores = scores_of(h)
                n0 = h * B_STEPS

                def turn(m, b):
                    pe.wait_ge(b_norm, n0 + m + 1)
                    wait(pe, b_recT, n0 + m)
                    for t in range(2):
                        last = nc.tensor.transpose(ps[:, 0, t * P:(t + 1) * P], b_xn[:, b, t, :], ident[:, :])
                    last.then_inc(b_xnT_psum, 1)

                def project(m, b):
                    pe.wait_ge(b_xnT_ok, n0 + m + 1)
                    wait(pe, b_feat, n0 + m)
                    wait(pe, b_st, n0 + m)
                    for k in range(2):
                        nc.tensor.matmul(ps[:, 1, k * S:(k + 1) * S], wb[:, k, :], b_xnT[:, :], start=True, stop=True)
                    for t in range(2):
                        last = nc.tensor.matmul(ps[:, 2, t * P:(t + 1) * P], b_xnT[:, t * P:(t + 1) * P], wb[:, 2, :],
                                                start=True, stop=True)
                    last.then_inc(b_qkv, 1)

                def denominators(m, b):
                    pe.wait_ge(b_qz, n0 + m + 1)
                    pe.wait_ge(b_v, n0 + m + 1)
                    for t in range(2):
                        last = nc.tensor.matmul(ps[:, 2, S + t * HEADS:S + (t + 1) * HEADS], qz[:, t * P:(t + 1) * P],
                                                head_sum[:, :], start=True, stop=True)
                    last.then_inc(b_den, 1)
                    nc.tensor.transpose(ps[:, 0, S:S + P], qk[:, b, 1, 0:P], ident[:, :]).then_inc(b_kt_psum, 1)

                def states(m, b):
                    pe.wait_ge(b_kt, n0 + m + 1)
                    pe.wait_ge(b_eps, n0 + m + 1)
                    nc.tensor.matmul(ps[:, 2, S + 2 * HEADS:S + 2 * HEADS + P], k_tok[:, :], plain_v(b, 0), start=True,
                                     stop=True).then_inc(b_st_psum, 1)

                def turn_reciprocals(m, b):
                    pe.wait_ge(b_recx, n0 + m + 1)
                    for t in range(2):
                        last = nc.tensor.transpose(ps[:, 0, t * P:(t + 1) * P], recx[:, t * HEADS:(t + 1) * HEADS, :].rearrange(
                            "p h e -> p (h e)"), ident[:, :])
                    last.then_inc(b_rT, 1)

                def score(n, b, blk, g):
                    c = 8 * (n0 + n) + 4 * blk + g
                    wait(pe, b_masked, c - 3)
                    if g == 0 and blk == 0:
                        pe.wait_ge(b_kx, n0 + n + 1)
                        pe.wait_ge(b_qx, n0 + n + 1)
                    nc.tensor.matmul(ps[:, 3 + g, :], kx[:, b, g, blk * P:(blk + 1) * P], qx[:, b, :, blk * P:(blk + 1) * P],
                                     start=True, stop=True).then_inc(b_sc, 1)

                def weigh(n, b, blk):
                    pe.wait_ge(b_masked, 8 * (n0 + n) + 4 * blk + 4)
                    wait(pe, b_o, n0 + n)
                    out = ps[:, 7, blk * P:(blk + 1) * P]
                    if blk == 0:
                        wait(pe, b_added, n0 + n)
                    else:
                        pe.wait_ge(b_st, n0 + n + 1)
                        nc.tensor.matmul(out, state[:, b, 0:P], qk[:, b, 0, P:S], start=True, stop=False,
                                         skip_group_check=True)
                    for k in range(4):
                        for g in range(4):
                            q = slice(32 * g, 32 * g + 32)
                            last = nc.tensor.matmul(out[q, :], vx[:, b, blk, k * P + g * 32:k * P + g * 32 + 32],
                                                    scores[:, blk, g, k, :], start=(k == 0 and blk == 0), stop=(k == 3),
                                                    tile_position=(0, 32 * g), skip_group_check=True)
                    last.then_inc(b_o_psum, 1)

                def back(n, b):
                    pe.wait_ge(b_o, n0 + n + 1)
                    for t in range(2):
                        last = nc.tensor.matmul(ps[:, 7, S + t * P:S + (t + 1) * P], oT[:, b, t * P:(t + 1) * P],
                                                wb[:, 3, :], start=True, stop=True)
                    last.then_inc(b_y, 1)

                def step(n, b):
                    more = not isinstance(n, int) or n + 1 < B_STEPS
                    score(n, b, 0, 0)
                    score(n, b, 0, 1)
                    if more:
                        turn(n + 1, 1 - b)
                    score(n, b, 0, 2)
                    score(n, b, 0, 3)
                    if more:
                        project(n + 1, 1 - b)
                    if not is_at(n, 0):
                        back(n - 1, 1 - b)
                    for g in range(4):
                        score(n, b, 1, g)
                    if more:
                        denominators(n + 1, 1 - b)
                    weigh(n, b, 0)
                    if more:
                        states(n + 1, 1 - b)
                    weigh(n, b, 1)
                    if more:
                        turn_reciprocals(n + 1, 1 - b)
                turn(0, 0)
                project(0, 0)
                denominators(0, 0)
                states(0, 0)
                turn_reciprocals(0, 0)
                run_steps(pe, B_STEPS, 2, step)
                back(B_STEPS - 1, 1)

            for rnd in range(2):
                for h in range(HALVES):
                    if rnd == 0:
                        layer_a(h)
                    elif stages >= 3:
                        layer_b(h)
                    if rnd * 2 + 2 <= stages:
                        gates(rnd * HALVES + h)
                for h in range(HALVES):
                    if rnd * 2 + 2 <= stages:
                        experts(rnd * HALVES + h, h)

        @block.scalar
        def _(act):
            big = t_rows[:, :, :, :].rearrange("p h t d -> p (h t) d")
            act.dma_start(big[:, 32:35, :], w_qkva.rearrange("(c p) d -> p c d", p=P)).then_inc(w_loaded, 16)
            act.dma_start(big[:, 0:16, :], w1.rearrange("e (c p) d -> p (e c) d", p=P)).then_inc(w_loaded, 16)
            act.dma_start(big[:, 16:32, :].rearrange("p (e c) d -> p e (c d)", e=E),
                          w2.rearrange("e d h -> d e h")).then_inc(w_loaded, 16)
            act.dma_start(big[0:E, 35, :], gate_w).then_inc(w_loaded, 16)
            act.dma_start(big[0:E * HC, 36, :], b1.rearrange("e (c p) -> (e c) p", p=P)).then_inc(w_loaded, 16)
            act.dma_start(gam[:, :], gamma.rearrange("(p a) -> p a", a=1)).then_inc(w_loaded, 16)
            act.dma_start(nw[:, :], norm_w.rearrange("(p a) -> p a", a=1)).then_inc(w_loaded, 16)
            for k, w in enumerate((b_wq, b_wk, b_wv, b_wo)):
                act.dma_start(wb[:, k, :], w).then_inc(w_loaded, 16)
            act.dma_start(b2_all[:, :, :], b2.rearrange("(a e) d -> a e d", a=1).to_broadcast([P, E, D])).then_inc(w_loaded, 16)
            act.wait_ge(w_loaded, 16 * LOADS)
            act.wait_ge(wT_psum, 1)
            for n in range(4):
                for k in range(2):
                    nc.scalar.activation(w1T[:, 2 * n + k, 0:HID], ps[:, n, k * HID:(k + 1) * HID], ACT.Copy,
                                         scale=nw[:, 0:1])
            for n in range(4):
                last = nc.scalar.copy(w2T[:, 4 * n:4 * n + 4, :].rearrange("p a d -> p (a d)"), ps[:, 4 + n, :])
            last.then_inc(wT_done, 1)
            act.wait_ge(wT_psum, 2)
            nc.scalar.activation(wa[:, :, :].rearrange("p c e -> p (c e)"), ps[:, 0, 0:3 * P], ACT.Copy, scale=gam[:, 0:1])
            nc.scalar.activation(gT[:, :], ps[:, 0, 3 * P:3 * P + E], ACT.Copy, scale=nw[:, 0:1])
            nc.scalar.copy(w1T[:, :, HID:W1C], ps[:, 0, 3 * P + E:3 * P + E + E * HC].rearrange("p (e c) -> p e c", c=HC)
                           ).then_inc(wT_done, 1)
            def normalise(dst, t):
                return nc.scalar.activation(dst, tile_of(x, t), ACT.Identity, bias=n_bias[:, bass.ds(t, 1)],
                                            scale=n_scale[:, bass.ds(t, 1)])

            def layer_a(h):
                n0 = h * A_STEPS

                def copy_xnT(i, b):
                    act.wait_ge(a_xnT_psum, n0 + i + 1)
                    wait(act, a_mm, 3 * (n0 + i - 1))
                    nc.scalar.copy(xnT[:, b, :], ps[:, 0, :]).then_inc(a_xnT, 1)

                def norm(i, b):
                    wait(act, a_xnT_psum, n0 + i - 1)
                    for t in range(QUAD):
                        last = normalise(xn[:, b, t, :], h * HT + i * QUAD + t)
                    last.then_inc(a_xn, 1)

                def step(i, b):
                    if not isinstance(i, int) or i + 1 < A_STEPS:
                        copy_xnT(i + 1, 1 - b)
                    act.wait_ge(a_mm, (n0 + i) * 3 + 1)
                    wait(act, a_scan, n0 + i - 1)
                    nc.scalar.activation(gate[:, b, :], ps[:, 6 + b, :], ACT.Sigmoid).then_inc(a_gate, 1)
                    if not isinstance(i, int) or i + 2 < A_STEPS:
                        norm(i + 2, b)
                act.wait_ge(scaled_a, h + 1)
                norm(0, 0)
                norm(1, 1)
                if h and stages >= 2:
                    act.wait_ge(g_mm, h * G_STEPS)
                copy_xnT(0, 0)
                run_steps(act, A_STEPS, 2, step)

            def gates(call):
                n0 = call * G_STEPS
                if call < HALVES:
                    act.wait_ge(a_mm, 3 * A_STEPS * (call + 1))
                for i in range(G_STEPS + 1):
                    b = i % 2
                    if i < G_STEPS:
                        act.wait_ge(g_tT_psum, n0 + i + 1)
                        wait(act, g_mm, n0 + i - 1)
                        nc.scalar.copy(xnT[:, b, :], ps[:, b, :]).then_inc(g_tT, 1)
                    if i:
                        j = i - 1
                        act.wait_ge(g_mm, n0 + j + 1)
                        nc.scalar.copy(logits[:, j * QUAD:(j + 1) * QUAD, :].rearrange("p t e -> p (t e)"),
                                       ps[:, 2 + j % 2, 0:QUAD * E]).then_inc(g_logits, 1)
                act.wait_ge(r_diff, call + 1)
                nc.scalar.activation(ex[:, :], m2[:, :], ACT.Exp).then_inc(r_exp, 1)

            def experts(call, h):
                n0 = call * E_STEPS

                def feed(m, b):
                    act.wait_ge(e_tT_psum, n0 + m + 1)
                    wait(act, e_h_psum, n0 + m - 1)
                    nc.scalar.copy(tT[:, b, :], ps[:, b, 0:SLOTS]).then_inc(e_tT, 1)
                    e = act.value_load(step_exp[0:1, h, bass.ds(m, 1)], min_val=0, max_val=E - 1)
                    wait(act, e_h, n0 + m - 1)
                    nc.scalar.copy(w1s[:, b, :], tile_of(w1T, e)).then_inc(e_w1, 1)

                def residual(m):
                    t = h * HT + m
                    nc.scalar.activation(tile_of(x, t), tile_of(x, t), ACT.Identity, bias=res_bias[:, bass.ds(t, 1)],
                                         scale=res_scale[:, bass.ds(t, 1)]).then_inc(g_res, 1)

                def step(m, k):
                    b = k % 2
                    if not isinstance(m, int) or m + 1 < E_STEPS:
                        feed(m + 1, 1 - b)
                    act.wait_ge(e_h_psum, n0 + m + 1)
                    wait(act, e_o_psum, n0 + m - 1)
                    for c in range(HC):
                        last = nc.scalar.activation(hT[:, b, c, :], ps[:, 2 + b, c * SLOTS:(c + 1) * SLOTS], ACT.Gelu,
                                                    bias=w1s[:, b, HID + c:HID + c + 1])
                    last.then_inc(e_h, 1)
                def step_and_residual(m, k):
                    step(m, k)
                    residual(m)
                feed(0, 0)
                straight(0, E_UNROLL, E_UNROLL, step_and_residual)
                looped(act, E_UNROLL, HT, E_UNROLL, step_and_residual)
                straight(HT, E_STEPS, E_UNROLL, step)

            def layer_b(h):
                n0 = h * B_STEPS

                def norm(m, b):
                    wait(act, b_xnT_psum, n0 + m - 1)
                    for t in range(2):
                        last = normalise(b_xn[:, b, t, :], h * HT + 2 * m + t)
                    last.then_inc(b_norm, 1)

                def front(m, b):
                    act.wait_ge(b_xnT_psum, n0 + m + 1)
                    wait(act, b_qkv, n0 + m)
                    nc.scalar.copy(b_xnT[:, :], ps[:, 0, 0:S]).then_inc(b_xnT_ok, 1)
                    act.wait_ge(b_qkv, n0 + m + 1)
                    wait(act, b_feat, n0 + m)
                    nc.scalar.activation(b_exp[:, :], ps[:, 1, :], ACT.Exp).then_inc(b_expd, 1)
                    wait(act, b_o_psum, 2 * (n0 + m) - 2)
                    for t in range(2):
                        last = nc.scalar.copy(plain_v(b, t), ps[:, 2, t * P:(t + 1) * P].rearrange(
                            "p (g k e) -> p g k e", g=4, k=4))
                    last.then_inc(b_v, 1)

                def split_keys(m, b):
                    act.wait_ge(b_feat, n0 + m + 1)
                    wait(act, b_sc, 8 * (n0 + m - 1))
                    for g in range(4):
                        last = nc.scalar.activation(kx[:, b, g, :], qk[:, b, 1, :], ACT.Copy, scale=group_mask[:, g:g + 1])
                    last.then_inc(b_kx, 1)

                def split_queries(m, b):
                    wait(act, b_sc, 8 * (n0 + m - 1))
                    for k in range(4):
                        last = nc.scalar.activation(qx[:, b, k, :], qk[:, b, 0, :], ACT.Copy, scale=head_pick[:, k:k + 1])
                    last.then_inc(b_qx, 1)

                def turned_keys(m):
                    act.wait_ge(b_kt_psum, n0 + m + 1)
                    wait(act, b_st_psum, n0 + m)
                    nc.scalar.copy(k_tok[:, :], ps[:, 0, S:S + P]).then_inc(b_kt, 1)

                def spread_reciprocals(m):
                    act.wait_ge(b_rec, n0 + m + 1)
                    wait(act, b_rT, n0 + m)
                    nc.scalar.copy(recx[:, :, :], rec[:, :].rearrange("p (h a) -> p h a", a=1).to_broadcast(
                        [P, 2 * HEADS, HD])).then_inc(b_recx, 1)

                def turned_reciprocals(m, b):
                    act.wait_ge(b_rT, n0 + m + 1)
                    wait(act, b_o, n0 + m - 1)
                    nc.scalar.copy(recT[:, b, :], ps[:, 0, 0:S]).then_inc(b_recT, 1)

                def step(n, b):
                    more = not isinstance(n, int) or n + 1 < B_STEPS
                    turned_reciprocals(n, b)
                    if more:
                        front(n + 1, 1 - b)
                        split_keys(n + 1, 1 - b)
                        turned_keys(n + 1)
                        split_queries(n + 1, 1 - b)
                        spread_reciprocals(n + 1)
                    if not isinstance(n, int) or n + 2 < B_STEPS:
                        norm(n + 2, b)
                if h == 0:
                    act.wait_ge(vx_zero, 1)
                act.wait_ge(scaled_b, 1 if h == 0 else 3)
                norm(0, 0)
                norm(1, 1)
                front(0, 0)
                split_keys(0, 0)
                turned_keys(0)
                split_queries(0, 0)
                spread_reciprocals(0)
                early = PT // 2 - 2
                straight(0, 2, 2, step)
                looped(act, 2, early, 2, step)
                if h == 0:
                    act.wait_ge(scaled_b, 2)
                looped(act, early, B_STEPS - 2, 2, step)
                straight(B_STEPS - 2, B_STEPS, 2, step)

            for rnd in range(2):
                for h in range(HALVES):
                    if rnd == 0:
                        layer_a(h)
                    elif stages >= 3:
                        layer_b(h)
                    if rnd * 2 + 2 <= stages:
                        gates(rnd * HALVES + h)
                for h in range(HALVES):
                    if rnd * 2 + 2 <= stages:
                        act.wait_ge(r_slots, rnd * HALVES + h + 1)
                        experts(rnd * HALVES + h, h)

        @block.vector
        def _(dve):
            links = [0]

            def link(ins):
                links[0] += 1
                ins.then_inc(chain, 1)
                dve.wait_ge(chain, links[0])

            def inv_roots(cols):
                v, r, w = (sv[:, k, 0:cols] for k in (0, 1, 2))
                link(nc.vector.tensor_scalar(r.bitcast(I32), v.bitcast(I32), -0.5, float(0x5f3759df), ALU.mult, ALU.add))
                for _ in range(3):
                    link(nc.vector.tensor_tensor(w, r, r, ALU.mult))
                    link(nc.vector.scalar_tensor_tensor(out=w, in0=w, scalar=-0.5, in1=v, op0=ALU.mult, op1=ALU.mult))
                    link(nc.vector.scalar_tensor_tensor(out=r, in0=w, scalar=1.5, in1=r, op0=ALU.add, op1=ALU.mult))

            def moments(t0, n):
                sl = slice(t0, t0 + n)
                me, qe, mo, qo = (stats[:, sl, k] for k in (1, 2, 4, 5))
                d, q, m = (sv[:, k, 0:n] for k in (0, 1, 2))
                nc.vector.tensor_tensor(d, me, mo, ALU.subtract)
                nc.vector.tensor_tensor(q, qe, qo, ALU.add)
                link(nc.vector.tensor_tensor(m, me, mo, ALU.add))
                nc.vector.tensor_scalar(mean[:, sl], m, 0.5, None, ALU.mult)
                link(nc.vector.scalar_tensor_tensor(out=d, in0=d, scalar=0.25, in1=d, op0=ALU.mult, op1=ALU.mult))
                link(nc.vector.scalar_tensor_tensor(out=var[:, sl], in0=q, scalar=1.0 / D, in1=d, op0=ALU.mult,
                                                    op1=ALU.add))

            def set_bias(t0, n, dst, scale):
                return nc.vector.scalar_tensor_tensor(out=dst[:, t0:t0 + n], in0=mean[:, t0:t0 + n], scalar=-1.0,
                                                      in1=scale, op0=ALU.mult, op1=ALU.mult)

            def scale_a(t0, n, nth):
                sl = slice(t0, t0 + n)
                moments(t0, n)
                link(nc.vector.tensor_scalar(sv[:, 0, 0:n], var[:, sl], LN_EPS, A_EPS * A_EPS / D, ALU.add, ALU.mult))
                link(nc.vector.tensor_tensor(sv[:, 0, 0:n], sv[:, 0, 0:n], var[:, sl], ALU.max))
                inv_roots(n)
                nc.vector.tensor_copy(n_scale[:, sl], sv[:, 1, 0:n])
                set_bias(t0, n, n_bias, sv[:, 1, 0:n]).then_inc(scaled_a, 1)
                dve.wait_ge(scaled_a, nth)

            def scale_b(t0, n, nth):
                sl = slice(t0, t0 + n)
                moments(t0, n)
                link(nc.vector.tensor_scalar(sv[:, 0, 0:n], var[:, sl], LN_EPS, None, ALU.add))
                inv_roots(n)
                nc.vector.tensor_copy(n_scale[:, sl], sv[:, 1, 0:n])
                set_bias(t0, n, n_bias, sv[:, 1, 0:n]).then_inc(scaled_b, 1)
                dve.wait_ge(scaled_b, nth)

            def scale_f(t0, n, nth):
                sl = slice(t0, t0 + n)
                moments(t0, n)
                link(nc.vector.tensor_scalar(sv[:, 0, 0:n], var[:, sl], LN_EPS, None, ALU.add))
                link(nc.vector.scalar_tensor_tensor(out=sv[:, 0, n:2 * n], in0=sv[:, 0, 0:n], scalar=RMS_EPS,
                                                    in1=var[:, sl], op0=ALU.mult, op1=ALU.add))
                inv_roots(2 * n)
                nc.vector.tensor_scalar(res_scale[:, sl], sv[:, 1, 0:n], 1.0, None, ALU.add)
                set_bias(t0, n, res_bias, sv[:, 1, 0:n])
                nc.vector.tensor_copy(n_scale[:, sl], sv[:, 1, n:2 * n]).then_inc(scaled_f, 1)
                dve.wait_ge(scaled_f, nth)

            def normalise(dst, t):
                return nc.vector.tensor_scalar(dst, tile_of(x, t), mean[:, bass.ds(t, 1)], n_scale[:, bass.ds(t, 1)],
                                               ALU.subtract, ALU.mult)

            def tile_stats(t):
                return nc.vector.bn_stats(tile_of(stats, t), tile_of(x, t))

            def layer_a(h):
                n0 = h * A_STEPS
                t0 = h * HT

                def scan(i, b):
                    dve.wait_ge(a_gate, n0 + i + 1)
                    dve.wait_ge(a_mm, (n0 + i) * 3 + 3)
                    wait(dve, a_back, n0 + i - 1)
                    for k in range(QUAD * P // S):
                        last = nc.vector.tensor_tensor_scan(yq[:, b, k * S:(k + 1) * S], gate[:, b, k * S:(k + 1) * S],
                                                            ps[:, 4 + b, k * S:(k + 1) * S], 0.0, ALU.mult, ALU.add)
                    last.then_inc(a_scan, 1)
                    dve.wait_ge(a_scan, n0 + i + 1)
                    nc.vector.tensor_tensor(yq[:, b, :], yq[:, b, :], ps[:, 2 + b, :], ALU.mult).then_inc(a_yq, 1)

                def add(i):
                    dve.wait_ge(a_back, n0 + i + 1)
                    xs = x[:, bass.ds(t0 + i * QUAD, QUAD), :]
                    nc.vector.tensor_tensor(xs, xs, ps[:, 1, :].rearrange("p (t d) -> p t d", d=D), ALU.add
                                            ).then_inc(a_added, 1)
                    dve.wait_ge(a_added, n0 + i + 1)
                    for t in range(QUAD):
                        tile_stats(t0 + i * QUAD + t)

                def step(i, b):
                    scan(i, b)
                    if h == 0:
                        for t in range(QUAD):
                            tile_stats(HT + i * QUAD + t)
                    if not is_at(i, 0):
                        add(i - 1)
                if h == 0:
                    dve.wait_ge(x_loaded[1], 16)
                run_steps(dve, A_STEPS, 2, step)
                add(A_STEPS - 1)
                link(nc.vector.tensor_copy(sv[:, 4, 0:1], sv[:, 5, 0:1]))

            def gates(call, h):
                n0 = call * G_STEPS
                if call == 0:
                    dve.wait_ge(wT_psum, 2)
                dve.wait_ge(scaled_f, call + 1)
                wait(dve, scattered[h], 16 * 2 * HT * (call // HALVES))
                with dve.Fori(0, G_STEPS) as i:
                    for t in range(QUAD):
                        last = normalise(tile_of(t_rows[:, h, :, :], i * QUAD + t), h * HT + i * QUAD + t)
                    last.then_inc(g_t, 1)
                route(call, h)

            def route(call, h):
                V = nc.vector
                tiles = [P, HT, E]

                def per_tile(v):
                    return v.rearrange("p (t a) -> p t a", a=1).to_broadcast(tiles)
                descb = desc[:, :].rearrange("p (a e) -> p a e", a=1).to_broadcast(tiles)
                dve.wait_ge(g_logits, (call + 1) * G_STEPS)
                if call == 0:
                    dve.wait_ge(consts, ALL_CONSTS)
                wait(dve, r_rank, call)
                for src, m, pick in ((logits, m1, pick1), (r_b, m2, pick2)):
                    if m is m2:
                        link(V.scalar_tensor_tensor(out=r_b[:, :, :], in0=pick1[:, :, :], scalar=-BIG,
                                                    in1=logits[:, :, :], op0=ALU.mult, op1=ALU.add))
                    link(V.tensor_reduce(m[:, :], src[:, :, :], X, ALU.max))
                    link(V.tensor_tensor(r_a[:, :, :], src[:, :, :], per_tile(m[:, :]), ALU.is_equal))
                    link(V.tensor_tensor(r_a[:, :, :], r_a[:, :, :], descb, ALU.mult))
                    link(V.tensor_reduce(mi[:, :], r_a[:, :, :], X, ALU.max))
                    link(V.tensor_tensor(pick[:, :, :], per_tile(mi[:, :]), descb, ALU.is_equal))
                V.tensor_tensor(picked[:, :, :], pick1[:, :, :], pick2[:, :, :], ALU.add).then_inc(r_picked, 1)
                dve.wait_ge(r_rank, call + 1)
                te = "p (t e) -> p t e"
                V.tensor_copy(tile_tot[:, :, :], ps[:, 7, 0:HT * E].rearrange("p (t e) -> p e t", e=E))
                V.tensor_copy(r_a[:, :, :], ps[:, 6, 0:HT * E].rearrange(te, e=E)).then_inc(r_read, 1)
                dve.wait_ge(r_read, call + 1)
                wait(dve, combined, call - 1)
                V.tensor_tensor(m2[:, :], m2[:, :], m1[:, :], ALU.subtract).then_inc(r_diff, 1)
                dve.wait_ge(r_exp, call + 1)
                link(V.tensor_scalar(m1[:, :], ex[:, :], 1.0, None, ALU.add))
                link(V.reciprocal(prob[:, 0, h, :], m1[:, :]))
                link(V.tensor_tensor(prob[:, 1, h, :], prob[:, 0, h, :], ex[:, :], ALU.mult))
                flat = "p e t -> p (e t)"
                link(V.tensor_tensor_scan(tile_inc[:, :, :].rearrange(flat), not_first[:, :, :].rearrange(flat),
                                          tile_tot[:, :, :].rearrange(flat), 0.0, ALU.mult, ALU.add))
                link(V.tensor_scalar(cnt_i[:, :], tile_inc[:, :, HT - 1], float(SLOTS - 1), None, ALU.add))
                link(V.tensor_scalar(cnt_i[:, :], cnt_i[:, :], -SLOTS, None, ALU.bitwise_and))
                link(V.tensor_copy(cnt_f[:, :], cnt_i[:, :]))
                link(V.tensor_tensor_scan(ends[:, :], ones8[:, :], cnt_f[:, :], 0.0, ALU.mult, ALU.add))
                link(V.tensor_tensor(base[:, :], ends[:, :], cnt_f[:, :], ALU.subtract))
                link(V.tensor_tensor(tile_inc[:, :, :], tile_inc[:, :, :], tile_tot[:, :, :], ALU.subtract))
                link(V.tensor_tensor(tile_inc[:, :, :], tile_inc[:, :, :],
                                     base[:, :].rearrange("p (e a) -> p e a", a=1).to_broadcast([P, E, HT]), ALU.add))
                link(V.tensor_tensor(r_a[:, :, :], r_a[:, :, :], tile_inc[:, :, :].rearrange("p e t -> p t e"), ALU.add))
                for k, pick in enumerate((pick1, pick2)):
                    link(V.tensor_tensor(r_b[:, :, :], r_a[:, :, :], pick[:, :, :], ALU.mult))
                    link(V.tensor_reduce(mi[:, :], r_b[:, :, :], X, ALU.add))
                    link(V.tensor_copy(slot[:, k, h, :], mi[:, :]))
                link(V.tensor_tensor(step_cmp[:, :, :],
                                     step_slot[:, :].rearrange("p (m a) -> p m a", a=1).to_broadcast([P, E_STEPS, E]),
                                     ends[:, :].rearrange("p (a e) -> p a e", a=1).to_broadcast([P, E_STEPS, E]),
                                     ALU.is_ge))
                link(V.tensor_reduce(step_e[:, :], step_cmp[:, :, :], X, ALU.add))
                V.tensor_scalar(step_exp[:, h, :], step_e[:, :], float(E - 1), None, ALU.min).then_inc(r_slots, 1)

            def experts(call, h):
                n0 = call * E_STEPS

                def step(m, k):
                    dve.wait_ge(e_o_psum, n0 + m + 1)
                    wait(dve, e_stored[k], rounds(call, m, k))
                    e = dve.value_load(step_exp[0:1, h, bass.ds(m, 1)], min_val=0, max_val=E - 1)
                    nc.vector.tensor_tensor(o_sb[:, k, :, :], ps[:, 4 + k % 2, 0:SLOTS].rearrange("p (s d) -> p s d", d=D),
                                            b2_all[:, bass.ds(e, 1), :].to_broadcast([P, SUB, D]), ALU.add
                                            ).then_inc(e_o, 1)
                if h == 0:
                    run_steps(dve, E_STEPS, E_UNROLL, step)
                else:
                    def step_and_combine(m, k):
                        step(m, k)
                        if k % 2:
                            combine(call - 1, (m - first) // 2)
                    first = E_STEPS - 2 * E_UNROLL
                    straight(0, E_UNROLL, E_UNROLL, step)
                    looped(dve, E_UNROLL, first, E_UNROLL, step)
                    straight(first, first + E_UNROLL, E_UNROLL, step_and_combine)
                    if call < HALVES:
                        link(nc.vector.tensor_copy(sv[:, 4, 0:1], sv[:, 5, 0:1]))
                        scale_b(0, PT, 1)
                    straight(first + E_UNROLL, E_STEPS, E_UNROLL, step)

            def wait_gathered(call, q):
                dve.wait_ge(gathered[call % HALVES][q], 16 * 2 * PT * (call // HALVES + 1))

            def combine(call, c):
                h = call % HALVES
                n = call * CHUNKS + c
                if is_at(c, 0):
                    wait_gathered(call, 0)
                    dve.wait_ge(g_res, (call + 1) * HT)
                if is_at(c, PART_CHUNKS):
                    wait_gathered(call, 1)
                for k, done in enumerate((first_added, combined)):
                    for j in range(QUAD):
                        t = c * QUAD + j
                        xt = tile_of(x, h * HT + t)
                        last = nc.vector.scalar_tensor_tensor(out=xt, in0=tile_of(got[:, k, :, :], t),
                                                              scalar=prob[:, k, h, bass.ds(t, 1)], in1=xt,
                                                              op0=ALU.mult, op1=ALU.add)
                    last.then_inc(done, 1)
                    dve.wait_ge(done, n + 1)
                if call < HALVES:
                    for j in range(QUAD):
                        tile_stats(h * HT + c * QUAD + j)

            def layer_b(h):
                scores = scores_of(h)
                n0 = h * B_STEPS
                t0 = h * HT

                def features(m, b):
                    dve.wait_ge(b_expd, n0 + m + 1)
                    wait(dve, b_o_psum, 2 * (n0 + m) - 2)
                    nc.vector.tensor_scalar(b_exp[:, :], b_exp[:, :], 1.0, None, ALU.min).then_inc(b_clip, 1)
                    dve.wait_ge(b_clip, n0 + m + 1)
                    nc.vector.scalar_tensor_tensor(out=qk[:, b, :, :].rearrange("p a s -> p (a s)"), in0=ps[:, 1, :],
                                                   scalar=0.0, in1=b_exp[:, :], op0=ALU.max, op1=ALU.add
                                                   ).then_inc(b_feat, 1)
                    dve.wait_ge(b_feat, n0 + m + 1)
                    wait(dve, b_den, n0 + m)
                    nc.vector.tensor_tensor_scan(zc[:, :], one_row[:, :], qk[:, b, 1, :], 0.0, ALU.mult, ALU.add
                                                 ).then_inc(b_keys, 1)
                    dve.wait_ge(b_keys, n0 + m + 1)
                    nc.vector.tensor_tensor(qz[:, :], zc[:, :], qk[:, b, 0, :], ALU.mult).then_inc(b_qz, 1)

                def mask(n, b, blk, g):
                    dve.wait_ge(b_sc, 8 * (n0 + n) + 4 * blk + g + 1)
                    wait(dve, b_o_psum, 2 * (n0 + n) + blk - 1)
                    nc.vector.tensor_tensor(scores[:, blk, g, :, :], ps[:, 3 + g, :].rearrange("p (k i) -> p k i", k=4),
                                            causal[:, :].rearrange("p (a i) -> p a i", a=1).to_broadcast([P, 4, P]),
                                            ALU.mult).then_inc(b_masked, 1)

                def middle(m, b):
                    dve.wait_ge(b_den, n0 + m + 1)
                    wait(dve, b_recx, n0 + m)
                    nc.vector.tensor_scalar(den[:, :], ps[:, 2, S:S + 2 * HEADS], B_EPS, None, ALU.add).then_inc(b_eps, 1)
                    dve.wait_ge(b_eps, n0 + m + 1)
                    nc.vector.reciprocal(rec[:, :], den[:, :]).then_inc(b_rec, 1)
                    dve.wait_ge(b_st_psum, n0 + m + 1)
                    wait(dve, b_o_psum, 2 * (n0 + m) - 2)
                    nc.vector.tensor_tensor(state[:, b, 0:P], ps[:, 2, S + 2 * HEADS:S + 2 * HEADS + P], head_diag[:, :],
                                            ALU.mult).then_inc(b_st, 1)

                def divide(n, b):
                    dve.wait_ge(b_o_psum, 2 * (n0 + n) + 2)
                    dve.wait_ge(b_recT, n0 + n + 1)
                    wait(dve, b_y, n0 + n - 1)
                    nc.vector.tensor_tensor(oT[:, b, 0:S], ps[:, 7, 0:S], recT[:, b, :], ALU.mult).then_inc(b_o, 1)

                def add(n):
                    dve.wait_ge(b_y, n0 + n + 1)
                    xs = x[:, bass.ds(t0 + n * 2, 2), :]
                    nc.vector.tensor_tensor(xs, xs, ps[:, 7, S:2 * S].rearrange("p (t d) -> p t d", d=D), ALU.add
                                            ).then_inc(b_added, 1)
                    dve.wait_ge(b_added, n0 + n + 1)
                    for t in range(2):
                        tile_stats(t0 + n * 2 + t)

                def step(n, b):
                    more = not isinstance(n, int) or n + 1 < B_STEPS
                    mask(n, b, 0, 0)
                    mask(n, b, 0, 1)
                    mask(n, b, 0, 2)
                    mask(n, b, 0, 3)
                    if more:
                        features(n + 1, 1 - b)
                    if not is_at(n, 0):
                        add(n - 1)
                    for g in range(4):
                        mask(n, b, 1, g)
                    if more:
                        middle(n + 1, 1 - b)
                    divide(n, b)
                features(0, 0)
                middle(0, 0)
                if h == 0:
                    def step_and_second_part(n, b):
                        step(n, b)
                        combine(0, n + PART_CHUNKS)

                    def step_and_second_half(n, b):
                        step(n, b)
                        combine(1, n - (B_STEPS - CHUNKS))
                    straight(0, PART_CHUNKS, 2, step_and_second_part)
                    link(nc.vector.tensor_copy(sv[:, 4, 0:1], sv[:, 5, 0:1]))
                    scale_b(PT, PT, 2)
                    looped(dve, PART_CHUNKS, B_STEPS - CHUNKS, 2, step)
                    wait_gathered(1, 0)
                    wait_gathered(1, 1)
                    dve.wait_ge(g_res, 2 * HT)
                    looped(dve, B_STEPS - CHUNKS, B_STEPS - 2, 2, step_and_second_half)
                    straight(B_STEPS - 2, B_STEPS, 2, step_and_second_half)
                else:
                    run_steps(dve, B_STEPS, 2, step)
                add(B_STEPS - 1)
                link(nc.vector.tensor_copy(sv[:, 4, 0:1], sv[:, 5, 0:1]))

            dve.wait_ge(consts, ALL_CONSTS)
            nc.vector.memset(vx[:, :, :, :], 0.0).then_inc(vx_zero, 1)
            dve.wait_ge(x_loaded[0], 16)
            with dve.Fori(0, CHUNKS) as i:
                for j in range(QUAD):
                    tile_stats(i * QUAD + j)
            link(nc.vector.tensor_copy(sv[:, 4, 0:1], sv[:, 5, 0:1]))
            scale_a(0, HT, 1)
            for rnd in range(2):
                for h in range(HALVES):
                    if rnd == 0:
                        layer_a(h)
                        if h == 0:
                            scale_a(HT, HT, 2)
                    else:
                        layer_b(h)
                        if h == 0:
                            scale_b(HT, HT, 3)
                    scale_f(h * HT, HT, rnd * HALVES + h + 1)
                    gates(rnd * HALVES + h, h)
                for h in range(HALVES):
                    experts(rnd * HALVES + h, h)
            for call, c0 in ((HALVES, PART_CHUNKS), (HALVES + 1, 0)):
                for c in range(c0, CHUNKS):
                    combine(call, c)


_INS = ['L0_attn_a_x', 'L0_attn_a_W_qkva', 'L0_attn_a_gamma', 'L0_attn_b_wq', 'L0_attn_b_wk', 'L0_attn_b_wv',
        'L0_attn_b_wo', 'L0_ffn_norm_weight', 'L0_ffn_gate_w', 'L0_ffn_w1', 'L0_ffn_b1', 'L0_ffn_w2', 'L0_ffn_b2']
STAGES = 4


def kernel(**inputs):
    import numpy as _np
    import concourse.bacc as _bacc
    from concourse import mybir as _mybir
    from concourse.bass_utils import run_bass_kernel_spmd as _run

    nc = _bacc.Bacc("TRN2", target_bir_lowering=False, num_devices=1)
    arrays, args = {}, []
    for name in _INS:
        a = _np.ascontiguousarray(inputs[name])
        arrays[f"in_{name}"] = a
        args.append(nc.dram_tensor(f"in_{name}", a.shape, _mybir.dt.from_np(a.dtype), kind="ExternalInput").ap())
    out = nc.dram_tensor("out_x", inputs['L0_attn_a_x'].shape, _mybir.dt.float32, kind="ExternalOutput").ap()
    build_hybrid(nc, *args, out, stages=STAGES)
    r = _run(nc, [arrays], core_ids=[0])
    return r.results[0]["out_x"]
```

```python
from contextlib import ExitStack

import concourse.bass as bass
from concourse import mybir

F32 = mybir.dt.float32
BF16 = mybir.dt.bfloat16
I32 = mybir.dt.int32
U32 = mybir.dt.uint32
ALU = mybir.AluOpType
ACT = mybir.ActivationFunctionType
X = mybir.AxisListType.X
P = 128

HEADS, HD = 16, 8
LN_EPS = 1e-5
A_EPS = 1e-12
RMS_EPS = 1e-6
B_EPS = 1e-6
PARTS = 2
C = 64
HALVES = 2
QUAD = 4
SLOTS = 256
BIG = 3.0e38


def straight(lo, hi, unroll, body):
    for m in range(lo, hi):
        body(m, m % unroll)


def looped(eng, lo, hi, unroll, body):
    with eng.Fori(lo // unroll, hi // unroll) as n:
        for j in range(unroll):
            body(n * unroll + j, j)


def run_steps(eng, steps, unroll, body):
    straight(0, unroll, unroll, body)
    looped(eng, unroll, steps - unroll, unroll, body)
    straight(steps - unroll, steps, unroll, body)


def is_at(step, n):
    return isinstance(step, int) and step == n


def wait(eng, sem, value):
    if not isinstance(value, int) or value > 0:
        eng.wait_ge(sem, value)


def build_hybrid(nc, x_in, w_qkva, gamma, b_wq, b_wk, b_wv, b_wo, norm_w, gate_w, w1, b1, w2, b2, x_out):
    B, S, D = x_in.shape
    E, HID, _ = w1.shape
    HC = HID // P
    TILES = B * S // P
    HT = TILES // HALVES
    PT = HT // PARTS
    CHUNKS = HT // QUAD
    PART_CHUNKS = PT // QUAD
    BACK_CHUNKS = 2
    A_STEPS = HT // QUAD
    B_STEPS = HT * P // S
    G_STEPS = HT // QUAD
    E_UNROLL = 8
    AHEAD = 6
    E_STEPS = -(-((2 * HT * P + E * (SLOTS - 1)) // SLOTS) // E_UNROLL) * E_UNROLL
    ROWS = E_STEPS * SLOTS
    SUB = SLOTS // P
    W1C = HID + HC
    assert D == P and S == 2 * P and HEADS * HD == D and SLOTS == 2 * P

    x_tiles = x_in.rearrange("b (t p) d -> p (b t) d", p=P)
    out_tiles = x_out.rearrange("b (t p) d -> p (b t) d", p=P)
    tok_rows = [nc.dram_tensor(f"tok_rows{h}", [ROWS, D], F32).ap() for h in range(HALVES)]
    exp_rows = [nc.dram_tensor(f"exp_rows{h}", [ROWS, D], F32).ap() for h in range(HALVES)]

    with ExitStack() as ctx:
        def sb(name, shape, dt=F32):
            return ctx.enter_context(nc.sbuf_tensor(name, shape, dt))

        def sem(name):
            return ctx.enter_context(nc.semaphore(name))

        ps = ctx.enter_context(nc.psum_tensor("ps", [P, 8, 512], F32))
        x = sb("x", [P, TILES, D])
        ident = sb("ident", [P, P])
        before = sb("before", [P, P], BF16)
        ones = sb("ones", [P, P], BF16)
        causal = sb("causal", [P, P])
        head_diag = sb("head_diag", [P, P])
        head_sum = sb("head_sum", [P, HEADS])
        head_pick = sb("head_pick", [P, 4])
        desc = sb("desc", [P, E])
        step_slot = sb("step_slot", [P, E_STEPS])
        not_first = sb("not_first", [P, E, HT])
        ones8 = sb("ones8", [P, E])
        one_row = sb("one_row", [P, S])
        wa = sb("wa", [P, 3, P])
        wb = sb("wb", [P, 4, P])
        gT = sb("gT", [P, P // QUAD])
        w1T = sb("w1T", [P, E, W1C])
        w2T = sb("w2T", [P, E * HC, P])
        b2_all = sb("b2_all", [P, E, D])
        gam = sb("gam", [P, 1])
        nw = sb("nw", [P, 1])
        stats = sb("stats", [P, TILES, 6])
        mean = sb("mean", [P, TILES])
        var = sb("var", [P, TILES])
        n_scale = sb("n_scale", [P, TILES])
        n_bias = sb("n_bias", [P, TILES])
        res_scale = sb("res_scale", [P, TILES])
        res_bias = sb("res_bias", [P, TILES])
        sv = sb("sv", [P, 3, 3 * HT])
        settled = sb("settled", [P, 2])
        xn = sb("xn", [P, 2, QUAD, D])
        xnT = sb("xnT", [P, 2, QUAD * P])
        gate = sb("gate", [P, 2, QUAD * P])
        yq = sb("yq", [P, 2, QUAD * P])
        t_rows = sb("t_rows", [P, HALVES, HT, D])
        got = sb("got", [P, 2, HT, D])
        r_a = sb("r_a", [P, HT, E])
        r_b = sb("r_b", [P, HT, E])
        pick1 = sb("pick1", [P, HT, E])
        pick2 = sb("pick2", [P, HT, E])
        picked = sb("picked", [P, HT, E], BF16)
        tile_tot = sb("tile_tot", [P, E, HT])
        tile_inc = sb("tile_inc", [P, E, HT])
        m1 = sb("m1", [P, HT])
        m2 = sb("m2", [P, HT])
        mi = sb("mi", [P, HT])
        ex = sb("ex", [P, HT])
        prob = sb("prob", [P, 2, HALVES, HT])
        cnt_i = sb("cnt_i", [P, E], I32)
        cnt_f = sb("cnt_f", [P, E])
        ends = sb("ends", [P, E])
        base = sb("base", [P, E])
        slot = sb("slot", [P, 2, HALVES, HT], U32)
        step_cmp = sb("step_cmp", [P, E_STEPS, E])
        step_e = sb("step_e", [P, E_STEPS])
        step_exp = sb("step_exp", [P, HALVES, E_STEPS], I32)
        ts = sb("ts", [P, E_UNROLL, SUB, D])
        tT = sb("tT", [P, 2, SLOTS])
        w1s = sb("w1s", [P, 2, W1C])
        hT = sb("hT", [P, 2, HC, SLOTS])
        o_sb = sb("o_sb", [P, E_UNROLL, SUB, D])

        VW = HEADS // 4 * (P + HD)
        b_xn = xn
        b_xnT = sb("b_xnT", [P, S])
        b_exp = sb("b_exp", [P, 2 * S])
        qk = sb("qk", [P, 2, 2, S])
        zc = sb("zc", [P, S])
        qz = sb("qz", [P, S])
        den = sb("den", [P, 2 * HEADS])
        rec = sb("rec", [P, 2 * HEADS])
        recx = sb("recx", [P, 2 * HEADS, HD])
        qx = sb("qx", [P, 2, 4, S])
        group_mask = sb("group_mask", [P, 4])
        vx = sb("vx", [P, 2, 2, VW])
        k_tok = sb("k_tok", [P, 2, P])
        kx = ts[:, :, :, :].rearrange("p (b g) s d -> p b g (s d)", b=2)
        state = gate
        oT = yq
        recT = yq[:, :, S:2 * S]

        x_loaded = [sem(f"x_loaded{n}") for n in range(HALVES * PARTS)]
        first_w_loaded = sem("first_w_loaded")
        expert_w_loaded = sem("expert_w_loaded")
        w_loaded = sem("w_loaded")
        consts = sem("consts")
        wT_psum = sem("wT_psum")
        wT_done = sem("wT_done")
        ewT_psum = sem("ewT_psum")
        ewT_done = sem("ewT_done")
        zero_tile = sem("zero_tile")
        zeroed = [sem(f"zeroed{h}") for h in range(HALVES)]
        chain = sem("chain")
        pchain = sem("pchain")
        scaled_a, scaled_f, scaled_b = (sem(f"scaled_{n}") for n in "afb")
        a_centred_pool = sem("a_centred_pool")
        a_normed_pool = sem("a_normed_pool")
        a_normed_dve = sem("a_normed_dve")
        a_centred_act = sem("a_centred_act")
        a_normed_act = sem("a_normed_act")
        a_turned = sem("a_turned")
        a_turned_copied = sem("a_turned_copied")
        a_projected = sem("a_projected")
        a_gated = sem("a_gated")
        a_scanned = sem("a_scanned")
        a_multiplied = sem("a_multiplied")
        a_turned_back = sem("a_turned_back")
        a_added = sem("a_added")
        g_rows_dve = sem("g_rows_dve")
        g_centred = sem("g_centred")
        g_rows_act = sem("g_rows_act")
        g_turned = sem("g_turned")
        g_turned_copied = sem("g_turned_copied")
        g_projected = sem("g_projected")
        g_projected_copied = sem("g_projected_copied")
        g_logits_psum = sem("g_logits_psum")
        g_logits_copied = sem("g_logits_copied")
        r_picked = sem("r_picked")
        r_counted = sem("r_counted")
        r_counts_copied = sem("r_counts_copied")
        r_diffed = sem("r_diffed")
        r_exponential = sem("r_exponential")
        r_slotted = sem("r_slotted")
        r_routed = sem("r_routed")
        scattered = [sem(f"scattered{h}") for h in range(HALVES)]
        e_loaded = [sem(f"e_loaded{k}") for k in range(E_UNROLL)]
        e_turned = sem("e_turned")
        e_turned_copied = sem("e_turned_copied")
        e_w1_copied = sem("e_w1_copied")
        e_up_done = sem("e_up_done")
        e_gelu_done = sem("e_gelu_done")
        e_down_done = sem("e_down_done")
        e_biased = sem("e_biased")
        e_stored = [sem(f"e_stored{k}") for k in range(E_UNROLL)]
        residual_added = sem("residual_added")
        gathered = [[sem(f"gathered{h}_{g}") for g in range(CHUNKS // BACK_CHUNKS)] for h in range(HALVES)]
        weighted = sem("weighted")
        first_added = sem("first_added")
        combined = sem("combined")
        b_normed = sem("b_normed")
        b_turned = sem("b_turned")
        b_turned_copied = sem("b_turned_copied")
        b_projected = sem("b_projected")
        b_negated = sem("b_negated")
        b_exponential = sem("b_exponential")
        b_features = sem("b_features")
        b_key_sums = sem("b_key_sums")
        b_query_sums = sem("b_query_sums")
        b_values_copied = sem("b_values_copied")
        b_keys_split = sem("b_keys_split")
        b_queries_split = sem("b_queries_split")
        b_den_psum = sem("b_den_psum")
        b_den_read = sem("b_den_read")
        b_reciprocal = sem("b_reciprocal")
        b_rec_spread = sem("b_rec_spread")
        b_rec_turned = sem("b_rec_turned")
        b_rec_copied = sem("b_rec_copied")
        b_keys_turned = sem("b_keys_turned")
        b_keys_copied = sem("b_keys_copied")
        b_states_psum = sem("b_states_psum")
        b_states_masked = sem("b_states_masked")
        b_banks_zeroed = sem("b_banks_zeroed")
        b_scored = sem("b_scored")
        b_masked = sem("b_masked")
        b_weighed = sem("b_weighed")
        b_divided = sem("b_divided")
        b_out_psum = sem("b_out_psum")
        b_added = sem("b_added")
        stored = sem("stored")

        def rounds(call, m, k):
            per = 16 // E_UNROLL
            return 16 * call * (E_STEPS // E_UNROLL) + (m - k) * per

        def plain_v(b, t, rows=P):
            return vx[0:rows, b, t, :].rearrange("p (k z) -> p k z", k=4)[:, :, 0:P].rearrange("p k (g c) -> p g k c", g=4)[
                :, :, :, 0:HD]

        lt = gate[:, :, 3 * P:4 * P]

        logits_psum = ps[:, 2, 0:HT * E]
        logits = tile_inc[:, :, :].rearrange("p e t -> p (e t)").rearrange("p (t e) -> p t e", e=E)
        ranks_psum, counts_psum = ps[:, 1, 0:HT * E], ps[:, 1, HT * E:2 * HT * E]

        def scores_of(h):
            return t_rows[:, h, :, :].rearrange("p (t g k) d -> p t g k d", t=2, g=4)

        def tile_of(buf, i):
            return buf[:, bass.ds(i, 1), :].rearrange("p a d -> p (a d)")

        ALL_CONSTS = 15
        ZERO_TILES = 16
        LATE = HALVES
        e_stage = got[:, 1, :, :]
        stage = got[:, 0, ZERO_TILES:, :]

        block = ctx.enter_context(nc.Block())

        @block.sync
        def _(sp):
            def load_x(n):
                tiles = slice(n * PT, (n + 1) * PT)
                sp.dma_start(x[:, tiles, :], x_tiles[:, tiles, :]).then_inc(x_loaded[n], 16)
            load_x(0)
            load_x(1)
            sp.wait_ge(first_w_loaded, 16 * 5)
            load_x(2)
            load_x(3)
            sp.wait_ge(x_loaded[3], 16)
            sp.wait_ge(expert_w_loaded, 16 * 2)
            sp.wait_ge(w_loaded, 16 * 5)
            sp.wait_ge(zero_tile, 1)
            for h in range(HALVES):
                for c in range(0, ROWS, ZERO_TILES * P):
                    sp.dma_start(tok_rows[h][c:c + ZERO_TILES * P, :].rearrange("(p t) d -> p t d", t=ZERO_TILES),
                                 got[:, 0, 0:ZERO_TILES, :]).then_inc(zeroed[h], 16)

            def experts(call):
                h = call % HALVES
                n0 = call * E_STEPS

                def load(m, k, h=h, n0=n0):
                    wait(sp, e_turned, n0 + m - (E_UNROLL - 1))
                    sp.dma_start(ts[:, k, :, :], tok_rows[h][bass.ds(m * SLOTS, SLOTS), :].rearrange(
                        "(p s) d -> p s d", s=SUB)).then_inc(e_loaded[k], 16)

                def store(m, k):
                    sp.wait_ge(e_biased, n0 + m + 1)
                    sp.dma_start(exp_rows[h][bass.ds(m * SLOTS, SLOTS), :].rearrange("(p s) d -> p s d", s=SUB),
                                 o_sb[:, k, :, :]).then_inc(e_stored[k], 16)

                def wait_scattered(h):
                    sp.wait_ge(scattered[h], 16 * 2 * HT * (call // HALVES + 1))

                def step(m, k):
                    if not isinstance(m, int) or m + AHEAD < E_STEPS:
                        load(m + AHEAD, (k + AHEAD) % E_UNROLL)
                    elif h == 0:
                        if m + AHEAD == E_STEPS:
                            wait_scattered(1)
                        load(m + AHEAD - E_STEPS, (k + AHEAD) % E_UNROLL, 1, n0 + E_STEPS)
                    store(m, k)
                if h == 0:
                    wait_scattered(0)
                    if call == HALVES:
                        sp.wait_ge(b_scored, 8 * HALVES * B_STEPS)
                    for m in range(AHEAD):
                        load(m, m)
                run_steps(sp, E_STEPS, E_UNROLL, step)

            for call in range(2 * HALVES):
                experts(call)
            for n in range(0, HALVES * CHUNKS, BACK_CHUNKS):
                sp.wait_ge(combined, HALVES * CHUNKS + n + BACK_CHUNKS)
                tiles = slice(n * QUAD, (n + BACK_CHUNKS) * QUAD)
                sp.dma_start(out_tiles[:, tiles, :], x[:, tiles, :]).then_inc(stored, 16)
            sp.wait_ge(stored, 16 * HALVES * CHUNKS // BACK_CHUNKS)

        @block.gpsimd
        def _(pool):
            links = [0]

            def link(ins):
                links[0] += 1
                ins.then_inc(pchain, 1)
                pool.wait_ge(pchain, links[0])

            link(nc.gpsimd.memset(ident[:, :], 0.0))
            nc.gpsimd.affine_select(out=ident[:, :], in_=ident[:, :], compare_op=ALU.not_equal, fill=1.0, base=0,
                                    pattern=[[-1, P]], channel_multiplier=1).then_inc(consts, 1)
            nc.gpsimd.memset(ones[:, :], 1.0).then_inc(consts, 1)
            nc.gpsimd.memset(one_row[:, :], 1.0).then_inc(consts, 1)
            link(nc.gpsimd.memset(before[:, :], 1.0))
            nc.gpsimd.affine_select(out=before[:, :], in_=before[:, :], compare_op=ALU.is_gt, fill=0.0, base=0,
                                    pattern=[[1, P]], channel_multiplier=-1).then_inc(consts, 1)
            link(nc.gpsimd.memset(causal[:, :], 1.0))
            nc.gpsimd.affine_select(out=causal[:, :], in_=causal[:, :], compare_op=ALU.is_ge, fill=0.0, base=0,
                                    pattern=[[1, P]], channel_multiplier=-1).then_inc(consts, 1)
            link(nc.gpsimd.memset(head_diag[:, :], 1.0))
            hd3 = head_diag[:, :].rearrange("p (h e) -> p h e", e=HD)
            link(nc.gpsimd.affine_select(out=hd3, in_=hd3, compare_op=ALU.is_ge, fill=0.0, base=0,
                                         pattern=[[-HD, HEADS], [0, HD]], channel_multiplier=1))
            link(nc.gpsimd.affine_select(out=hd3, in_=hd3, compare_op=ALU.is_ge, fill=0.0, base=HD - 1,
                                         pattern=[[HD, HEADS], [0, HD]], channel_multiplier=-1))
            nc.gpsimd.tensor_copy(head_sum[:, :], hd3[:, :, 0]).then_inc(consts, 1)
            link(nc.gpsimd.memset(desc[:, :], 1.0))
            for e in range(E):
                last = nc.gpsimd.memset(desc[:, e:e + 1], float(E - e))
            last.then_inc(consts, 1)
            nc.gpsimd.iota(step_slot[:, :], pattern=[[SLOTS, E_STEPS]], base=0, channel_multiplier=0,
                           allow_small_or_imprecise_dtypes=True).then_inc(consts, 1)
            link(nc.gpsimd.memset(not_first[:, :, :], 1.0))
            nc.gpsimd.memset(not_first[:, :, 0:1], 0.0).then_inc(consts, 1)
            nc.gpsimd.memset(ones8[:, :], 1.0).then_inc(consts, 1)
            nc.gpsimd.memset(gT[:, E:], 0.0).then_inc(consts, 1)
            link(nc.gpsimd.memset(head_pick[:, :], 0.0))
            pool.wait_ge(consts, 10)
            hs4 = head_sum[:, :].rearrange("p (g k) -> p g k", k=4)
            link(nc.gpsimd.tensor_tensor(head_pick[:, :], hs4[:, 0, :], hs4[:, 1, :], ALU.add))
            link(nc.gpsimd.tensor_tensor(head_pick[:, :], head_pick[:, :], hs4[:, 2, :], ALU.add))
            nc.gpsimd.tensor_tensor(head_pick[:, :], head_pick[:, :], hs4[:, 3, :], ALU.add).then_inc(consts, 1)
            link(nc.gpsimd.memset(group_mask[:, :], 1.0))
            link(nc.gpsimd.affine_select(out=group_mask[:, :], in_=group_mask[:, :], compare_op=ALU.is_ge, fill=0.0, base=0,
                                         pattern=[[-4 * HD, 4]], channel_multiplier=1))
            nc.gpsimd.affine_select(out=group_mask[:, :], in_=group_mask[:, :], compare_op=ALU.is_ge, fill=0.0,
                                    base=4 * HD - 1, pattern=[[4 * HD, 4]], channel_multiplier=-1).then_inc(consts, 1)
            nc.gpsimd.memset(settled[:, :], 0.0).then_inc(consts, 1)

            nc.gpsimd.memset(got[:, 0, 0:ZERO_TILES, :], 0.0).then_inc(zero_tile, 1)
            nc.gpsimd.memset(vx[:, :, :, :], 0.0).then_inc(consts, 1)

            pool.wait_ge(scaled_a, 1)
            for i in range(A_STEPS):
                tiles = slice(i * QUAD, (i + 1) * QUAD)
                shape = [P, QUAD, D]
                wait(pool, a_turned, i - 1)
                nc.gpsimd.tensor_tensor(xn[:, i % 2, :, :], x[:, tiles, :],
                                        mean[:, tiles].rearrange("p (t a) -> p t a", a=1).to_broadcast(shape),
                                        ALU.subtract).then_inc(a_centred_pool, 1)
                pool.wait_ge(a_centred_pool, i + 1)
                nc.gpsimd.tensor_tensor(xn[:, i % 2, :, :], xn[:, i % 2, :, :],
                                        n_scale[:, tiles].rearrange("p (t a) -> p t a", a=1).to_broadcast(shape),
                                        ALU.mult).then_inc(a_normed_pool, 1)

            def scatter(call, h):
                pool.wait_ge(zeroed[h], 16 * (ROWS // (ZERO_TILES * P)))
                for k in range(2):
                    pool.wait_ge(r_slotted, 2 * call + k + 1)
                    for t in range(HT):
                        pool.indirect_dma_start(tok_rows[h], bass.IndirectOffsetOnAxis(ap=slot[:, k, h, t:t + 1], axis=0),
                                                t_rows[:, h, t, :], None).then_inc(scattered[h], 16)

            def gather(call, h):
                for k in range(E_UNROLL):
                    pool.wait_ge(e_stored[k], 16 * (E_STEPS // E_UNROLL) * (call + 1))
                for q in range(PARTS):
                    wait(pool, combined, (call - 1) * CHUNKS + (q + 1) * PART_CHUNKS)
                    for t in range(q * PT, (q + 1) * PT):
                        for k in range(2):
                            pool.indirect_dma_start(got[:, k, t, :], None, exp_rows[h],
                                                    bass.IndirectOffsetOnAxis(ap=slot[:, k, h, t:t + 1], axis=0)
                                                    ).then_inc(gathered[h][t // (QUAD * BACK_CHUNKS)], 16)

            def add_rows(call, q):
                pool.wait_ge(combined, call * CHUNKS + q * PART_CHUNKS)
                pool.wait_ge(residual_added, (call + 1) * HT)
                for c in range(q * PART_CHUNKS, (q + 1) * PART_CHUNKS):
                    n = call * CHUNKS + c + 1
                    if c % BACK_CHUNKS == 0:
                        pool.wait_ge(gathered[call][c // BACK_CHUNKS], 16 * 2 * QUAD * BACK_CHUNKS)
                    rows = [got[:, k, c * QUAD:(c + 1) * QUAD, :] for k in range(2)]
                    xs = x[:, (n - 1) * QUAD:n * QUAD, :]
                    for k in range(2):
                        p = prob[:, k, call, c * QUAD:(c + 1) * QUAD].rearrange("p (t a) -> p t a", a=1)
                        last = nc.gpsimd.tensor_tensor(rows[k], rows[k], p.to_broadcast([P, QUAD, D]), ALU.mult)
                    last.then_inc(weighted, 1)
                    pool.wait_ge(weighted, n - PART_CHUNKS)
                    nc.gpsimd.tensor_tensor(rows[0], rows[0], rows[1], ALU.add).then_inc(first_added, 1)
                    pool.wait_ge(first_added, n)
                    nc.gpsimd.tensor_tensor(xs, xs, rows[0], ALU.add).then_inc(combined, 1)

            for rnd in range(2):
                for h in range(HALVES):
                    scatter(rnd * HALVES + h, h)
                for h in range(HALVES):
                    gather(rnd * HALVES + h, h)
                    if rnd == 0:
                        for q in range(1 - h, PARTS):
                            add_rows(h, q)

        @block.tensor
        def _(pe):
            pe.wait_ge(consts, 1)
            pe.wait_ge(first_w_loaded, 16 * 5)
            for c in range(3):
                nc.tensor.transpose(ps[:, 0, c * P:(c + 1) * P], stage[:, c, :], ident[:, :])
            nc.tensor.transpose(ps[:, 0, 3 * P:3 * P + E], stage[0:E, 3, :], ident[0:E, 0:E])
            nc.tensor.transpose(ps[:, 0, 3 * P + E:3 * P + E + E * HC], stage[0:E * HC, 4, :],
                                ident[0:E * HC, 0:E * HC]).then_inc(wT_psum, 1)
            pe.wait_ge(wT_done, 1)

            def expert_weights():
                pe.wait_ge(expert_w_loaded, 16 * 2)
                for r in range(2 * E * HC):
                    last = nc.tensor.transpose(ps[:, r // QUAD, r % QUAD * P:(r % QUAD + 1) * P], e_stage[:, r, :],
                                               ident[:, :])
                last.then_inc(ewT_psum, 1)
                pe.wait_ge(ewT_done, 1)

            pe.wait_ge(consts, ALL_CONSTS)

            def layer_a(h):
                n0 = h * A_STEPS

                def turn(i, b):
                    if h == 0:
                        pe.wait_ge(a_normed_pool, i + 1)
                    else:
                        pe.wait_ge(a_normed_dve, i + 1)
                        pe.wait_ge(a_normed_act, i + 1)
                    wait(pe, a_turned_copied, n0 + i)
                    for t in range(QUAD):
                        last = nc.tensor.transpose(ps[:, 0, t * P:(t + 1) * P], xn[:, b, t, :], ident[:, :])
                    last.then_inc(a_turned, 1)

                def project(i, b):
                    pe.wait_ge(a_turned_copied, n0 + i + 1)
                    wait(pe, a_multiplied, n0 + i - 1)
                    for bank, c in ((6, 2), (4, 1), (2, 0)):
                        nc.tensor.matmul(ps[:, bank + b, :], wa[:, c, :], xnT[:, b, :], start=True,
                                         stop=True).then_inc(a_projected, 1)

                def back(i, b):
                    pe.wait_ge(a_multiplied, n0 + i + 1)
                    wait(pe, a_added, n0 + i)
                    for t in range(QUAD):
                        last = nc.tensor.transpose(ps[:, 1, t * P:(t + 1) * P], yq[:, b, t * P:(t + 1) * P], ident[:, :])
                    last.then_inc(a_turned_back, 1)

                def step(i, b):
                    if not isinstance(i, int) or i + 1 < A_STEPS:
                        turn(i + 1, 1 - b)
                    project(i, b)
                    if not is_at(i, 0):
                        back(i - 1, 1 - b)
                turn(0, 0)
                run_steps(pe, A_STEPS, 2, step)
                back(A_STEPS - 1, 1)

            def gates(call):
                n0 = call * G_STEPS

                def turn(i, b):
                    pe.wait_ge(g_rows_dve, n0 + i + 1)
                    pe.wait_ge(g_rows_act, n0 + i + 1)
                    wait(pe, g_turned_copied, n0 + i - 1)
                    for t in range(QUAD):
                        last = nc.tensor.transpose(ps[:, b, t * P:(t + 1) * P], t_rows[:, call % HALVES, i * QUAD + t, :],
                                                   ident[:, :])
                    last.then_inc(g_turned, 1)

                def project(i, b):
                    pe.wait_ge(g_turned_copied, n0 + i + 1)
                    wait(pe, g_projected_copied, n0 + i)
                    for t in range(QUAD):
                        rows = slice(t * P // QUAD, (t + 1) * P // QUAD)
                        last = nc.tensor.matmul(ps[rows, 7, 0:P], gT[:, :], xnT[:, b, t * P:(t + 1) * P], start=True,
                                                stop=True, tile_position=(0, t * P // QUAD))
                    last.then_inc(g_projected, 1)

                def logit(i, b):
                    pe.wait_ge(g_projected_copied, n0 + i + 1)
                    nc.tensor.matmul(logits_psum[:, i * QUAD * E:(i + 1) * QUAD * E], lt[:, b, :],
                                     ident[:, :].rearrange("p (t c) -> p t c", t=QUAD)[:, :, 0:E], start=True, stop=True
                                     ).then_inc(g_logits_psum, 1)
                turn(0, 0)
                for i in range(G_STEPS):
                    if i + 1 < G_STEPS:
                        turn(i + 1, (i + 1) % 2)
                    project(i, i % 2)
                    if i:
                        logit(i - 1, (i - 1) % 2)
                logit(G_STEPS - 1, (G_STEPS - 1) % 2)
                pe.wait_ge(g_logits_copied, call + 1)
                if call != LATE:
                    count(call)
                    pe.wait_ge(r_counts_copied, call + 1)

            def count(call):
                pe.wait_ge(r_picked, call + 1)
                cols = picked[:, :, :].rearrange("p t e -> p (t e)")
                nc.tensor.matmul(ranks_psum, before[:, :], cols, start=True, stop=True)
                nc.tensor.matmul(counts_psum, ones[:, :], cols, start=True, stop=True).then_inc(r_counted, 1)

            def experts(call, h):
                n0 = call * E_STEPS

                def turn(m, k):
                    pe.wait_ge(e_loaded[k], rounds(call, m, k) + 16)
                    wait(pe, e_turned_copied, n0 + m - 1)
                    for s in range(SUB):
                        last = nc.tensor.transpose(ps[:, k % 2, s * P:(s + 1) * P], ts[:, k, s, :], ident[:, :])
                    last.then_inc(e_turned, 1)

                def up(m, b):
                    pe.wait_ge(e_turned_copied, n0 + m + 1)
                    pe.wait_ge(e_w1_copied, n0 + m + 1)
                    wait(pe, e_gelu_done, n0 + m - 1)
                    for c in range(HC):
                        last = nc.tensor.matmul(ps[:, 2 + b, c * SLOTS:(c + 1) * SLOTS], w1s[:, b, c * P:(c + 1) * P],
                                                tT[:, b, :], start=True, stop=True)
                    last.then_inc(e_up_done, 1)

                def down(m, b):
                    pe.wait_ge(e_gelu_done, n0 + m + 1)
                    wait(pe, e_biased, n0 + m - 1)
                    e = pe.value_load(step_exp[0:1, h, bass.ds(m, 1)], min_val=0, max_val=E - 1)
                    for s in range(SUB):
                        for c in range(HC):
                            last = nc.tensor.matmul(ps[:, 4 + b, s * P:(s + 1) * P], hT[:, b, c, s * P:(s + 1) * P],
                                                    tile_of(w2T, e * HC + c), start=(c == 0), stop=(c == HC - 1))
                    last.then_inc(e_down_done, 1)

                def step(m, k):
                    if not isinstance(m, int) or m + 1 < E_STEPS:
                        turn(m + 1, (k + 1) % E_UNROLL)
                    up(m, k % 2)
                    if not is_at(m, 0):
                        down(m - 1, (k + 1) % 2)
                turn(0, 0)
                run_steps(pe, E_STEPS, E_UNROLL, step)
                down(E_STEPS - 1, 1)

            def layer_b(h):
                scores = scores_of(h)
                n0 = h * B_STEPS

                def turn(m, b):
                    pe.wait_ge(b_normed, n0 + m + 1)
                    wait(pe, b_rec_copied, n0 + m - 1)
                    wait(pe, b_states_masked, n0 + m)
                    wait(pe, b_turned_copied, n0 + m)
                    for t in range(2):
                        last = nc.tensor.transpose(ps[:, 0, t * P:(t + 1) * P], b_xn[:, b, t, :], ident[:, :])
                    last.then_inc(b_turned, 1)

                def project(m, b):
                    pe.wait_ge(b_turned_copied, n0 + m + 1)
                    wait(pe, b_features, n0 + m)
                    wait(pe, b_states_masked, n0 + m)
                    if h == 1 and is_at(m, 4):
                        pe.wait_ge(r_counts_copied, LATE + 1)
                    for k in range(2):
                        nc.tensor.matmul(ps[:, 1, k * S:(k + 1) * S], wb[:, k, :], b_xnT[:, :], start=True, stop=True)
                    for t in range(2):
                        last = nc.tensor.matmul(ps[:, 2, t * P:(t + 1) * P], b_xnT[:, t * P:(t + 1) * P], wb[:, 2, :],
                                                start=True, stop=True)
                    last.then_inc(b_projected, 1)

                def denominators(m, b):
                    pe.wait_ge(b_query_sums, n0 + m + 1)
                    pe.wait_ge(b_values_copied, n0 + m + 1)
                    wait(pe, b_rec_copied, n0 + m)
                    for t in range(2):
                        last = nc.tensor.matmul(ps[:, 2, S + t * HEADS:S + (t + 1) * HEADS], qz[:, t * P:(t + 1) * P],
                                                head_sum[:, :], start=True, stop=True)
                    last.then_inc(b_den_psum, 1)
                    for t in range(2):
                        last = nc.tensor.transpose(ps[:, 0, S + t * P:S + (t + 1) * P], qk[:, b, 1, t * P:(t + 1) * P],
                                                   ident[:, :])
                    last.then_inc(b_keys_turned, 1)

                def states(m, b):
                    pe.wait_ge(b_keys_copied, n0 + m + 1)
                    pe.wait_ge(b_den_read, n0 + m + 1)
                    nc.tensor.matmul(ps[:, 0, S:S + P], k_tok[0:C, 0, :], plain_v(b, 0, C), start=True, stop=True)
                    nc.tensor.matmul(ps[:, 2, S + 2 * HEADS:S + 2 * HEADS + P], k_tok[:, 0, :], plain_v(b, 0), start=True,
                                     stop=True)
                    nc.tensor.matmul(ps[:, 0, S + P:S + 2 * P], k_tok[:, 0, :], plain_v(b, 0), start=True, stop=False)
                    nc.tensor.matmul(ps[:, 0, S + P:S + 2 * P], k_tok[0:C, 1, :], plain_v(b, 1, C), start=False,
                                     stop=True).then_inc(b_states_psum, 1)

                def turn_reciprocals(m, b, m_next=None):
                    pe.wait_ge(b_rec_spread, n0 + m + 1)
                    pe.wait_ge(b_states_masked, n0 + m + 1)
                    if m_next is not None:
                        pe.wait_ge(b_turned_copied, m_next)
                    for t in range(2):
                        rows = recx[:, t * HEADS:(t + 1) * HEADS, :].rearrange("p h e -> p (h e)")
                        last = nc.tensor.transpose(ps[:, 0, t * P:(t + 1) * P], rows, ident[:, :])
                    last.then_inc(b_rec_turned, 1)

                def score(n, b, blk, g):
                    c = 8 * (n0 + n) + 4 * blk + g
                    wait(pe, b_masked, c - 3)
                    if g == 0 and blk == 0:
                        pe.wait_ge(b_keys_split, n0 + n + 1)
                        pe.wait_ge(b_queries_split, n0 + n + 1)
                    bank = ps[:, 3 + g, :].rearrange("p (k i) -> p k i", k=4)
                    for c in range(2):
                        tokens = slice(blk * P + c * C, blk * P + (c + 1) * C)
                        last = nc.tensor.matmul(bank[c * C:(c + 1) * C, :, c * C:(c + 1) * C], kx[:, b, g, tokens],
                                                qx[:, b, :, tokens], start=True, stop=True, tile_position=(0, c * C))
                    last.then_inc(b_scored, 1)

                def weigh(n, b, blk):
                    pe.wait_ge(b_masked, 8 * (n0 + n) + 4 * blk + 4)
                    wait(pe, b_divided, n0 + n)
                    out = ps[:, 7, blk * P:(blk + 1) * P]
                    if blk == 0:
                        wait(pe, b_added, n0 + n)
                        pe.wait_ge(b_states_masked, n0 + n + 1)
                    for k in range(4):
                        for g in range(4):
                            q = slice(32 * g, 32 * g + 32)
                            nc.tensor.matmul(out[q, :], vx[:, b, blk, k * P + g * 32:k * P + g * 32 + 32],
                                             scores[:, blk, g, k, :], start=(k == 0), stop=False,
                                             tile_position=(0, 32 * g), skip_group_check=True)
                    for c, st in ((1, 0),) if blk == 0 else ((0, 2), (1, 1)):
                        last = nc.tensor.matmul(out[:, c * C:(c + 1) * C], state[:, b, st * P:(st + 1) * P],
                                                qk[:, b, 0, blk * P + c * C:blk * P + (c + 1) * C], start=False, stop=True,
                                                skip_group_check=True)
                    last.then_inc(b_weighed, 1)

                def back(n, b):
                    pe.wait_ge(b_divided, n0 + n + 1)
                    for t in range(2):
                        last = nc.tensor.matmul(ps[:, 7, S + t * P:S + (t + 1) * P], oT[:, b, t * P:(t + 1) * P],
                                                wb[:, 3, :], start=True, stop=True)
                    last.then_inc(b_out_psum, 1)

                def step(n, b):
                    more = not isinstance(n, int) or n + 1 < B_STEPS
                    if more:
                        turn(n + 1, 1 - b)
                    score(n, b, 0, 0)
                    score(n, b, 0, 1)
                    if more:
                        project(n + 1, 1 - b)
                    score(n, b, 0, 2)
                    if not is_at(n, 0):
                        back(n - 1, 1 - b)
                    score(n, b, 0, 3)
                    turn_reciprocals(n, b, n0 + n + 2 if more else None)
                    for g in range(4):
                        score(n, b, 1, g)
                    if more:
                        denominators(n + 1, 1 - b)
                    weigh(n, b, 0)
                    if more:
                        states(n + 1, 1 - b)
                    weigh(n, b, 1)
                turn(0, 0)
                project(0, 0)
                if h == 0:
                    pe.wait_ge(b_banks_zeroed, 1)
                denominators(0, 0)
                states(0, 0)
                if h == 0:
                    run_steps(pe, B_STEPS, 2, step)
                else:
                    straight(0, 3, 2, step)
                    count(LATE)
                    straight(3, 6, 2, step)
                    looped(pe, 6, B_STEPS - 2, 2, step)
                    straight(B_STEPS - 2, B_STEPS, 2, step)
                back(B_STEPS - 1, 1)

            for rnd in range(2):
                for h in range(HALVES):
                    if rnd == 0:
                        layer_a(h)
                    else:
                        if h == 0:
                            pe.wait_ge(w_loaded, 16 * 5)
                        layer_b(h)
                    gates(rnd * HALVES + h)
                    if rnd == 0 and h == 0:
                        expert_weights()
                for h in range(HALVES):
                    experts(rnd * HALVES + h, h)

        @block.scalar
        def _(act):
            act.dma_start(stage[:, 0:3, :], w_qkva.rearrange("(c p) d -> p c d", p=P)).then_inc(first_w_loaded, 16)
            act.dma_start(gam[:, :], gamma.rearrange("(p a) -> p a", a=1)).then_inc(first_w_loaded, 16)
            act.dma_start(nw[:, :], norm_w.rearrange("(p a) -> p a", a=1)).then_inc(first_w_loaded, 16)
            act.dma_start(stage[0:E, 3, :], gate_w).then_inc(first_w_loaded, 16)
            act.dma_start(stage[0:E * HC, 4, :], b1.rearrange("e (c p) -> (e c) p", p=P)).then_inc(first_w_loaded, 16)
            act.wait_ge(x_loaded[1], 16)
            act.dma_start(e_stage[:, 0:E * HC, :], w1.rearrange("e (c p) d -> p (e c) d", p=P)
                          ).then_inc(expert_w_loaded, 16)
            act.dma_start(e_stage[:, E * HC:2 * E * HC, :].rearrange("p (e c) d -> p e (c d)", e=E),
                          w2.rearrange("e d h -> d e h")).then_inc(expert_w_loaded, 16)
            for k, w in enumerate((b_wq, b_wk, b_wv, b_wo)):
                act.dma_start(wb[:, k, :], w).then_inc(w_loaded, 16)
            act.dma_start(b2_all[:, :, :], b2.rearrange("(a e) d -> a e d", a=1).to_broadcast([P, E, D])
                          ).then_inc(w_loaded, 16)
            act.wait_ge(wT_psum, 1)
            nc.scalar.activation(wa[:, :, :].rearrange("p c e -> p (c e)"), ps[:, 0, 0:3 * P], ACT.Copy, scale=gam[:, 0:1])
            nc.scalar.activation(gT[:, 0:E], ps[:, 0, 3 * P:3 * P + E], ACT.Copy, scale=nw[:, 0:1])
            nc.scalar.copy(w1T[:, :, HID:W1C], ps[:, 0, 3 * P + E:3 * P + E + E * HC].rearrange("p (e c) -> p e c", c=HC)
                           ).then_inc(wT_done, 1)

            def expert_weights():
                act.wait_ge(ewT_psum, 1)
                for n in range(4):
                    nc.scalar.activation(w1T[:, 2 * n:2 * n + 2, 0:HID], ps[:, n, :].rearrange("p (e h) -> p e h", e=2),
                                         ACT.Copy, scale=nw[:, 0:1])
                for n in range(4):
                    last = nc.scalar.copy(w2T[:, 4 * n:4 * n + 4, :].rearrange("p a d -> p (a d)"), ps[:, 4 + n, :])
                last.then_inc(ewT_done, 1)

            def centre(dst, t):
                return nc.scalar.activation(dst, tile_of(x, t), ACT.Identity, bias=n_bias[:, bass.ds(t, 1)])

            def scale(dst, t):
                return nc.scalar.activation(dst, dst, ACT.Copy, scale=n_scale[:, bass.ds(t, 1)])

            def layer_a(h):
                n0 = h * A_STEPS

                def copy_xnT(i, b):
                    act.wait_ge(a_turned, n0 + i + 1)
                    wait(act, a_projected, 3 * (n0 + i - 1))
                    nc.scalar.copy(xnT[:, b, :], ps[:, 0, :]).then_inc(a_turned_copied, 1)

                def norm(i, b):
                    wait(act, a_turned, n0 + i - 1)
                    tiles = range(QUAD // 2, QUAD)
                    for t in tiles:
                        last = centre(xn[:, b, t, :], h * HT + i * QUAD + t)
                    last.then_inc(a_centred_act, 1)
                    act.wait_ge(a_centred_act, i + 1)
                    for t in tiles:
                        last = scale(xn[:, b, t, :], h * HT + i * QUAD + t)
                    last.then_inc(a_normed_act, 1)

                def step(i, b):
                    if not isinstance(i, int) or i + 1 < A_STEPS:
                        copy_xnT(i + 1, 1 - b)
                    if h == 1 and (not isinstance(i, int) or i + 2 < A_STEPS):
                        norm(i + 2, b)
                    act.wait_ge(a_projected, (n0 + i) * 3 + 1)
                    wait(act, a_scanned, n0 + i - 1)
                    nc.scalar.activation(gate[:, b, :], ps[:, 6 + b, :], ACT.Sigmoid).then_inc(a_gated, 1)
                if h == 1:
                    act.wait_ge(scaled_a, 2)
                    norm(0, 0)
                    norm(1, 1)
                    expert_weights()
                    act.wait_ge(g_logits_psum, h * G_STEPS)
                copy_xnT(0, 0)
                run_steps(act, A_STEPS, 2, step)

            def gates(call):
                n0 = call * G_STEPS
                if call < HALVES:
                    act.wait_ge(a_projected, 3 * A_STEPS * (call + 1))
                h = call % HALVES

                def norm(i):
                    t = i * QUAD + QUAD - 1
                    centre(t_rows[:, h, t, :], h * HT + t).then_inc(g_centred, 1)
                    act.wait_ge(g_centred, n0 + i + 1)
                    scale(t_rows[:, h, t, :], h * HT + t).then_inc(g_rows_act, 1)
                act.wait_ge(scaled_f, call + 1)
                wait(act, scattered[h], 16 * 2 * HT * (call // HALVES))
                norm(0)
                norm(1)
                for i in range(G_STEPS):
                    b = i % 2
                    act.wait_ge(g_turned, n0 + i + 1)
                    wait(act, g_projected, n0 + i - 1)
                    nc.scalar.copy(xnT[:, b, :], ps[:, b, :]).then_inc(g_turned_copied, 1)
                    if i + 2 < G_STEPS:
                        norm(i + 2)
                    act.wait_ge(g_projected, n0 + i + 1)
                    wait(act, g_logits_psum, n0 + i - 1)
                    nc.scalar.copy(lt[:, b, :], ps[:, 7, 0:P]).then_inc(g_projected_copied, 1)
                if call != LATE:
                    exponential(call)

            def exponential(call):
                act.wait_ge(r_diffed, call + 1)
                nc.scalar.activation(ex[:, :], m2[:, :], ACT.Exp).then_inc(r_exponential, 1)

            def experts(call, h):
                n0 = call * E_STEPS

                def feed(m, b):
                    act.wait_ge(e_turned, n0 + m + 1)
                    wait(act, e_up_done, n0 + m - 1)
                    nc.scalar.copy(tT[:, b, :], ps[:, b, 0:SLOTS]).then_inc(e_turned_copied, 1)
                    e = act.value_load(step_exp[0:1, h, bass.ds(m, 1)], min_val=0, max_val=E - 1)
                    wait(act, e_gelu_done, n0 + m - 1)
                    nc.scalar.copy(w1s[:, b, :], tile_of(w1T, e)).then_inc(e_w1_copied, 1)

                def residual(m):
                    t = h * HT + m
                    nc.scalar.activation(tile_of(x, t), tile_of(x, t), ACT.Identity, bias=res_bias[:, bass.ds(t, 1)],
                                         scale=res_scale[:, bass.ds(t, 1)]).then_inc(residual_added, 1)

                def step(m, k):
                    b = k % 2
                    if not isinstance(m, int) or m + 1 < E_STEPS:
                        feed(m + 1, 1 - b)
                    act.wait_ge(e_up_done, n0 + m + 1)
                    wait(act, e_down_done, n0 + m - 1)
                    for c in range(HC):
                        last = nc.scalar.activation(hT[:, b, c, :], ps[:, 2 + b, c * SLOTS:(c + 1) * SLOTS], ACT.Gelu,
                                                    bias=w1s[:, b, HID + c:HID + c + 1])
                    last.then_inc(e_gelu_done, 1)

                def step_and_residual(m, k):
                    step(m, k)
                    residual(m)
                feed(0, 0)
                straight(0, E_UNROLL, E_UNROLL, step_and_residual)
                looped(act, E_UNROLL, HT, E_UNROLL, step_and_residual)
                straight(HT, E_STEPS, E_UNROLL, step)

            def layer_b(h):
                n0 = h * B_STEPS

                def norm(m, b):
                    wait(act, b_turned, n0 + m - 1)
                    for t in range(2):
                        tile = h * HT + 2 * m + t
                        last = nc.scalar.activation(b_xn[:, b, t, :], tile_of(x, tile), ACT.Identity,
                                                    bias=n_bias[:, bass.ds(tile, 1)], scale=n_scale[:, bass.ds(tile, 1)])
                    last.then_inc(b_normed, 1)

                def front(m, b):
                    act.wait_ge(b_turned, n0 + m + 1)
                    wait(act, b_projected, n0 + m)
                    nc.scalar.copy(b_xnT[:, :], ps[:, 0, 0:S]).then_inc(b_turned_copied, 1)
                    act.wait_ge(b_projected, n0 + m + 1)
                    wait(act, b_features, n0 + m)
                    nc.scalar.activation(b_exp[:, :], ps[:, 1, :], ACT.Relu, scale=-1.0).then_inc(b_negated, 1)
                    act.wait_ge(b_negated, n0 + m + 1)
                    nc.scalar.activation(b_exp[:, :], b_exp[:, :], ACT.Exp, scale=-1.0).then_inc(b_exponential, 1)

                def values(m, b):
                    wait(act, b_weighed, 2 * (n0 + m) - 2)
                    for t in range(2):
                        last = nc.scalar.copy(plain_v(b, t), ps[:, 2, t * P:(t + 1) * P].rearrange(
                            "p (g k e) -> p g k e", g=4, k=4))
                    last.then_inc(b_values_copied, 1)

                def split_keys(m, b):
                    act.wait_ge(b_features, n0 + m + 1)
                    wait(act, b_scored, 8 * (n0 + m - 1))
                    for g in range(4):
                        last = nc.scalar.activation(kx[:, b, g, :], qk[:, b, 1, :], ACT.Copy, scale=group_mask[:, g:g + 1])
                    last.then_inc(b_keys_split, 1)

                def split_queries(m, b):
                    wait(act, b_scored, 8 * (n0 + m - 1))
                    for k in range(4):
                        last = nc.scalar.activation(qx[:, b, k, :], qk[:, b, 0, :], ACT.Copy, scale=head_pick[:, k:k + 1])
                    last.then_inc(b_queries_split, 1)

                def turned_keys(m):
                    act.wait_ge(b_keys_turned, n0 + m + 1)
                    wait(act, b_states_psum, n0 + m)
                    nc.scalar.copy(k_tok[:, :, :].rearrange("p t d -> p (t d)"), ps[:, 0, S:2 * S]).then_inc(b_keys_copied, 1)

                def spread_reciprocals(m):
                    act.wait_ge(b_reciprocal, n0 + m + 1)
                    wait(act, b_rec_turned, n0 + m)
                    nc.scalar.copy(recx[:, :, :], rec[:, :].rearrange("p (h a) -> p h a", a=1).to_broadcast(
                        [P, 2 * HEADS, HD])).then_inc(b_rec_spread, 1)

                def turned_reciprocals(m, b):
                    act.wait_ge(b_rec_turned, n0 + m + 1)
                    wait(act, b_divided, n0 + m - 1)
                    nc.scalar.copy(recT[:, b, :], ps[:, 0, 0:S]).then_inc(b_rec_copied, 1)

                def step(n, b):
                    more = not isinstance(n, int) or n + 1 < B_STEPS
                    if more:
                        front(n + 1, 1 - b)
                    turned_reciprocals(n, b)
                    if more:
                        values(n + 1, 1 - b)
                        split_keys(n + 1, 1 - b)
                        turned_keys(n + 1)
                        split_queries(n + 1, 1 - b)
                        spread_reciprocals(n + 1)
                    if not isinstance(n, int) or n + 2 < B_STEPS:
                        norm(n + 2, b)
                act.wait_ge(scaled_b, 1 if h == 0 else 3)
                norm(0, 0)
                norm(1, 1)
                front(0, 0)
                values(0, 0)
                split_keys(0, 0)
                turned_keys(0)
                split_queries(0, 0)
                spread_reciprocals(0)
                if h == 0:
                    early = PT // 2 - 2
                    straight(0, 2, 2, step)
                    looped(act, 2, early, 2, step)
                    act.wait_ge(scaled_b, 2)
                    looped(act, early, B_STEPS - 2, 2, step)
                else:
                    straight(0, 4, 2, step)
                    exponential(LATE)
                    looped(act, 4, B_STEPS - 2, 2, step)
                straight(B_STEPS - 2, B_STEPS, 2, step)

            for rnd in range(2):
                for h in range(HALVES):
                    if rnd == 0:
                        layer_a(h)
                    else:
                        layer_b(h)
                    gates(rnd * HALVES + h)
                for h in range(HALVES):
                    act.wait_ge(r_routed, rnd * HALVES + h + 1)
                    experts(rnd * HALVES + h, h)

        @block.vector
        def _(dve):
            links = [0]

            def link(ins):
                links[0] += 1
                ins.then_inc(chain, 1)
                dve.wait_ge(chain, links[0])

            def settle():
                link(nc.vector.tensor_copy(settled[:, 0:1], settled[:, 1:2]))

            def inv_roots(cols):
                v, r, w = (sv[:, k, 0:cols] for k in (0, 1, 2))
                link(nc.vector.tensor_scalar(r.bitcast(I32), v.bitcast(I32), -0.5, float(0x5f3759df), ALU.mult, ALU.add))
                for _ in range(3):
                    link(nc.vector.tensor_tensor(w, r, r, ALU.mult))
                    link(nc.vector.scalar_tensor_tensor(out=w, in0=w, scalar=-0.5, in1=v, op0=ALU.mult, op1=ALU.mult))
                    link(nc.vector.scalar_tensor_tensor(out=r, in0=w, scalar=1.5, in1=r, op0=ALU.add, op1=ALU.mult))

            def moments(t0, n):
                sl = slice(t0, t0 + n)
                me, qe, mo, qo = (stats[:, sl, k] for k in (1, 2, 4, 5))
                d, q, m = (sv[:, k, 0:n] for k in (0, 1, 2))
                nc.vector.tensor_tensor(d, me, mo, ALU.subtract)
                nc.vector.tensor_tensor(q, qe, qo, ALU.add)
                link(nc.vector.tensor_tensor(m, me, mo, ALU.add))
                nc.vector.tensor_scalar(mean[:, sl], m, 0.5, None, ALU.mult)
                link(nc.vector.scalar_tensor_tensor(out=d, in0=d, scalar=0.25, in1=d, op0=ALU.mult, op1=ALU.mult))
                link(nc.vector.scalar_tensor_tensor(out=var[:, sl], in0=q, scalar=1.0 / D, in1=d, op0=ALU.mult,
                                                    op1=ALU.add))

            def set_bias(t0, n, dst, scale):
                return nc.vector.scalar_tensor_tensor(out=dst[:, t0:t0 + n], in0=mean[:, t0:t0 + n], scalar=-1.0,
                                                      in1=scale, op0=ALU.mult, op1=ALU.mult)


            def args_a(t0, n, c0):
                v, va = sv[:, 0, c0:c0 + n], var[:, t0:t0 + n]
                link(nc.vector.tensor_scalar(v, va, LN_EPS, A_EPS * A_EPS / D, ALU.add, ALU.mult))
                link(nc.vector.tensor_tensor(v, v, va, ALU.max))

            def args_b(t0, n, c0):
                link(nc.vector.tensor_scalar(sv[:, 0, c0:c0 + n], var[:, t0:t0 + n], LN_EPS, None, ALU.add))

            def args_f(t0, n, c0):
                args_b(t0, n, c0)
                link(nc.vector.scalar_tensor_tensor(out=sv[:, 0, c0 + n:c0 + 2 * n], in0=sv[:, 0, c0:c0 + n],
                                                    scalar=RMS_EPS, in1=var[:, t0:t0 + n], op0=ALU.mult, op1=ALU.add))

            def set_norm(t0, n, c0, done, nth):
                nc.vector.tensor_copy(n_scale[:, t0:t0 + n], sv[:, 1, c0:c0 + n])
                if done is scaled_b:
                    set_bias(t0, n, n_bias, sv[:, 1, c0:c0 + n]).then_inc(done, 1)
                else:
                    nc.vector.tensor_scalar(n_bias[:, t0:t0 + n], mean[:, t0:t0 + n], -1.0, None, ALU.mult
                                            ).then_inc(done, 1)
                dve.wait_ge(done, nth)

            def set_f(t0, n, c0, nth):
                nc.vector.tensor_scalar(res_scale[:, t0:t0 + n], sv[:, 1, c0:c0 + n], 1.0, None, ALU.add)
                set_bias(t0, n, res_bias, sv[:, 1, c0:c0 + n])
                set_norm(t0, n, c0 + n, scaled_f, nth)

            def scale_a(t0, n, nth):
                moments(t0, n)
                args_a(t0, n, 0)
                inv_roots(n)
                set_norm(t0, n, 0, scaled_a, nth)

            def scale_b(t0, n, nth):
                moments(t0, n)
                args_b(t0, n, 0)
                inv_roots(n)
                set_norm(t0, n, 0, scaled_b, nth)

            def scale_f(t0, n, nth):
                moments(t0, n)
                args_f(t0, n, 0)
                inv_roots(2 * n)
                set_f(t0, n, 0, nth)

            def scale_both(rnd):
                moments(0, TILES)
                args_f(0, HT, 0)
                (args_a, args_b)[rnd](HT, HT, 2 * HT)
                inv_roots(3 * HT)
                set_f(0, HT, 0, rnd * HALVES + 1)
                set_norm(HT, HT, 2 * HT, (scaled_a, scaled_b)[rnd], (2, 3)[rnd])

            def normalise(dst, t):
                return nc.vector.tensor_scalar(dst, tile_of(x, t), mean[:, bass.ds(t, 1)], n_scale[:, bass.ds(t, 1)],
                                               ALU.subtract, ALU.mult)

            def tile_stats(t):
                return nc.vector.bn_stats(tile_of(stats, t), tile_of(x, t))

            def layer_a(h):
                n0 = h * A_STEPS
                t0 = h * HT

                def scan(i, b):
                    dve.wait_ge(a_gated, n0 + i + 1)
                    dve.wait_ge(a_projected, (n0 + i) * 3 + 3)
                    wait(dve, a_turned_back, n0 + i - 1)
                    for k in range(QUAD * P // S):
                        last = nc.vector.tensor_tensor_scan(yq[:, b, k * S:(k + 1) * S], gate[:, b, k * S:(k + 1) * S],
                                                            ps[:, 4 + b, k * S:(k + 1) * S], 0.0, ALU.mult, ALU.add)
                    last.then_inc(a_scanned, 1)
                    dve.wait_ge(a_scanned, n0 + i + 1)
                    nc.vector.tensor_tensor(yq[:, b, :], yq[:, b, :], ps[:, 2 + b, :], ALU.mult).then_inc(a_multiplied, 1)

                def add(i):
                    dve.wait_ge(a_turned_back, n0 + i + 1)
                    xs = x[:, bass.ds(t0 + i * QUAD, QUAD), :]
                    nc.vector.tensor_tensor(xs, xs, ps[:, 1, :].rearrange("p (t d) -> p t d", d=D), ALU.add
                                            ).then_inc(a_added, 1)
                    dve.wait_ge(a_added, n0 + i + 1)
                    for t in range(QUAD):
                        tile_stats(t0 + i * QUAD + t)

                def norm(i, b):
                    wait(dve, a_turned, n0 + i - 1)
                    for t in range(QUAD // 2):
                        last = normalise(xn[:, b, t, :], t0 + i * QUAD + t)
                    last.then_inc(a_normed_dve, 1)

                def step(i, b):
                    if h == 1 and (not isinstance(i, int) or i + 2 < A_STEPS):
                        norm(i + 2, b)
                    scan(i, b)
                    if not is_at(i, 0):
                        add(i - 1)
                if h == 0:
                    part_stats(range(PARTS, HALVES * PARTS))
                else:
                    norm(0, 0)
                    norm(1, 1)
                run_steps(dve, A_STEPS, 2, step)
                add(A_STEPS - 1)
                settle()

            def gates(call, h):
                n0 = call * G_STEPS
                dve.wait_ge(scaled_f, call + 1)
                wait(dve, scattered[h], 16 * 2 * HT * (call // HALVES))
                for i in range(G_STEPS):
                    for t in range(QUAD - 1):
                        last = normalise(tile_of(t_rows[:, h, :, :], i * QUAD + t), h * HT + i * QUAD + t)
                    last.then_inc(g_rows_dve, 1)
                dve.wait_ge(g_logits_psum, (call + 1) * G_STEPS)
                nc.vector.tensor_copy(logits, logits_psum.rearrange("p (t e) -> p t e", e=E)).then_inc(g_logits_copied, 1)
                dve.wait_ge(g_logits_copied, call + 1)
                if call == LATE:
                    return
                route_first(call)
                route_second(call)
                route_counts(call)
                if h == 0:
                    route_bases(call)
                    route_slots(call)
                    route_steps(call)

            V = nc.vector
            tiles = [P, HT, E]
            flat = "p e t -> p (e t)"
            descb = desc[:, :].rearrange("p (a e) -> p a e", a=1).to_broadcast(tiles)

            def per_tile(v):
                return v.rearrange("p (t a) -> p t a", a=1).to_broadcast(tiles)

            def pick_first(src, m, pick):
                link(V.tensor_reduce(m[:, :], src, X, ALU.max))
                link(V.tensor_tensor(r_a[:, :, :], src, per_tile(m[:, :]), ALU.is_equal))
                link(V.tensor_tensor(r_a[:, :, :], r_a[:, :, :], descb, ALU.mult))
                link(V.tensor_reduce(mi[:, :], r_a[:, :, :], X, ALU.max))
                link(V.tensor_tensor(pick[:, :, :], per_tile(mi[:, :]), descb, ALU.is_equal))


            def route_first(call):
                pick_first(logits, m1, pick1)

            def route_second(call):
                wait(dve, r_counted, call)
                link(V.scalar_tensor_tensor(out=r_b[:, :, :], in0=pick1[:, :, :], scalar=-BIG,
                                            in1=logits, op0=ALU.mult, op1=ALU.add))
                pick_first(r_b[:, :, :], m2, pick2)
                V.tensor_tensor(picked[:, :, :], pick1[:, :, :], pick2[:, :, :], ALU.add).then_inc(r_picked, 1)

            def route_counts(call):
                dve.wait_ge(r_counted, call + 1)
                V.tensor_copy(tile_tot[:, :, :], counts_psum.rearrange("p (t e) -> p e t", e=E))
                V.tensor_copy(r_a[:, :, :], ranks_psum.rearrange("p (t e) -> p t e", e=E)).then_inc(r_counts_copied, 1)
                dve.wait_ge(r_counts_copied, call + 1)
                V.tensor_tensor(m2[:, :], m2[:, :], m1[:, :], ALU.subtract).then_inc(r_diffed, 1)

            def route_bases(call):
                h = call % HALVES
                link(V.tensor_tensor_scan(tile_inc[:, :, :].rearrange(flat), not_first[:, :, :].rearrange(flat),
                                          tile_tot[:, :, :].rearrange(flat), 0.0, ALU.mult, ALU.add))
                link(V.tensor_scalar(cnt_i[:, :], tile_inc[:, :, HT - 1], float(SLOTS - 1), None, ALU.add))
                link(V.tensor_scalar(cnt_i[:, :], cnt_i[:, :], -SLOTS, None, ALU.bitwise_and))
                link(V.tensor_copy(cnt_f[:, :], cnt_i[:, :]))
                link(V.tensor_tensor_scan(ends[:, :], ones8[:, :], cnt_f[:, :], 0.0, ALU.mult, ALU.add))
                link(V.tensor_tensor(base[:, :], ends[:, :], cnt_f[:, :], ALU.subtract))
                dve.wait_ge(r_exponential, call + 1)
                link(V.tensor_scalar(m1[:, :], ex[:, :], 1.0, None, ALU.add))
                link(V.reciprocal(prob[:, 0, h, :], m1[:, :]))
                link(V.tensor_tensor(prob[:, 1, h, :], prob[:, 0, h, :], ex[:, :], ALU.mult))

            def route_slots(call):
                h = call % HALVES
                link(V.tensor_tensor(tile_inc[:, :, :], tile_inc[:, :, :], tile_tot[:, :, :], ALU.subtract))
                link(V.tensor_tensor(tile_inc[:, :, :], tile_inc[:, :, :],
                                     base[:, :].rearrange("p (e a) -> p e a", a=1).to_broadcast([P, E, HT]), ALU.add))
                link(V.tensor_tensor(r_a[:, :, :], r_a[:, :, :], tile_inc[:, :, :].rearrange("p e t -> p t e"), ALU.add))
                for k, pick in enumerate((pick1, pick2)):
                    link(V.tensor_tensor(r_b[:, :, :], r_a[:, :, :], pick[:, :, :], ALU.mult))
                    link(V.tensor_reduce(mi[:, :], r_b[:, :, :], X, ALU.add))
                    V.tensor_copy(slot[:, k, h, :], mi[:, :]).then_inc(r_slotted, 1)
                    dve.wait_ge(r_slotted, 2 * call + k + 1)

            def route_steps(call):
                h = call % HALVES
                link(V.tensor_tensor(step_cmp[:, :, :],
                                     step_slot[:, :].rearrange("p (m a) -> p m a", a=1).to_broadcast([P, E_STEPS, E]),
                                     ends[:, :].rearrange("p (a e) -> p a e", a=1).to_broadcast([P, E_STEPS, E]),
                                     ALU.is_ge))
                link(V.tensor_reduce(step_e[:, :], step_cmp[:, :, :], X, ALU.add))
                V.tensor_scalar(step_exp[:, h, :], step_e[:, :], float(E - 1), None, ALU.min
                                ).then_inc(r_routed, 1)

            def experts(call, h):
                n0 = call * E_STEPS

                def step(m, k):
                    dve.wait_ge(e_down_done, n0 + m + 1)
                    wait(dve, e_stored[k], rounds(call, m, k))
                    e = dve.value_load(step_exp[0:1, h, bass.ds(m, 1)], min_val=0, max_val=E - 1)
                    nc.vector.tensor_tensor(o_sb[:, k, :, :], ps[:, 4 + k % 2, 0:SLOTS].rearrange("p (s d) -> p s d", d=D),
                                            b2_all[:, bass.ds(e, 1), :].to_broadcast([P, SUB, D]), ALU.add
                                            ).then_inc(e_biased, 1)
                if h == 0:
                    route_bases(call + 1)
                    route_slots(call + 1)
                    step(0, 0)
                    route_steps(call + 1)
                    step(1, 1)
                    straight(2, E_UNROLL, E_UNROLL, step)
                    looped(dve, E_UNROLL, E_STEPS - E_UNROLL, E_UNROLL, step)
                    straight(E_STEPS - E_UNROLL, E_STEPS, E_UNROLL, step)
                else:
                    first = E_STEPS - 2 * E_UNROLL
                    straight(0, E_UNROLL, E_UNROLL, step)
                    looped(dve, E_UNROLL, first, E_UNROLL, step)
                    for m in range(first, E_STEPS):
                        step(m, m % E_UNROLL)
                        c, rest = divmod(m - first, 3)
                        if c < PART_CHUNKS and rest == 2:
                            combine(call - 1, c)
                        if call < HALVES and m == first + 3 * PART_CHUNKS:
                            settle()
                            scale_b(0, PT, 1)

            def combine(call, c):
                h = call % HALVES
                n = call * CHUNKS + c
                if c == 0:
                    dve.wait_ge(residual_added, (call + 1) * HT)
                if c % BACK_CHUNKS == 0:
                    dve.wait_ge(gathered[h][c // BACK_CHUNKS], 16 * 2 * QUAD * BACK_CHUNKS * (call // HALVES + 1))
                for k, done in enumerate((first_added, combined)):
                    for j in range(QUAD):
                        t = c * QUAD + j
                        xt = tile_of(x, h * HT + t)
                        last = nc.vector.scalar_tensor_tensor(out=xt, in0=tile_of(got[:, k, :, :], t),
                                                              scalar=prob[:, k, h, bass.ds(t, 1)], in1=xt,
                                                              op0=ALU.mult, op1=ALU.add)
                    last.then_inc(done, 1)
                    dve.wait_ge(done, n + 1)
                if call < HALVES:
                    for j in range(QUAD):
                        tile_stats(h * HT + c * QUAD + j)

            def layer_b(h):
                scores = scores_of(h)
                n0 = h * B_STEPS
                t0 = h * HT

                def features(m, b):
                    dve.wait_ge(b_exponential, n0 + m + 1)
                    wait(dve, b_weighed, 2 * (n0 + m) - 2)
                    nc.vector.scalar_tensor_tensor(out=qk[:, b, :, :].rearrange("p a s -> p (a s)"), in0=ps[:, 1, :],
                                                   scalar=0.0, in1=b_exp[:, :], op0=ALU.max, op1=ALU.add
                                                   ).then_inc(b_features, 1)
                    dve.wait_ge(b_features, n0 + m + 1)
                    wait(dve, b_den_psum, n0 + m)
                    nc.vector.tensor_tensor_scan(zc[:, :], one_row[:, :], qk[:, b, 1, :], 0.0, ALU.mult, ALU.add
                                                 ).then_inc(b_key_sums, 1)
                    dve.wait_ge(b_key_sums, n0 + m + 1)
                    nc.vector.tensor_tensor(qz[:, :], zc[:, :], qk[:, b, 0, :], ALU.mult).then_inc(b_query_sums, 1)

                def mask(n, b, blk, g):
                    dve.wait_ge(b_scored, 8 * (n0 + n) + 4 * blk + g + 1)
                    wait(dve, b_weighed, 2 * (n0 + n) + blk - 1)
                    nc.vector.tensor_tensor(scores[:, blk, g, :, :], ps[:, 3 + g, :].rearrange("p (k i) -> p k i", k=4),
                                            causal[:, :].rearrange("p (a i) -> p a i", a=1).to_broadcast([P, 4, P]),
                                            ALU.mult).then_inc(b_masked, 1)

                def reciprocals(m):
                    dve.wait_ge(b_den_psum, n0 + m + 1)
                    wait(dve, b_rec_spread, n0 + m)
                    nc.vector.tensor_scalar(den[:, :], ps[:, 2, S:S + 2 * HEADS], B_EPS, None, ALU.add).then_inc(b_den_read, 1)
                    dve.wait_ge(b_den_read, n0 + m + 1)
                    nc.vector.reciprocal(rec[:, :], den[:, :]).then_inc(b_reciprocal, 1)

                def states(m, b):
                    dve.wait_ge(b_states_psum, n0 + m + 1)
                    wait(dve, b_weighed, 2 * (n0 + m) - 2)
                    nc.vector.tensor_tensor(state[:, b, 2 * P:3 * P], ps[:, 2, S + 2 * HEADS:S + 2 * HEADS + P],
                                            head_diag[:, :], ALU.mult)
                    nc.vector.tensor_tensor(state[:, b, 0:2 * P].rearrange("p (t d) -> p t d", d=P),
                                            ps[:, 0, S:2 * S].rearrange("p (t d) -> p t d", d=P),
                                            head_diag[:, :].rearrange("p (a d) -> p a d", a=1).to_broadcast([P, 2, P]),
                                            ALU.mult).then_inc(b_states_masked, 1)

                def divide(n, b):
                    dve.wait_ge(b_weighed, 2 * (n0 + n) + 2)
                    dve.wait_ge(b_rec_copied, n0 + n + 1)
                    wait(dve, b_out_psum, n0 + n - 1)
                    nc.vector.tensor_tensor(oT[:, b, 0:S], ps[:, 7, 0:S], recT[:, b, :], ALU.mult).then_inc(b_divided, 1)

                def add(n):
                    dve.wait_ge(b_out_psum, n0 + n + 1)
                    xs = x[:, bass.ds(t0 + n * 2, 2), :]
                    nc.vector.tensor_tensor(xs, xs, ps[:, 7, S:2 * S].rearrange("p (t d) -> p t d", d=D), ALU.add
                                            ).then_inc(b_added, 1)

                def batch_stats(n):
                    dve.wait_ge(b_added, n0 + n + 1)
                    for t in range(2):
                        tile_stats(t0 + n * 2 + t)

                def step(n, b):
                    more = not isinstance(n, int) or n + 1 < B_STEPS
                    for g in range(3):
                        mask(n, b, 0, g)
                    if not is_at(n, 0):
                        add(n - 1)
                    mask(n, b, 0, 3)
                    if more:
                        features(n + 1, 1 - b)
                    mask(n, b, 1, 0)
                    mask(n, b, 1, 1)
                    if more:
                        reciprocals(n + 1)
                    mask(n, b, 1, 2)
                    mask(n, b, 1, 3)
                    if more:
                        states(n + 1, 1 - b)
                    if not is_at(n, 0):
                        batch_stats(n - 1)
                    divide(n, b)
                if h == 0:
                    dve.wait_ge(e_biased, HALVES * E_STEPS)
                    nc.vector.memset(ps[:, 3:7, :], 0.0).then_inc(b_banks_zeroed, 1)
                features(0, 0)
                reciprocals(0)
                states(0, 0)
                if h == 0:
                    def added_stats(c):
                        dve.wait_ge(combined, c + 1)
                        for j in range(QUAD):
                            tile_stats(c * QUAD + j)

                    def step_and_second_part(n, b):
                        step(n, b)
                        added_stats(n + PART_CHUNKS)

                    def step_and_second_half(n, b):
                        step(n, b)
                        added_stats(n - (B_STEPS - CHUNKS) + CHUNKS)
                    straight(0, PART_CHUNKS, 2, step_and_second_part)
                    settle()
                    scale_b(PT, PT, 2)
                    looped(dve, PART_CHUNKS, B_STEPS - CHUNKS, 2, step)
                    looped(dve, B_STEPS - CHUNKS, B_STEPS - 2, 2, step_and_second_half)
                    straight(B_STEPS - 2, B_STEPS, 2, step_and_second_half)
                else:
                    for n, piece in enumerate((route_first, route_second, route_counts, route_bases, route_slots,
                                               route_steps)):
                        step(n, n % 2)
                        piece(LATE)
                    looped(dve, 6, B_STEPS - 2, 2, step)
                    straight(B_STEPS - 2, B_STEPS, 2, step)
                add(B_STEPS - 1)
                batch_stats(B_STEPS - 1)
                settle()

            def part_stats(parts):
                for part in parts:
                    dve.wait_ge(x_loaded[part], 16)
                    for t in range(part * PT, (part + 1) * PT):
                        tile_stats(t)
                dve.wait_ge(consts, ALL_CONSTS)
                settle()

            part_stats(range(PARTS))
            scale_a(0, HT, 1)
            for rnd in range(2):
                for h in range(HALVES):
                    if rnd == 0:
                        layer_a(h)
                    else:
                        layer_b(h)
                    if h == 0:
                        scale_both(rnd)
                    else:
                        scale_f(HT, HT, rnd * HALVES + 2)
                    gates(rnd * HALVES + h, h)
                for h in range(HALVES):
                    experts(rnd * HALVES + h, h)
            for call, c0 in ((HALVES, PART_CHUNKS), (HALVES + 1, 0)):
                for c in range(c0, CHUNKS):
                    combine(call, c)


_INS = ['L0_attn_a_x', 'L0_attn_a_W_qkva', 'L0_attn_a_gamma', 'L0_attn_b_wq', 'L0_attn_b_wk', 'L0_attn_b_wv',
        'L0_attn_b_wo', 'L0_ffn_norm_weight', 'L0_ffn_gate_w', 'L0_ffn_w1', 'L0_ffn_b1', 'L0_ffn_w2', 'L0_ffn_b2']


def kernel(**inputs):
    import numpy as _np
    import concourse.bacc as _bacc
    from concourse import mybir as _mybir
    from concourse.bass_utils import run_bass_kernel_spmd as _run

    nc = _bacc.Bacc("TRN2", target_bir_lowering=False, num_devices=1)
    arrays, args = {}, []
    for name in _INS:
        a = _np.ascontiguousarray(inputs[name])
        arrays[f"in_{name}"] = a
        args.append(nc.dram_tensor(f"in_{name}", a.shape, _mybir.dt.from_np(a.dtype), kind="ExternalInput").ap())
    out = nc.dram_tensor("out_x", inputs['L0_attn_a_x'].shape, _mybir.dt.float32, kind="ExternalOutput").ap()
    build_hybrid(nc, *args, out)
    r = _run(nc, [arrays], core_ids=[0])
    return r.results[0]["out_x"]
```
